# Optimizing a Trainium2 kernel written in Bass

```python
import numpy as np
import jax
import jax.numpy as jnp

def _softmax(x, axis=-1):
    return jax.nn.softmax(x, axis=axis)

def _gelu(x):
    return jax.nn.gelu(x, approximate=True)

def _silu(x):
    return jax.nn.silu(x)

def _sigmoid(x):
    return jax.nn.sigmoid(x)

def _layernorm(x, axis=-1, eps=1e-05):
    m = jnp.mean(x, axis=axis, keepdims=True)
    v = jnp.var(x, axis=axis, keepdims=True)
    return (x - m) / jnp.sqrt(v + eps)

def _scatter_add(tgt, idx, src, axis=0):
    return tgt.at[idx].add(src)

def _segment_sum(src, seg, n):
    return jax.ops.segment_sum(src, seg, n)
kernel_name = 'mk_flamingo_gated_d1_seqx_r2_c3399b'

def setup_inputs(seed: int=0):
    np.random.seed(seed)
    _w = jnp.asarray

    def _rec_inputs():
        import jax
        import jax.numpy as jnp
        _rk = jax.random.key(seed)
        x = -0.000125 + 0.9999 * jax.random.normal(jax.random.fold_in(_rk, 1), (4, 1024, 1024), jnp.float32)
        _lenS = 1024 - jax.random.randint(jax.random.fold_in(_rk, 7), (4,), 0, max(1, 1024 // 4) + 1, jnp.int32)
        _lenS2 = 1024 - jax.random.randint(jax.random.fold_in(_rk, 8), (4,), 0, max(1, 1024 // 4) + 1, jnp.int32)
        _ctx_2048P = jax.random.normal(jax.random.fold_in(_rk, 11), (4, 16, 1024), jnp.float32)
        _ctx_2048c = jax.random.dirichlet(jax.random.fold_in(_rk, 511), 0.3 * jnp.ones((16,), jnp.float32), (4, 1024))
        _ctx_2048t = jnp.einsum('bsk,bkd->bsd', _ctx_2048c, _ctx_2048P)
        _ctx_2048t = _ctx_2048t * jax.lax.rsqrt(jnp.mean(jnp.square(_ctx_2048t)) + 1e-12) * 0.953939
        ctx_2048 = -1.52775e-05 + 0.999936 * (_ctx_2048t + 0.3 * jax.random.normal(jax.random.fold_in(_rk, 611), (4, 1024, 1024), jnp.float32))
        _g = jax.random.normal(jax.random.fold_in(_rk, 9001), (2, 1), jnp.float32)
        _g = jnp.sign(_g) * jnp.maximum(jnp.abs(_g), 1.0) + (_g == 0) * 1.0
        g_xattn = _g[0]
        g_ffn = _g[1]
        return (x, ctx_2048, g_xattn, g_ffn)
    x, ctx_2048, g_xattn, g_ffn = _rec_inputs()

    def _L0_xattn_setup():
        import jax, jax.numpy as jnp
        import numpy as np
        B, S, D, H = (4, 2048, 1024, 16)
        HD = D // H
        key = jax.random.key(seed)
        ks = jax.random.split(key, 12)
        sc = 1.0 / np.sqrt(D)
        inp = {'q': jax.random.normal(ks[0], (B, S, D), jnp.float32), 'k': jax.random.normal(ks[1], (B, S, D), jnp.float32), 'v': jax.random.normal(ks[2], (B, S, D), jnp.float32), 'Wq': jax.random.normal(ks[3], (D, D), jnp.float32) * sc, 'bq': jnp.zeros((D,), jnp.float32), 'Wk': jax.random.normal(ks[4], (D, D), jnp.float32) * sc, 'bk': jnp.zeros((D,), jnp.float32), 'Wv': jax.random.normal(ks[5], (D, D), jnp.float32) * sc, 'bv': jnp.zeros((D,), jnp.float32), 'Wo': jax.random.normal(ks[6], (D, D), jnp.float32) * sc, 'bo': jnp.zeros((D,), jnp.float32)}
        return inp
    _L0_xattn_all = _L0_xattn_setup()
    _L0_xattn_in = {k: v for k, v in _L0_xattn_all.items() if k in ('Wq', 'bq', 'Wk', 'bk', 'Wv', 'bv', 'Wo', 'bo')}
    del _L0_xattn_all

    def _L0_ffn_setup():
        import jax, jax.numpy as jnp
        import numpy as np
        TOPK = 6
        CAP = 512
        ROUTE_SCALE = 1.0
        key = jax.random.key(seed)
        k = jax.random.split(key, 6)
        B, T, C = (2, 1024, 1024)
        E, H, HS = (64, 128, 256)
        std = 0.01
        return {'x': jax.random.normal(k[0], (B, T, C), jnp.float32), 'w_gate': jax.random.normal(k[1], (C, E), jnp.float32) * std, 'w_shared_up': jax.random.normal(k[2], (C, 2 * HS), jnp.float32) * std, 'w_shared_down': jax.random.normal(k[3], (HS, C), jnp.float32) * std, 'w_up': jax.random.normal(k[4], (E, C, 2 * H), jnp.float32) * std, 'w_down': jax.random.normal(k[5], (E, H, C), jnp.float32) * std}
    _L0_ffn_all = _L0_ffn_setup()
    _L0_ffn_in = {k: v for k, v in _L0_ffn_all.items() if k in ('w_gate', 'w_shared_up', 'w_shared_down', 'w_up', 'w_down')}
    del _L0_ffn_all
    return {'x': x, 'ctx_2048': ctx_2048, 'g_xattn': g_xattn, 'g_ffn': g_ffn, 'L0_xattn_Wq': _L0_xattn_in['Wq'], 'L0_xattn_bq': _L0_xattn_in['bq'], 'L0_xattn_Wk': _L0_xattn_in['Wk'], 'L0_xattn_bk': _L0_xattn_in['bk'], 'L0_xattn_Wv': _L0_xattn_in['Wv'], 'L0_xattn_bv': _L0_xattn_in['bv'], 'L0_xattn_Wo': _L0_xattn_in['Wo'], 'L0_xattn_bo': _L0_xattn_in['bo'], 'L0_ffn_w_gate': _L0_ffn_in['w_gate'], 'L0_ffn_w_shared_up': _L0_ffn_in['w_shared_up'], 'L0_ffn_w_shared_down': _L0_ffn_in['w_shared_down'], 'L0_ffn_w_up': _L0_ffn_in['w_up'], 'L0_ffn_w_down': _L0_ffn_in['w_down']}

def reference(x, ctx_2048, g_xattn, g_ffn, L0_xattn_Wq, L0_xattn_bq, L0_xattn_Wk, L0_xattn_bk, L0_xattn_Wv, L0_xattn_bv, L0_xattn_Wo, L0_xattn_bo, L0_ffn_w_gate, L0_ffn_w_shared_up, L0_ffn_w_shared_down, L0_ffn_w_up, L0_ffn_w_down):
    import jax
    import jax.numpy as jnp

    def _L0_xattn_ref(q, k, v, Wq, bq, Wk, bk, Wv, bv, Wo, bo):
        import jax, jax.numpy as jnp
        import numpy as np
        B, S, D, H = (4, 2048, 1024, 16)
        HD = D // H
        bs, sl, nf = q.shape
        Q = (q @ Wq.T + bq).reshape(bs, sl, H, HD)
        K = (k @ Wk.T + bk).reshape(bs, sl, H, HD)
        V = (v @ Wv.T + bv).reshape(bs, sl, H, HD)
        score = jnp.einsum('bshd,bsgd->bshg', Q, K)
        weight = jax.nn.softmax(score, axis=-1)
        attn = jnp.einsum('bshg,bsgd->bshd', weight, V).reshape(bs, sl, nf)
        return attn @ Wo.T + bo

    def _L0_ffn_ref(x, w_gate, w_shared_up, w_shared_down, w_up, w_down):
        import jax, jax.numpy as jnp
        import numpy as np
        TOPK = 6
        CAP = 512
        ROUTE_SCALE = 1.0
        B, T, C = x.shape
        E = w_gate.shape[1]
        x_flat = x.reshape(-1, C)
        N = x_flat.shape[0]
        su = x_flat @ w_shared_up
        y_s, g_s = jnp.split(su, 2, axis=-1)
        shared = jax.nn.silu(g_s) * y_s @ w_shared_down
        scores = jax.nn.sigmoid(x_flat @ w_gate)
        _, topk_idx = jax.lax.top_k(scores, TOPK)
        w = jnp.take_along_axis(scores, topk_idx, axis=-1)
        w = w / w.sum(-1, keepdims=True) * ROUTE_SCALE
        flat_e = topk_idx.reshape(-1)
        oh = jax.nn.one_hot(flat_e, E, dtype=jnp.int32)
        pos = jnp.take_along_axis(jnp.cumsum(oh, axis=0), flat_e[:, None], axis=1)[:, 0] - 1
        valid = pos < CAP
        pos_c = jnp.where(valid, pos, CAP - 1)
        token_ids = jnp.repeat(jnp.arange(N), TOPK)
        x_disp = jnp.zeros((E, CAP, C), x.dtype).at[flat_e, pos].set(x_flat[token_ids], mode='drop')
        up = jnp.einsum('ecd,edh->ech', x_disp, w_up)
        g_r, v_r = jnp.split(up, 2, axis=-1)
        h_r = jax.nn.silu(g_r) * v_r
        out_r = jnp.einsum('ech,ehd->ecd', h_r, w_down)
        y_ts = out_r[flat_e, pos_c]
        y_ts = jnp.where(valid[:, None], y_ts, 0.0)
        routed = (y_ts.reshape(N, TOPK, C) * w[:, :, None]).sum(axis=1)
        return (shared + routed).reshape(B, T, C)
    x = x + jnp.tanh(g_xattn[0]) * _L0_xattn_ref(_layernorm(x, axis=-1), ctx_2048, ctx_2048, L0_xattn_Wq, L0_xattn_bq, L0_xattn_Wk, L0_xattn_bk, L0_xattn_Wv, L0_xattn_bv, L0_xattn_Wo, L0_xattn_bo)
    x = x + jnp.tanh(g_ffn[0]) * _L0_ffn_ref(_layernorm(x, axis=-1), L0_ffn_w_gate, L0_ffn_w_shared_up, L0_ffn_w_shared_down, L0_ffn_w_up, L0_ffn_w_down)
    return x

_drawn_inputs = setup_inputs


def setup_inputs(seed=0):
    import zlib

    import numpy as np

    out = dict(_drawn_inputs(seed))
    spreads = {'L0_xattn_bq': (0.0, 0.1),
     'L0_xattn_bk': (0.0, 0.1),
     'L0_xattn_bv': (0.0, 0.1),
     'L0_xattn_bo': (0.0, 0.1)}
    factors = {'L0_ffn_w_gate': 8.0,
     'L0_ffn_w_shared_up': 8.0,
     'L0_ffn_w_shared_down': 8.0,
     'L0_ffn_w_up': 8.0,
     'L0_ffn_w_down': 8.0}
    for name, (base, spread) in spreads.items():
        noise = np.random.default_rng([zlib.crc32(name.encode()), seed]).standard_normal(out[name].shape)
        drawn = base * np.exp(spread * noise) if base else spread * noise
        out[name] = jnp.asarray(drawn.astype(out[name].dtype))
    for name, factor in factors.items():
        out[name] = (out[name] * factor).astype(out[name].dtype)
    return out
```

```python
from contextlib import ExitStack

import concourse.bass as bass
from concourse import mybir

F32 = mybir.dt.float32
F16 = mybir.dt.float16
BF16 = mybir.dt.bfloat16
I32 = mybir.dt.int32
U32 = mybir.dt.uint32
ALU = mybir.AluOpType
ACT = mybir.ActivationFunctionType
AX_X = mybir.AxisListType.X

P = 128
N = 4096
D = 1024
H = 16
HD = D // H
KC = D // P
EPS = 1e-5
SCALE = 64.0
NEG = -1e30

BLK = 256
NBLK = N // BLK
TOK = P // H
QUAD = 4
PEELED = 3
NQ = BLK // (TOK * QUAD)
NT = N // P

E = 64
TOPK = 6
CAP = 512
TPE = CAP // P
HR = 128
HS = 256




class Step:

    def __init__(self, base, register=None, factor=0):
        self.base, self.register, self.factor = base, register, factor

    def plus(self, n):
        return Step(self.base + n, self.register, self.factor)

    def half(self):
        return Step(self.base // 2, self.register, self.factor // 2)

    def times(self, per, extra=0):
        n = self.base * per + extra
        return max(n, 0) if self.register is None else self.register * (self.factor * per) + n


CHUNKS = 3 * KC
SLOT = [0, 2, 5, 8, 10, 13, 16, 18]
TURN = [12, 18]
STATS = [3, 4]


def work_after(n):
    found = []
    for q, s in enumerate(SLOT):
        for stage, lag in (("weighted", 4), ("turned", 3), ("values", 1), ("scores", 0)):
            if s + lag == n:
                found.append((stage, q))
    return sorted(found, key=lambda f: f[1])


def attention_phase(nc, persistent, x, ctx_t, w_qkv, b_qkv, attn_dram):
    ident, apart = persistent["ident"], persistent["apart"]
    with ExitStack() as ctx:
        def sb(name, shape, dt):
            return ctx.enter_context(nc.sbuf_tensor(name, shape, dt))

        def ps(name, shape, dt=F32):
            return ctx.enter_context(nc.psum_tensor(name, shape, dt))

        def sem(name):
            return ctx.enter_context(nc.semaphore(name))

        w_hi = sb("w_hi", [P, 3, KC, D], F16)
        w_lo = sb("w_lo", [P, 3, KC, D], F16)
        bias = sb("bias", [P, 3 * KC], F32)
        x_in = sb("x_in", [P, 2, D], F32)
        c_in = sb("c_in", [P, KC, BLK], F32)
        xt_hi = sb("xt_hi", [P, KC, BLK], F16)
        xt_lo = sb("xt_lo", [P, KC, BLK], F16)
        ct_hi = sb("ct_hi", [P, KC, BLK], F16)
        ct_lo = sb("ct_lo", [P, KC, BLK], F16)
        qkv = sb("qkv", [P, 2, 3, P, H], F32)
        probs = sb("probs", [P, 2, QUAD, P], F32)
        probs_t = sb("probs_t", [P, 2, QUAD, P], F32)
        values = sb("values", [P, 2, QUAD, HD], F32)
        attn = sb("attn", [P, 2, 2, KC, P], F32)
        stats = sb("stats", [P, 2, 2, 6], F32)
        moments = sb("moments", [P, 2, 2], F32)
        veps = sb("veps", [P, 2], F32)
        rstd = sb("rstd", [P, 2], F32)
        power = sb("power", [P, 1], F32)
        neg_max = sb("neg_max", [P, 2, QUAD], F32)
        sums = sb("sums", [P, 2, QUAD], F32)
        rsums = sb("rsums", [P, 2, QUAD], F32)
        own = sb("own", [TOK, P], BF16)
        others = sb("others", [TOK, QUAD * P], BF16)

        turn_ps = ps("turn_ps", [P, KC, P])
        proj_ps = [ps(f"proj_ps{i}", [P, 512]) for i in range(2)]
        score_ps = [ps(f"score_ps{i}", [P, QUAD, P]) for i in range(2)]
        probs_ps = ps("probs_ps", [P, QUAD, P])
        attn_ps = ps("attn_ps", [HD, QUAD, P])
        values_ps = turn_ps[:, 0:2, :].rearrange("p k (c d) -> p (k c) d", d=HD)

        w_landed = [sem(f"w_landed{i}") for i in range(4)]
        w_hi_made = sem("w_hi_made")
        w_lo_made = sem("w_lo_made")
        bias_landed = sem("bias_landed")
        consts_made = sem("consts_made")
        x_landed = sem("x_landed")
        c_landed = sem("c_landed")
        stats_made = sem("stats_made")
        moments_made = sem("moments_made")
        veps_made = sem("veps_made")
        rstd_made = sem("rstd_made")
        x_normed = sem("x_normed")
        x_turned = sem("x_turned")
        xt_hi_made = sem("xt_hi_made")
        xt_lo_made = sem("xt_lo_made")
        ct_hi_made = sem("ct_hi_made")
        ct_made = sem("ct_made")
        projected = sem("projected")
        even_kept = sem("even_kept")
        odd_kept = sem("odd_kept")
        scored = sem("scored")
        max_made = sem("max_made")
        exp_made = sem("exp_made")
        rsum_made = sem("rsum_made")
        probs_made = sem("probs_made")
        probs_turned = sem("probs_turned")
        probs_kept = sem("probs_kept")
        values_turned = sem("values_turned")
        values_kept = sem("values_kept")
        attn_made = sem("attn_made")
        attn_kept = sem("attn_kept")
        attn_stored = [sem(f"attn_stored{i}") for i in range(2)]

        stage_w = attn[:, :, :, :, :].rearrange("p a b k t -> p (a b) (k t)")

        def steps(eng, first, step):
            first()
            step(Step(0), True, False, True)
            for b in range(1, PEELED):
                step(Step(b), True, True, True)
            with eng.Fori(0, (NBLK - 1 - PEELED) // 2) as j:
                for r in range(2):
                    step(Step(PEELED + r, j, 2), True, True, True)
            step(Step(NBLK - 1), True, True, False)
            step(Step(NBLK), False, True, False)

        with nc.Block() as block:
            @block.sync
            def _(sp):
                sp.dma_start(bias[:], b_qkv).then_inc(bias_landed, 16)

                def load_x(b):
                    sp.wait_ge(x_turned, b.times(2))
                    sp.sem_inc(apart, 1)
                    sp.dma_start(x_in[:], x[bass.ds(b.times(BLK), BLK), :].rearrange("(a p) d -> p a d", p=P)
                                 ).then_inc(x_landed, 16)

                def load_ctx(b):
                    sp.wait_ge(ct_made, b.times(1))
                    sp.sem_inc(apart, 1)
                    sp.dma_start(c_in[:], ctx_t[:, bass.ds(b.times(BLK), BLK)].rearrange("(k p) t -> p k t", p=P)
                                 ).then_inc(c_landed, 16)

                def store(b):
                    sp.wait_ge(attn_kept, b.times(NQ, NQ))
                    sp.sem_inc(apart, 1)
                    par = b.base % 2
                    sp.dma_start(attn_dram[bass.ds(b.times(P), P), :],
                                 attn[:, par].rearrange("p a k t -> p (a k t)")).then_inc(attn_stored[par], 16)

                def first():
                    load_x(Step(0))
                    load_ctx(Step(0))
                    for m in range(CHUNKS):
                        sp.wait_ge(w_lo_made, max(m - 3, 0))
                        sp.sem_inc(apart, 1)
                        sp.dma_start(stage_w[:, m % 4, :], w_qkv[m * P:(m + 1) * P, :]).then_inc(w_landed[m % 4], 16)

                def step(b, proj, attend, more):
                    if more:
                        load_x(b.plus(1))
                        load_ctx(b.plus(1))
                    if attend:
                        store(b.plus(-1))

                steps(sp, first, step)
                for par in range(2):
                    sp.wait_ge(attn_stored[par], 16 * NBLK // 2)

            @block.gpsimd
            def _(pool):
                pool.memset(power[:], -0.5).then_inc(consts_made, 1)
                pool.memset(own[:], 0.0).then_inc(consts_made, 1)
                pool.memset(others[:], NEG).then_inc(consts_made, 1)
                pool.wait_ge(consts_made, 3)
                pool.affine_select(out=own[:].rearrange("k (t h) -> k t h", h=H),
                                   in_=own[:].rearrange("k (t h) -> k t h", h=H),
                                   compare_op=ALU.not_equal, fill=1.0, base=0,
                                   pattern=[[-1, TOK], [0, H]], channel_multiplier=1).then_inc(consts_made, 1)
                pool.affine_select(out=others[:].rearrange("k (g t h) -> k g t h", g=QUAD, h=H),
                                   in_=others[:].rearrange("k (g t h) -> k g t h", g=QUAD, h=H),
                                   compare_op=ALU.not_equal, fill=0.0, base=0,
                                   pattern=[[0, QUAD], [-1, TOK], [0, H]],
                                   channel_multiplier=1).then_inc(consts_made, 1)

                def deviation(b, t):
                    pool.wait_ge(moments_made, b.times(2, t + 1))
                    pool.sem_inc(apart, 1)
                    pool.tensor_scalar(veps[:, t:t + 1], moments[:, t, 1:2], EPS, None, ALU.add).then_inc(veps_made, 1)
                    pool.wait_ge(veps_made, b.times(2, t + 1))
                    pool.sem_inc(apart, 1)
                    pool.wait_ge(x_normed, b.times(2, t - 1))
                    pool.tensor_tensor(rstd[:, t:t + 1], veps[:, t:t + 1], power[:], ALU.pow).then_inc(rstd_made, 1)

                def split_ctx(b):
                    pool.wait_ge(ct_hi_made, b.times(1, 1))
                    pool.tensor_tensor(ct_lo[:], c_in[:], ct_hi[:], ALU.subtract).then_inc(ct_made, 1)

                def divide(a, q):
                    pool.wait_ge(rsum_made, a.times(NQ, q + 1))
                    pool.sem_inc(apart, 1)
                    pool.tensor_tensor(probs[:, q % 2], probs[:, q % 2],
                                       rsums[:, q % 2, :].unsqueeze(2).broadcast_to([P, QUAD, P]),
                                       ALU.mult).then_inc(probs_made, 1)

                def first():
                    for t in range(2):
                        deviation(Step(0), t)

                def step(b, proj, attend, more):
                    if proj:
                        split_ctx(b)
                    for n in range(CHUNKS):
                        if more and n in STATS:
                            deviation(b.plus(1), STATS.index(n))
                        if attend:
                            for stage, q in work_after(n - 1):
                                if stage == "scores":
                                    divide(b.plus(-1), q)

                steps(pool, first, step)

            @block.scalar
            def _(act):
                def split_ctx(b):
                    act.wait_ge(c_landed, b.times(16, 16))
                    act.wait_ge(projected, b.times(CHUNKS))
                    act.activation(ct_hi[:], c_in[:], ACT.Copy).then_inc(ct_hi_made, 1)

                def turn(b, t):
                    act.wait_ge(x_turned, b.times(2, t + 1))
                    act.wait_ge(projected, b.times(CHUNKS, KC - CHUNKS))
                    act.activation(xt_hi[:, :, t * P:(t + 1) * P], turn_ps[:], ACT.Copy).then_inc(xt_hi_made, 1)

                def keep(b, n):
                    par, part, head = b.base % 2, n // KC, 2 * (n % KC)
                    act.wait_ge(projected, b.times(CHUNKS, n + 1))
                    if n == 0:
                        act.wait_ge(attn_made, b.times(NQ, -NQ))
                    for half in range(2):
                        last = act.activation(qkv[half * HD:(half + 1) * HD, par, part, :, head],
                                              proj_ps[n % 2][0:HD, half * P:(half + 1) * P], ACT.Identity,
                                              bias=bias[0:HD, n:n + 1], scale=1.0 / SCALE)
                    last.then_inc(even_kept, 1)

                def exps(a, q):
                    act.wait_ge(max_made, a.times(NQ, q + 1))
                    act.wait_ge(probs_turned, a.times(NQ, q - 1))
                    act.wait_ge(rsum_made, a.times(NQ, q - 1))
                    for g in range(QUAD):
                        last = act.activation(probs[:, q % 2, g, :], score_ps[q % 2][:, g, :], ACT.Exp,
                                              bias=neg_max[:, q % 2, g:g + 1],
                                              accum_out=sums[:, q % 2, g:g + 1])
                    last.then_inc(exp_made, 1)

                def keep_probs(a, q):
                    act.wait_ge(probs_turned, a.times(NQ, q + 1))
                    act.wait_ge(attn_made, a.times(NQ, q - 1))
                    act.activation(probs_t[:, q % 2], probs_ps[:], ACT.Copy).then_inc(probs_kept, 1)

                def first():
                    for m in range(CHUNKS):
                        act.wait_ge(w_landed[m % 4], 16 * (m // 4 + 1))
                        act.activation(w_hi[:, m // KC, m % KC, :], stage_w[:, m % 4, :], ACT.Copy, scale=SCALE
                                       ).then_inc(w_hi_made, 1)
                    for t in range(2):
                        turn(Step(0), t)
                    act.wait_ge(bias_landed, 16)

                def step(b, proj, attend, more):
                    if proj:
                        split_ctx(b)
                    for n in range(CHUNKS):
                        if proj:
                            keep(b, n)
                        if attend:
                            for stage, q in work_after(n):
                                if stage == "scores":
                                    exps(b.plus(-1), q)
                                if stage == "turned":
                                    keep_probs(b.plus(-1), q)
                        if more and n in TURN:
                            turn(b.plus(1), TURN.index(n))

                steps(act, first, step)

            @block.vector
            def _(dve):
                def moment(b, t):
                    dve.wait_ge(x_landed, b.times(16, 16))
                    for half in range(2):
                        last = dve.bn_stats(stats[:, t, half, :], x_in[:, t, half * 512:(half + 1) * 512])
                    last.then_inc(stats_made, 1)
                    dve.wait_ge(stats_made, b.times(2, t + 1))
                    dve.wait_ge(x_normed, b.times(2, t - 1))
                    dve.sem_inc(apart, 1)
                    dve.bn_aggr(moments[:, t, :], stats[:, t]).then_inc(moments_made, 1)

                def norm(b, t):
                    dve.wait_ge(rstd_made, b.times(2, t + 1))
                    dve.tensor_scalar(x_in[:, t, :], x_in[:, t, :], moments[:, t, 0:1], rstd[:, t:t + 1],
                                      ALU.subtract, ALU.mult).then_inc(x_normed, 1)

                def turn(b, t):
                    dve.wait_ge(xt_hi_made, b.times(2, t + 1))
                    dve.tensor_tensor(xt_lo[:, :, t * P:(t + 1) * P], turn_ps[:], xt_hi[:, :, t * P:(t + 1) * P],
                                      ALU.subtract).then_inc(xt_lo_made, 1)

                def keep(b, n):
                    par, part, head = b.base % 2, n // KC, 2 * (n % KC) + 1
                    dve.wait_ge(projected, b.times(CHUNKS, n + 1))
                    if n == 0:
                        dve.wait_ge(attn_made, b.times(NQ, -NQ))
                    for half in range(2):
                        last = dve.tensor_scalar(qkv[half * HD:(half + 1) * HD, par, part, :, head],
                                                 proj_ps[n % 2][HD:P, half * P:(half + 1) * P],
                                                 1.0 / SCALE, bias[HD:P, n:n + 1], ALU.mult, ALU.add)
                    last.then_inc(odd_kept, 1)

                def maxima(a, q):
                    dve.wait_ge(scored, a.times(NQ, q + 1))
                    dve.wait_ge(exp_made, a.times(NQ, q - 1))
                    dve.tensor_reduce(neg_max[:, q % 2, :], score_ps[q % 2][:], AX_X, ALU.max, negate=True
                                      ).then_inc(max_made, 1)

                def inverses(a, q):
                    dve.wait_ge(exp_made, a.times(NQ, q + 1))
                    dve.wait_ge(probs_made, a.times(NQ, q - 1))
                    dve.reciprocal(rsums[:, q % 2, :], sums[:, q % 2, :]).then_inc(rsum_made, 1)

                def keep_values(a, q):
                    dve.wait_ge(values_turned, a.times(NQ, q + 1))
                    dve.wait_ge(attn_made, a.times(NQ, q - 1))
                    dve.tensor_copy(values[:, q % 2], values_ps).then_inc(values_kept, 1)

                def keep_attn(a, q):
                    par, half, t0 = a.base % 2, q % 2, (q // 2) * TOK * QUAD
                    dve.wait_ge(attn_made, a.times(NQ, q + 1))
                    if q == 0:
                        dve.wait_ge(attn_stored[par], a.half().times(16))
                    got = attn_ps[:].rearrange("d g (t o r) -> d r o (g t)", o=KC, r=2)
                    for r in range(2):
                        last = dve.tensor_copy(attn[r * HD:(r + 1) * HD, par, half, :, t0:t0 + TOK * QUAD],
                                               got[:, r])
                    last.then_inc(attn_kept, 1)

                def first():
                    for t in range(2):
                        moment(Step(0), t)
                    for t in range(2):
                        norm(Step(0), t)
                    for m in range(CHUNKS):
                        dve.wait_ge(w_hi_made, m + 1)
                        dve.scalar_tensor_tensor(w_lo[:, m // KC, m % KC, :], stage_w[:, m % 4, :], SCALE,
                                                 w_hi[:, m // KC, m % KC, :], ALU.mult, ALU.subtract
                                                 ).then_inc(w_lo_made, 1)
                    for t in range(2):
                        turn(Step(0), t)
                    dve.wait_ge(bias_landed, 16)

                def step(b, proj, attend, more):
                    for n in range(CHUNKS):
                        if proj:
                            keep(b, n)
                        if attend:
                            for stage, q in work_after(n - 1):
                                if stage == "scores":
                                    inverses(b.plus(-1), q)
                            for stage, q in work_after(n):
                                if stage == "scores":
                                    maxima(b.plus(-1), q)
                                if stage == "values":
                                    keep_values(b.plus(-1), q)
                                if stage == "weighted":
                                    keep_attn(b.plus(-1), q)
                        if more and n in STATS:
                            moment(b.plus(1), STATS.index(n))
                        if more and n - 2 in STATS:
                            norm(b.plus(1), STATS.index(n - 2))
                        if more and n in TURN:
                            turn(b.plus(1), TURN.index(n))

                steps(dve, first, step)

            @block.tensor
            def _(pe):
                def turn(b, t):
                    pe.wait_ge(x_normed, b.times(2, t + 1))
                    pe.wait_ge(xt_lo_made, b.times(2, t))
                    if b.base >= 2:
                        ahead = sum(s + 1 <= TURN[t] for s in SLOT)
                        pe.wait_ge(values_kept, b.plus(-2).times(NQ, ahead))
                    for k in range(KC):
                        last = pe.transpose(turn_ps[:, k, :], x_in[:, t, k * P:(k + 1) * P], ident[:])
                    last.then_inc(x_turned, 1)

                def project(b, n):
                    part, o = n // KC, n % KC
                    if n == 0:
                        pe.wait_ge(xt_lo_made, b.times(2, 2))
                    if n == KC:
                        pe.wait_ge(ct_made, b.times(1, 1))
                    pe.wait_ge(even_kept, b.times(CHUNKS, n - 1))
                    pe.wait_ge(odd_kept, b.times(CHUNKS, n - 1))
                    hi, lo = (xt_hi, xt_lo) if part == 0 else (ct_hi, ct_lo)
                    out = proj_ps[n % 2][:, 0:BLK]
                    for k in range(KC):
                        wh, wl = (w[:, part, k, o * P:(o + 1) * P] for w in (w_hi, w_lo))
                        pe.matmul(out, wh, hi[:, k, :], start=(k == 0), stop=False)
                        pe.matmul(out, wh, lo[:, k, :], start=False, stop=False)
                        last = pe.matmul(out, wl, hi[:, k, :], start=False, stop=(k == KC - 1))
                    last.then_inc(projected, 1)

                def rows(q):
                    half = q % 2
                    return slice(half * HD, (half + 1) * HD)

                def group(a, part, q, g):
                    t0 = ((q // 2) * QUAD + g) * TOK
                    return qkv[rows(q), a.base % 2, part, t0:t0 + TOK, :].rearrange("d t h -> d (t h)")

                def scores(a, q):
                    if q == 0:
                        pe.wait_ge(even_kept, a.times(CHUNKS, CHUNKS))
                        pe.wait_ge(odd_kept, a.times(CHUNKS, CHUNKS))
                    pe.wait_ge(exp_made, a.times(NQ, q - 1))
                    out = score_ps[q % 2]
                    pe.matmul(out[:].rearrange("p g c -> p (g c)"), own[:], others[:], start=True, stop=False,
                              skip_group_check=True)
                    for g in range(QUAD):
                        last = pe.matmul(out[:, g, :], group(a, 0, q, g), group(a, 1, q, g), start=False, stop=True,
                                         skip_group_check=True)
                    last.then_inc(scored, 1)

                def turn_values(a, q):
                    pe.wait_ge(values_kept, a.times(NQ, q))
                    ahead = a.plus(2).times(2, sum(SLOT[q] + 1 > n for n in TURN))
                    pe.wait_ge(xt_lo_made, min(ahead, 2 * NBLK) if isinstance(ahead, int) else ahead)
                    pe.sem_inc(apart, 1)
                    for g in range(QUAD):
                        last = pe.transpose(values_ps[:, g, :], group(a, 2, q, g), ident[rows(q), rows(q)])
                    last.then_inc(values_turned, 1)

                def turn_probs(a, q):
                    pe.wait_ge(probs_made, a.times(NQ, q + 1))
                    pe.wait_ge(probs_kept, a.times(NQ, q))
                    for g in range(QUAD):
                        last = pe.transpose(probs_ps[:, g, :], probs[:, q % 2, g, :], ident[:])
                    last.then_inc(probs_turned, 1)

                def weigh(a, q):
                    pe.wait_ge(probs_kept, a.times(NQ, q + 1))
                    pe.wait_ge(values_kept, a.times(NQ, q + 1))
                    pe.wait_ge(attn_kept, a.times(NQ, q))
                    for g in range(QUAD):
                        last = pe.matmul(attn_ps[:, g, :], values[:, q % 2, g, :], probs_t[:, q % 2, g, :],
                                         start=True, stop=True)
                    last.then_inc(attn_made, 1)

                def first():
                    pe.wait_ge(consts_made, 5)
                    for t in range(2):
                        turn(Step(0), t)
                    pe.wait_ge(w_lo_made, CHUNKS)

                def step(b, proj, attend, more):
                    for n in range(CHUNKS):
                        if proj:
                            project(b, n)
                        if attend:
                            for stage, q in work_after(n):
                                {"scores": scores, "values": turn_values, "turned": turn_probs,
                                 "weighted": weigh}[stage](b.plus(-1), q)
                        if more and n in TURN:
                            turn(b.plus(1), TURN.index(n))

                steps(pe, first, step)


def routing_phase(nc, persistent, x, w_o, b_o, gains, w_gate, w_shared_up, w_shared_down, attn_dram,
                  rows_dram, base_dram, table_dram):
    ident, gates, apart = persistent["ident"], persistent["gates"], persistent["apart"]
    places, weights = persistent["places"], persistent["weights"]
    with ExitStack() as ctx:
        def sb(name, shape, dt):
            return ctx.enter_context(nc.sbuf_tensor(name, shape, dt))

        def ps(name, shape, dt=F32):
            return ctx.enter_context(nc.psum_tensor(name, shape, dt))

        def sem(name):
            return ctx.enter_context(nc.semaphore("r_" + name))

        def pair(name, shape):
            return sb(name + "_hi", shape, F16), sb(name + "_lo", shape, F16)

        HC = HS // P
        wo = pair("wo", [P, KC, D])
        wg = pair("wg", [P, KC, E])
        wu = pair("wu", [P, KC, 2 * HS])
        wd = pair("wd", [P, HC, D])
        stage_w = sb("stage_w", [P, 4, D], F32)
        bo_row = sb("bo_row", [P, D], F32)
        x_in = sb("rx_in", [P, 2, D], F32)
        a_in = sb("a_in", [P, 2, KC, P], F32)
        at = pair("at", [P, KC, P])
        y = sb("y", [P, 2, D], F32)
        yn = sb("yn", [P, 2, D], F32)
        yt = pair("yt", [P, KC, P])
        gsig = sb("gsig", [P, HS], F32)
        gated = sb("gated", [P, HS], F32)
        hidden = sb("hidden", [P, HS], F32)
        ht = pair("ht", [P, HC, P])
        base = sb("base", [P, 2, D], F32)
        stats = sb("rstats", [P, 2, 6], F32)
        moments = sb("rmoments", [P, 2], F32)
        veps = sb("rveps", [P, 1], F32)
        rstd = sb("rrstd", [P, 1], F32)
        power = sb("rpower", [P, 1], F32)
        score = sb("score", [P, E], F32)
        best = sb("best", [P, 8], F32)
        best_at = sb("best_at", [P, 8], U32)
        expert = sb("expert", [P, TOPK], F32)
        number = sb("number", [P, E], F32)
        chosen = sb("chosen", [P, TOPK, E], BF16)
        member = sb("member", [P, E], BF16)
        members = sb("members", [P, E], BF16)
        earlier = sb("earlier", [P, P], BF16)
        ones = sb("ones", [P, P], BF16)
        picked = sb("picked", [P, TOPK, E], F32)
        pos = sb("pos", [P, TOPK], F32)
        total = sb("total", [P, 1], F32)
        rtotal = sb("rtotal", [P, 1], F32)
        valid = sb("valid", [P, TOPK], F32)
        tile1 = sb("tile1", [P, TOPK], F32)
        tile2 = sb("tile2", [P, TOPK], F32)
        tile3 = sb("tile3", [P, TOPK], F32)
        four_e = sb("four_e", [P, TOPK], F32)
        raw = sb("raw", [P, TOPK], F32)
        capped = sb("capped", [P, TOPK], F32)
        entry = sb("entry", [P, 2, TOPK], I32)
        tokens = sb("tokens", [P, 2], I32)
        zeros = sb("zeros", [P, E * TPE], I32)

        o_ps = ps("o_ps", [P, D])
        turn_ps = ps("rturn_ps", [P, KC, P])
        up_ps = ps("up_ps", [P, 2 * HS])
        misc_ps = ps("misc_ps", [P, 512])
        down_ps = ps("down_ps", [P, D])
        gate_ps = misc_ps[:, 0:E]
        pos_ps = misc_ps[:, E:2 * E]
        ht_ps = misc_ps[:, 2 * P:2 * P + HS].rearrange("p (c t) -> p c t", c=HC)

        consts_made = sem("consts_made")
        w_landed = [sem(f"w_landed{i}") for i in range(4)]
        w_hi_made = sem("w_hi_made")
        w_lo_made = sem("w_lo_made")
        row_landed = sem("row_landed")
        bo_made = sem("bo_made")
        table_cleared = sem("table_cleared")
        x_landed = [sem(f"x_landed{i}") for i in range(2)]
        a_landed = [sem(f"a_landed{i}") for i in range(2)]
        at_hi_made = sem("at_hi_made")
        at_lo_made = sem("at_lo_made")
        x_biased = sem("x_biased")
        o_made = sem("o_made")
        y_made = sem("y_made")
        stats_made = sem("stats_made")
        moments_made = sem("moments_made")
        veps_made = sem("veps_made")
        rstd_made = sem("rstd_made")
        y_normed = sem("y_normed")
        rows_stored = [sem(f"rows_stored{i}") for i in range(2)]
        y_turned = sem("y_turned")
        yt_hi_made = sem("yt_hi_made")
        yt_lo_made = sem("yt_lo_made")
        gate_done = sem("gate_done")
        score_made = sem("score_made")
        up_made = sem("up_made")
        gsig_made = sem("gsig_made")
        gated_made = sem("gated_made")
        hidden_made = sem("hidden_made")
        h_turned = sem("h_turned")
        ht_hi_made = sem("ht_hi_made")
        ht_lo_made = sem("ht_lo_made")
        down_made = sem("down_made")
        base_made = sem("base_made")
        base_stored = [sem(f"base_stored{i}") for i in range(2)]
        member_made = sem("member_made")
        members_added = sem("members_added")
        route_step = sem("route_step")
        entry_made = sem("entry_made")
        scattered = [sem(f"scattered{i}") for i in range(2)]
        tokens_made = sem("tokens_made")
        table_landed = sem("table_landed")

        jobs = [(w_o[k * P:(k + 1) * P, :], D, wo[0][:, k, :], wo[1][:, k, :]) for k in range(KC)]
        jobs += [(w_shared_up[k * P:(k + 1) * P, :], 2 * HS, wu[0][:, k, :], wu[1][:, k, :]) for k in range(KC)]
        jobs += [(w_shared_down[k * P:(k + 1) * P, :], D, wd[0][:, k, :], wd[1][:, k, :]) for k in range(HC)]
        jobs += [(w_gate[k * P:(k + 1) * P, :], E, wg[0][:, k, :], wg[1][:, k, :]) for k in range(KC)]
        CHAIN = 17

        def steps(eng, first, step):
            first()
            for t in range(4):
                step(Step(t), True, t >= 1, t >= 2)
            with eng.Fori(0, (NT - 6) // 2) as j:
                for r in range(2):
                    step(Step(4 + r, j, 2), True, True, True)
            step(Step(NT - 2), True, True, True)
            step(Step(NT - 1), True, True, True)
            step(Step(NT), False, True, True)
            step(Step(NT + 1), False, False, True)

        with nc.Block() as block:
            @block.sync
            def _(sp):
                def load(t):
                    par = t.base % 2
                    sp.wait_ge(y_made, t.times(1, -1))
                    sp.sem_inc(apart, 1)
                    sp.dma_start(x_in[:, par], x[bass.ds(t.times(P), P), :]).then_inc(x_landed[par], 16)
                    sp.wait_ge(at_lo_made, t.times(1, -1))
                    sp.sem_inc(apart, 1)
                    half = par
                    sp.dma_start(a_in[:, par].rearrange("p k t -> p (k t)"),
                                 attn_dram[bass.ds(t.plus(-half).times(P // 2), P), half * D:(half + 1) * D]
                                 ).then_inc(a_landed[par], 16)

                def first():
                    sp.dma_start(bo_row[:], b_o.to_broadcast([P, D])).then_inc(row_landed, 16)
                    sp.wait_ge(consts_made, 7)
                    sp.dma_start(table_dram.rearrange("(p c) o -> p (c o)", p=P), zeros[:]).then_inc(table_cleared, 16)
                    for m, (source, width, _, _) in enumerate(jobs):
                        sp.wait_ge(w_lo_made, max(m - 3, 0))
                        sp.sem_inc(apart, 1)
                        sp.dma_start(stage_w[:, m % 4, 0:width], source).then_inc(w_landed[m % 4], 16)
                    load(Step(0))

                def step(t, project, up, down):
                    if isinstance(t.times(1), int) and t.base + 1 >= NT:
                        pass
                    else:
                        load(t.plus(1))
                    if up:
                        s = t.plus(-1)
                        sp.wait_ge(y_normed, s.times(1, 1))
                        sp.sem_inc(apart, 1)
                        sp.dma_start(rows_dram[bass.ds(s.times(P), P), :], yn[:, s.base % 2]
                                     ).then_inc(rows_stored[s.base % 2], 16)
                    if down:
                        s = t.plus(-2)
                        sp.wait_ge(base_made, s.times(1, 1))
                        sp.sem_inc(apart, 1)
                        sp.dma_start(base_dram[bass.ds(s.times(P), P), :], base[:, s.base % 2]
                                     ).then_inc(base_stored[s.base % 2], 16)

                steps(sp, first, step)
                for par in range(2):
                    sp.wait_ge(rows_stored[par], 16 * NT // 2)
                    sp.wait_ge(base_stored[par], 16 * NT // 2)

            @block.gpsimd
            def _(pool):
                pool.memset(power[:], -0.5).then_inc(consts_made, 1)
                pool.memset(ones[:], 1.0).then_inc(consts_made, 1)
                pool.memset(earlier[:], 1.0).then_inc(consts_made, 1)
                pool.memset(zeros[:], 0).then_inc(consts_made, 1)
                pool.memset(members[:], 0.0).then_inc(consts_made, 1)
                pool.iota(number[:], pattern=[[1, E]], base=0, channel_multiplier=0,
                          allow_small_or_imprecise_dtypes=True).then_inc(consts_made, 1)
                pool.wait_ge(consts_made, 6)
                pool.affine_select(out=earlier[:], in_=earlier[:], compare_op=ALU.is_gt, fill=0.0, base=0,
                                   pattern=[[1, P]], channel_multiplier=-1).then_inc(consts_made, 1)
                for r in range(2):
                    pool.iota(tokens[:, r:r + 1], pattern=[[0, 1]], base=r * P, channel_multiplier=1
                              ).then_inc(tokens_made, 1)

                def split_attn(t):
                    par = t.base % 2
                    pool.wait_ge(at_hi_made, t.times(1, 1))
                    pool.sem_inc(apart, 1)
                    pool.tensor_tensor(at[1][:], a_in[:, par], at[0][:], ALU.subtract).then_inc(at_lo_made, 1)
                    pool.wait_ge(x_landed[par], t.half().times(16, 16))
                    pool.sem_inc(apart, 1)
                    pool.tensor_tensor(x_in[:, par], x_in[:, par], bo_row[:], ALU.add).then_inc(x_biased, 1)

                def deviation(t):
                    pool.wait_ge(moments_made, t.times(1, 1))
                    pool.sem_inc(apart, 1)
                    pool.tensor_scalar(veps[:], moments[:, 1:2], EPS, None, ALU.add).then_inc(veps_made, 1)
                    pool.wait_ge(veps_made, t.times(1, 1))
                    pool.sem_inc(apart, 1)
                    pool.wait_ge(y_normed, t.times(1))
                    pool.tensor_tensor(rstd[:], veps[:], power[:], ALU.pow).then_inc(rstd_made, 1)

                def scatter(t):
                    par = t.base % 2
                    pool.wait_ge(entry_made, t.times(1, 1))
                    pool.sem_inc(apart, 1)
                    pool.wait_ge(tokens_made, t.times(1, 1))
                    pool.sem_inc(apart, 1)
                    for k in range(TOPK):
                        pool.indirect_dma_start(
                            out=table_dram, out_offset=bass.IndirectOffsetOnAxis(ap=entry[:, par, k:k + 1], axis=0),
                            in_=tokens[:, par:par + 1], in_offset=None, bounds_check=E * CAP - 1,
                            oob_is_err=False).then_inc(scattered[par], 16)

                def advance(t):
                    par = t.base % 2
                    pool.wait_ge(scattered[par], t.half().times(16 * TOPK, 16 * TOPK))
                    pool.sem_inc(apart, 1)
                    pool.tensor_scalar(tokens[:, par:par + 1], tokens[:, par:par + 1], 2 * P, None, ALU.add
                                       ).then_inc(tokens_made, 1)

                def first():
                    pool.wait_ge(bo_made, 1)
                    pool.wait_ge(table_cleared, 16)
                    split_attn(Step(0))

                def step(t, project, up, down):
                    if not (isinstance(t.times(1), int) and t.base + 1 >= NT):
                        split_attn(t.plus(1))
                    if project:
                        deviation(t)
                    if down:
                        if t.base >= 4:
                            advance(t.plus(-4))
                        scatter(t.plus(-2))

                steps(pool, first, step)
                for r in range(2):
                    pool.wait_ge(scattered[r], 16 * TOPK * NT // 2)

            @block.scalar
            def _(act):
                def split_attn(t):
                    act.wait_ge(a_landed[t.base % 2], t.half().times(16, 16))
                    act.wait_ge(o_made, t.times(1))
                    act.activation(at[0][:], a_in[:, t.base % 2], ACT.Copy).then_inc(at_hi_made, 1)

                def first():
                    for m, (_, width, hi, _) in enumerate(jobs):
                        act.wait_ge(w_landed[m % 4], 16 * (m // 4 + 1))
                        act.activation(hi, stage_w[:, m % 4, 0:width], ACT.Copy, scale=SCALE).then_inc(w_hi_made, 1)
                    act.wait_ge(row_landed, 16)
                    act.activation(bo_row[:], bo_row[:], ACT.Copy, scale=gates[:, 0:1]).then_inc(bo_made, 1)
                    split_attn(Step(0))

                def step(t, project, up, down):
                    if down:
                        s = t.plus(-2)
                        act.wait_ge(h_turned, s.times(1, 1))
                        act.wait_ge(down_made, s.times(1))
                        act.activation(ht[0][:], ht_ps, ACT.Copy).then_inc(ht_hi_made, 1)
                    if up:
                        s = t.plus(-1)
                        act.wait_ge(y_turned, s.times(1, 1))
                        act.wait_ge(up_made, s.times(1))
                        act.activation(yt[0][:], turn_ps[:], ACT.Copy).then_inc(yt_hi_made, 1)
                    if not (isinstance(t.times(1), int) and t.base + 1 >= NT):
                        split_attn(t.plus(1))
                    if up:
                        s = t.plus(-1)
                        act.wait_ge(gate_done, s.times(1, 1))
                        act.wait_ge(member_made, s.times(1))
                        act.activation(score[:], gate_ps, ACT.Sigmoid, scale=1.0 / SCALE).then_inc(score_made, 1)
                        act.wait_ge(up_made, s.times(1, 1))
                        act.wait_ge(gated_made, s.times(1))
                        act.activation(gsig[:], up_ps[:, HS:2 * HS], ACT.Sigmoid, scale=1.0 / SCALE
                                       ).then_inc(gsig_made, 1)

                steps(act, first, step)

            @block.vector
            def _(dve):
                def norm(t):
                    par = t.base % 2
                    dve.wait_ge(rows_stored[par], t.half().times(16))
                    dve.wait_ge(y_turned, t.times(1, -1))
                    dve.wait_ge(rstd_made, t.times(1, 1))
                    dve.tensor_scalar(yn[:, par], y[:, par], moments[:, 0:1], rstd[:], ALU.subtract, ALU.mult
                                      ).then_inc(y_normed, 1)

                def route(t):
                    dve.wait_ge(score_made, t.times(1, 1))
                    dve.sem_inc(apart, 1)
                    chain = Step(t.base * CHAIN, t.register, t.factor * CHAIN)

                    def link(n, ins):
                        ins.then_inc(route_step, 1)
                        dve.wait_ge(route_step, chain.times(1, n + 1))
                        dve.sem_inc(apart, 1)

                    link(0, dve.max(out=best[:], in_=score[:]))
                    link(1, dve.max_index(out=best_at[:], in_max=best[:], in_values=score[:]))
                    link(2, dve.tensor_copy(expert[:], best_at[:, 0:TOPK]))
                    link(3, dve.tensor_tensor(chosen[:], number[:].unsqueeze(1).broadcast_to([P, TOPK, E]),
                                              expert[:].unsqueeze(2).broadcast_to([P, TOPK, E]), ALU.is_equal))
                    dve.wait_ge(h_turned, t.times(1))
                    with nc.allow_low_precision("small whole numbers"):
                        dve.tensor_reduce(member[:], chosen[:].rearrange("p k e -> p e k"), AX_X, ALU.add
                                          ).then_inc(member_made, 1)
                    link(4, dve.reduce_sum(total[:], best[:, 0:TOPK], AX_X))
                    link(5, dve.reciprocal(rtotal[:], total[:]))
                    link(6, dve.tensor_scalar(four_e[:], expert[:], float(TPE), None, ALU.mult))

                def place(t):
                    dve.wait_ge(ht_hi_made, t.times(1, 1))
                    chain = Step(t.base * CHAIN, t.register, t.factor * CHAIN)
                    par = t.base % 2

                    def link(n, ins):
                        ins.then_inc(route_step, 1)
                        dve.wait_ge(route_step, chain.times(1, n + 1))
                        dve.sem_inc(apart, 1)

                    dve.tensor_tensor(members[:], members[:], member[:], ALU.add).then_inc(members_added, 1)
                    link(7, dve.tensor_tensor(picked[:], chosen[:], pos_ps.unsqueeze(1).broadcast_to([P, TOPK, E]),
                                              ALU.mult))
                    link(8, dve.tensor_reduce(pos[:], picked[:], AX_X, ALU.add))
                    link(9, dve.tensor_scalar(valid[:], pos[:], float(CAP), rtotal[:], ALU.is_lt, ALU.mult))
                    link(10, dve.tensor_scalar(tile1[:], pos[:], float(P), None, ALU.is_ge))
                    link(11, dve.scalar_tensor_tensor(tile2[:], pos[:], 2.0 * P, tile1[:], ALU.is_ge, ALU.add))
                    link(12, dve.scalar_tensor_tensor(tile3[:], pos[:], 3.0 * P, tile2[:], ALU.is_ge, ALU.add))
                    link(13, dve.scalar_tensor_tensor(raw[:], pos[:], float(E * TPE), four_e[:], ALU.mult, ALU.add))
                    dve.wait_ge(scattered[par], t.half().times(16 * TOPK))
                    dve.scalar_tensor_tensor(entry[:, par], tile3[:], float(1 - P * E * TPE), raw[:], ALU.mult, ALU.add
                                             ).then_inc(entry_made, 1)
                    link(14, dve.tensor_scalar(capped[:], pos[:], CAP - 1.0, None, ALU.min))
                    link(15, dve.scalar_tensor_tensor(places[:, bass.ds(t.times(TOPK), TOPK)], expert[:], float(CAP),
                                                      capped[:], ALU.mult, ALU.add))
                    link(16, dve.scalar_tensor_tensor(weights[:, bass.ds(t.times(TOPK), TOPK)], best[:, 0:TOPK],
                                                      gates[:, 1:2], valid[:], ALU.mult, ALU.mult))

                def first():
                    for m, (_, width, hi, lo) in enumerate(jobs):
                        dve.wait_ge(w_hi_made, m + 1)
                        dve.scalar_tensor_tensor(lo, stage_w[:, m % 4, 0:width], SCALE, hi, ALU.mult, ALU.subtract
                                                 ).then_inc(w_lo_made, 1)
                    dve.wait_ge(consts_made, 7)

                def step(t, project, up, down):
                    if down:
                        s = t.plus(-2)
                        dve.wait_ge(ht_hi_made, s.times(1, 1))
                        dve.tensor_tensor(ht[1][:], ht_ps, ht[0][:], ALU.subtract).then_inc(ht_lo_made, 1)
                    if up:
                        s = t.plus(-1)
                        dve.wait_ge(yt_hi_made, s.times(1, 1))
                        dve.tensor_tensor(yt[1][:], turn_ps[:], yt[0][:], ALU.subtract).then_inc(yt_lo_made, 1)
                    if down:
                        s = t.plus(-2)
                        place(s)
                        dve.wait_ge(down_made, s.times(1, 1))
                        dve.wait_ge(base_stored[s.base % 2], s.half().times(16))
                        dve.scalar_tensor_tensor(base[:, s.base % 2], down_ps[:], gates[:, 3:4], y[:, s.base % 2],
                                                 ALU.mult, ALU.add).then_inc(base_made, 1)
                    if project:
                        dve.wait_ge(o_made, t.times(1, 1))
                        dve.wait_ge(x_biased, t.times(1, 1))
                        dve.wait_ge(y_normed, t.times(1, -1))
                        dve.wait_ge(base_made, t.times(1, -1))
                        dve.scalar_tensor_tensor(y[:, t.base % 2], o_ps[:], gates[:, 2:3], x_in[:, t.base % 2],
                                                 ALU.mult, ALU.add).then_inc(y_made, 1)
                        dve.wait_ge(y_made, t.times(1, 1))
                        for half in range(2):
                            last = dve.bn_stats(stats[:, half, :], y[:, t.base % 2, half * 512:(half + 1) * 512])
                        last.then_inc(stats_made, 1)
                        dve.wait_ge(stats_made, t.times(1, 1))
                        dve.wait_ge(y_normed, t.times(1))
                        dve.sem_inc(apart, 1)
                        dve.bn_aggr(moments[:], stats[:]).then_inc(moments_made, 1)
                        norm(t)
                    if up:
                        s = t.plus(-1)
                        route(s)
                        dve.wait_ge(gsig_made, s.times(1, 1))
                        dve.scalar_tensor_tensor(gated[:], up_ps[:, HS:2 * HS], 1.0 / SCALE ** 2, gsig[:],
                                                 ALU.mult, ALU.mult).then_inc(gated_made, 1)
                        dve.wait_ge(gated_made, s.times(1, 1))
                        dve.wait_ge(h_turned, s.times(1))
                        dve.tensor_tensor(hidden[:], gated[:], up_ps[:, 0:HS], ALU.mult).then_inc(hidden_made, 1)

                steps(dve, first, step)

            @block.tensor
            def _(pe):
                def three(out, stationary, moving, chunks, last_inc=None):
                    for c in range(chunks):
                        pe.matmul(out, stationary(0, c), moving(0, c), start=(c == 0), stop=False)
                        pe.matmul(out, stationary(0, c), moving(1, c), start=False, stop=False)
                        last = pe.matmul(out, stationary(1, c), moving(0, c), start=False, stop=(c == chunks - 1))
                    return last

                def project(t, half):
                    cols = slice(half * 512, (half + 1) * 512)
                    if half == 0:
                        pe.wait_ge(at_lo_made, t.times(1, 1))
                        pe.wait_ge(y_made, t.times(1))
                    last = three(o_ps[:, cols], lambda i, c: at[i][:, c, :], lambda i, c: wo[i][:, c, cols], KC)
                    if half == 1:
                        last.then_inc(o_made, 1)

                def first():
                    pe.wait_ge(consts_made, 7)
                    pe.wait_ge(w_lo_made, len(jobs))

                def step(t, project_it, up, down):
                    if project_it:
                        project(t, 0)
                    if down:
                        s = t.plus(-2)
                        pe.wait_ge(hidden_made, s.times(1, 1))
                        pe.wait_ge(score_made, s.times(1, 1))
                        pe.wait_ge(ht_lo_made, s.times(1))
                        pe.wait_ge(member_made, s.times(1, 1))
                        pe.wait_ge(members_added, s.times(1))
                        pe.wait_ge(route_step, Step(s.base * CHAIN, s.register, s.factor * CHAIN).times(1))
                        pe.matmul(pos_ps, earlier[:], member[:], start=True, stop=False)
                        pe.matmul(pos_ps, ones[:], members[:], start=False, stop=True)
                        for c in range(HC):
                            last = pe.transpose(ht_ps[:, c, :], hidden[:, c * P:(c + 1) * P], ident[:])
                        last.then_inc(h_turned, 1)
                    if up:
                        s = t.plus(-1)
                        pe.wait_ge(y_normed, s.times(1, 1))
                        pe.wait_ge(yt_lo_made, s.times(1))
                        for k in range(KC):
                            last = pe.transpose(turn_ps[:, k, :], yn[:, s.base % 2, k * P:(k + 1) * P], ident[:])
                        last.then_inc(y_turned, 1)
                    if down:
                        s = t.plus(-2)
                        pe.wait_ge(ht_lo_made, s.times(1, 1))
                        pe.wait_ge(base_made, s.times(1))
                        for half in range(2):
                            cols = slice(half * 512, (half + 1) * 512)
                            last = three(down_ps[:, cols], lambda i, c: ht[i][:, c, :],
                                         lambda i, c: wd[i][:, c, cols], HC)
                        last.then_inc(down_made, 1)
                    if project_it:
                        project(t, 1)
                    if up:
                        s = t.plus(-1)
                        pe.wait_ge(yt_lo_made, s.times(1, 1))
                        pe.wait_ge(score_made, s.times(1))
                        pe.wait_ge(ht_lo_made, s.times(1))
                        if down:
                            pe.wait_ge(route_step, Step((s.base - 1) * CHAIN, s.register, s.factor * CHAIN).times(1, 8))
                        for c in range(KC):
                            for i in range(2):
                                for w in range(2):
                                    last = pe.matmul(gate_ps, yt[i][:, c, :], wg[w][:, c, :],
                                                     start=(c == 0 and i == 0 and w == 0),
                                                     stop=(c == KC - 1 and i == 1 and w == 1))
                        last.then_inc(gate_done, 1)
                        pe.wait_ge(hidden_made, s.times(1))
                        three(up_ps[:], lambda i, c: yt[i][:, c, :], lambda i, c: wu[i][:, c, :], KC
                              ).then_inc(up_made, 1)

                steps(pe, first, step)


def expert_phase(nc, persistent, w_up, w_down, rows_dram, outs_dram, table_dram):
    ident, apart = persistent["ident"], persistent["apart"]
    with ExitStack() as ctx:
        def sb(name, shape, dt):
            return ctx.enter_context(nc.sbuf_tensor(name, shape, dt))

        def ps(name, shape, dt=F32):
            return ctx.enter_context(nc.psum_tensor(name, shape, dt))

        def sem(name):
            return ctx.enter_context(nc.semaphore("e_" + name))

        table = sb("table", [P, E * TPE], I32)
        index = sb("index", [P, 2, TPE], I32)
        rows = sb("rows", [P, 2 * TPE, D], F32)
        WU = KC * 2 * HR
        UP, DOWN = 0, 1
        part_cols = (slice(0, WU), slice(WU, WU + D))
        w_in = sb("ew_in", [P, 2, WU + D], F32)
        w_hi = sb("ew_hi", [P, 2, WU + D], F16)
        w_lo = sb("ew_lo", [P, 2, WU + D], F16)
        xt_hi = sb("ext_hi", [P, 2, KC, CAP], F16)
        xt_lo = sb("ext_lo", [P, 2, KC, CAP], F16)
        gsig = sb("egsig", [P, CAP], F32)
        gated = sb("egated", [P, CAP], F32)
        hidden = sb("ehidden", [P, CAP], F32)
        h_hi = sb("h_hi", [P, 2, CAP], F16)
        h_lo = sb("h_lo", [P, 2, CAP], F16)
        outs = sb("outs", [P, TPE, D], F32)

        turn_ps = ps("eturn_ps", [P, KC, P])
        g_ps = [ps(f"g_ps{i}", [P, CAP]) for i in range(2)]
        v_ps = [ps(f"v_ps{i}", [P, CAP]) for i in range(2)]
        down_ps = [ps(f"edown_ps{i}", [P, 512]) for i in range(2)]

        table_landed = sem("table_landed")
        index_made = sem("index_made")
        gathered = [sem(f"gathered{i}") for i in range(2)]
        w_landed = [[sem(f"w_landed{part}{i}") for i in range(2)] for part in (UP, DOWN)]
        w_hi_made = [sem(f"w_hi_made{part}") for part in (UP, DOWN)]
        w_lo_made = [sem(f"w_lo_made{part}") for part in (UP, DOWN)]
        turned = sem("turned")
        xt_hi_made = sem("xt_hi_made")
        xt_lo_made = sem("xt_lo_made")
        g_made = sem("g_made")
        v_made = sem("v_made")
        gsig_made = sem("gsig_made")
        gated_made = sem("gated_made")
        hidden_made = sem("hidden_made")
        h_hi_made = sem("h_hi_made")
        h_lo_made = sem("h_lo_made")
        down_made = sem("down_made")
        left_kept = sem("left_kept")
        right_kept = sem("right_kept")
        outs_stored = [sem(f"outs_stored{k}") for k in range(TPE)]

        def more(e, ahead):
            return not (isinstance(e.times(1), int) and e.base + ahead >= E)

        def steps(eng, first, step):
            first()
            for e in range(4):
                step(Step(e), True, e >= 1)
            with eng.Fori(0, (E - 6) // 2) as j:
                for r in range(2):
                    step(Step(4 + r, j, 2), True, True)
            step(Step(E - 2), True, True)
            step(Step(E - 1), True, True)
            step(Step(E), False, True)

        with nc.Block() as block:
            @block.sync
            def _(sp):
                def load_w(e):
                    par = e.base % 2
                    for part in (UP, DOWN):
                        sp.wait_ge(w_lo_made[part], e.times(1, -1))
                        sp.sem_inc(apart, 1)
                    sp.dma_start(w_in[:, par, 0:WU].rearrange("p (k n) -> p k n", k=KC),
                                 w_up[bass.ds(e.times(D), D), :].rearrange("(k p) n -> p k n", p=P)
                                 ).then_inc(w_landed[UP][par], 16)
                    sp.dma_start(w_in[:, par, WU:WU + D], w_down[bass.ds(e.times(HR), HR), :]
                                 ).then_inc(w_landed[DOWN][par], 16)

                def first():
                    sp.dma_start(table[:], table_dram.rearrange("(p c) o -> p (c o)", p=P)).then_inc(table_landed, 16)
                    load_w(Step(0))
                    load_w(Step(1))

                def step(e, up, down):
                    if more(e, 2):
                        load_w(e.plus(2))
                    if down:
                        s = e.plus(-1)
                        for k in range(TPE):
                            sp.wait_ge(left_kept, s.times(TPE, k + 1))
                            sp.sem_inc(apart, 1)
                            sp.wait_ge(right_kept, s.times(TPE, k + 1))
                            sp.sem_inc(apart, 1)
                            sp.dma_start(outs_dram[bass.ds(s.times(CAP, k * P), P), :], outs[:, k, :]
                                         ).then_inc(outs_stored[k], 16)

                steps(sp, first, step)
                for k in range(TPE):
                    sp.wait_ge(outs_stored[k], 16 * E)

            @block.gpsimd
            def _(pool):
                def gather(e):
                    par = e.base % 2
                    pool.wait_ge(gathered[par], e.half().times(16 * TPE))
                    pool.sem_inc(apart, 1)
                    pool.wait_ge(turned, e.times(TPE, -TPE))
                    pool.sem_inc(apart, 1)
                    pool.tensor_copy(index[:, par, :], table[:, bass.ds(e.times(TPE), TPE)]).then_inc(index_made, 1)
                    pool.wait_ge(index_made, e.times(1, 1))
                    pool.sem_inc(apart, 1)
                    for k in range(TPE):
                        pool.indirect_dma_start(
                            out=rows[:, par * TPE + k, :], out_offset=None, in_=rows_dram,
                            in_offset=bass.IndirectOffsetOnAxis(ap=index[:, par, k:k + 1], axis=0),
                            bounds_check=N - 1, oob_is_err=True).then_inc(gathered[par], 16)

                def first():
                    pool.wait_ge(table_landed, 16)
                    gather(Step(0))
                    gather(Step(1))

                def step(e, up, down):
                    if more(e, 2):
                        gather(e.plus(2))

                steps(pool, first, step)

            @block.scalar
            def _(act):
                def split_w(e, part):
                    w = (slice(None), e.base % 2, part_cols[part])
                    act.wait_ge(w_landed[part][e.base % 2], e.half().times(16, 16))
                    if part == UP:
                        act.wait_ge(v_made, e.times(1, -1))
                    else:
                        act.wait_ge(down_made, e.times(2 * TPE, -2 * TPE))
                    act.activation(w_hi[w], w_in[w], ACT.Copy, scale=SCALE).then_inc(w_hi_made[part], 1)

                def turn(e, k):
                    act.wait_ge(turned, e.times(TPE, k + 1))
                    if k == 0:
                        act.wait_ge(v_made, e.times(1, -1))
                    act.activation(xt_hi[:, e.base % 2, :, k * P:(k + 1) * P], turn_ps[:], ACT.Copy
                                   ).then_inc(xt_hi_made, 1)

                def first():
                    split_w(Step(0), UP)
                    for k in range(TPE):
                        turn(Step(0), k)

                def step(e, up, down):
                    par = e.base % 2
                    for k in range(TPE):
                        if up and more(e, 1):
                            turn(e.plus(1), k)
                        if up and k == 1:
                            act.wait_ge(g_made, e.times(1, 1))
                            act.wait_ge(gated_made, e.times(1))
                            act.activation(gsig[:], g_ps[par][:], ACT.Sigmoid, scale=1.0 / SCALE).then_inc(gsig_made, 1)
                        if up and k == 2:
                            split_w(e, DOWN)
                    if down:
                        s = e.plus(-1)
                        for k in range(TPE):
                            act.wait_ge(down_made, s.times(2 * TPE, 2 * k + 1))
                            act.wait_ge(outs_stored[k], s.times(16))
                            act.activation(outs[:, k, 0:512], down_ps[0][:], ACT.Copy, scale=1.0 / SCALE
                                           ).then_inc(left_kept, 1)
                            if k == 1 and more(e, 1):
                                split_w(e.plus(1), UP)
                    elif more(e, 1):
                        split_w(e.plus(1), UP)
                    if up:
                        act.wait_ge(hidden_made, e.times(1, 1))
                        act.wait_ge(down_made, e.times(2 * TPE, -2 * TPE))
                        act.activation(h_hi[:, par, :], hidden[:], ACT.Copy).then_inc(h_hi_made, 1)

                steps(act, first, step)

            @block.vector
            def _(dve):
                def split_w(e, part):
                    w = (slice(None), e.base % 2, part_cols[part])
                    dve.wait_ge(w_hi_made[part], e.times(1, 1))
                    dve.scalar_tensor_tensor(w_lo[w], w_in[w], SCALE, w_hi[w], ALU.mult, ALU.subtract
                                             ).then_inc(w_lo_made[part], 1)

                def turn(e, k):
                    dve.wait_ge(xt_hi_made, e.times(TPE, k + 1))
                    cols = slice(k * P, (k + 1) * P)
                    dve.tensor_tensor(xt_lo[:, e.base % 2, :, cols], turn_ps[:], xt_hi[:, e.base % 2, :, cols],
                                      ALU.subtract).then_inc(xt_lo_made, 1)

                def first():
                    split_w(Step(0), UP)
                    for k in range(TPE):
                        turn(Step(0), k)

                def step(e, up, down):
                    par = e.base % 2
                    for k in range(TPE):
                        if up and more(e, 1):
                            turn(e.plus(1), k)
                        if up and k == 2:
                            dve.wait_ge(gsig_made, e.times(1, 1))
                            dve.scalar_tensor_tensor(gated[:], g_ps[par][:], 1.0 / SCALE ** 2, gsig[:],
                                                     ALU.mult, ALU.mult).then_inc(gated_made, 1)
                            split_w(e, DOWN)
                    if up:
                        dve.wait_ge(v_made, e.times(1, 1))
                        dve.wait_ge(gated_made, e.times(1, 1))
                        dve.wait_ge(h_lo_made, e.times(1))
                        dve.tensor_tensor(hidden[:], gated[:], v_ps[par][:], ALU.mult).then_inc(hidden_made, 1)
                    if down:
                        s = e.plus(-1)
                        for k in range(TPE):
                            dve.wait_ge(down_made, s.times(2 * TPE, 2 * k + 2))
                            dve.wait_ge(outs_stored[k], s.times(16))
                            dve.tensor_scalar(outs[:, k, 512:D], down_ps[1][:], 1.0 / SCALE, None, ALU.mult
                                              ).then_inc(right_kept, 1)
                            if k == 1 and more(e, 1):
                                split_w(e.plus(1), UP)
                    elif more(e, 1):
                        split_w(e.plus(1), UP)
                    if up:
                        dve.wait_ge(h_hi_made, e.times(1, 1))
                        dve.tensor_tensor(h_lo[:, par, :], hidden[:], h_hi[:, par, :], ALU.subtract
                                          ).then_inc(h_lo_made, 1)

                steps(dve, first, step)

            @block.tensor
            def _(pe):
                def turn(e, k):
                    par = e.base % 2
                    if k == 0:
                        pe.wait_ge(gathered[par], e.half().times(16 * TPE, 16 * TPE))
                    pe.wait_ge(xt_lo_made, e.times(TPE, k))
                    for c in range(KC):
                        last = pe.transpose(turn_ps[:, c, :], rows[:, par * TPE + k, c * P:(c + 1) * P], ident[:])
                    last.then_inc(turned, 1)

                def up_half(e, part, half):
                    par = e.base % 2
                    out = (g_ps, v_ps)[part][par][:]
                    for c in range(half * KC // 2, (half + 1) * KC // 2):
                        at = c * 2 * HR + part * HR
                        wh, wl = (w[:, par, at:at + HR] for w in (w_hi, w_lo))
                        pe.matmul(out, wh, xt_hi[:, par, c, :], start=(c == 0), stop=False)
                        pe.matmul(out, wh, xt_lo[:, par, c, :], start=False, stop=False)
                        last = pe.matmul(out, wl, xt_hi[:, par, c, :], start=False, stop=(c == KC - 1))
                    if half == 1:
                        last.then_inc((g_made, v_made)[part], 1)

                def down_tile(s, k):
                    par = s.base % 2
                    for half, kept in ((0, left_kept), (1, right_kept)):
                        pe.wait_ge(kept, s.times(TPE, k))
                        cols = slice(WU + half * 512, WU + (half + 1) * 512)
                        hh, hl = (h[:, par, k * P:(k + 1) * P] for h in (h_hi, h_lo))
                        pe.matmul(down_ps[half][:], hh, w_hi[:, par, cols], start=True, stop=False)
                        pe.matmul(down_ps[half][:], hh, w_lo[:, par, cols], start=False, stop=False)
                        pe.matmul(down_ps[half][:], hl, w_hi[:, par, cols], start=False, stop=True
                                  ).then_inc(down_made, 1)

                def first():
                    for k in range(TPE):
                        turn(Step(0), k)

                def step(e, up, down):
                    if up:
                        pe.wait_ge(w_lo_made[UP], e.times(1, 1))
                        pe.wait_ge(xt_lo_made, e.times(TPE, TPE))
                        pe.wait_ge(hidden_made, e.times(1, -1))
                        for part in range(2):
                            for half in range(2):
                                up_half(e, part, half)
                                if more(e, 1):
                                    turn(e.plus(1), 2 * part + half)
                    if down:
                        s = e.plus(-1)
                        pe.wait_ge(h_lo_made, s.times(1, 1))
                        pe.wait_ge(w_lo_made[DOWN], s.times(1, 1))
                        for k in range(TPE):
                            down_tile(s, k)

                steps(pe, first, step)


def combining_phase(nc, persistent, base_dram, outs_dram, out):
    places, weights = persistent["places"], persistent["weights"]
    apart = persistent["apart"]
    with ExitStack() as ctx:
        def sb(name, shape, dt):
            return ctx.enter_context(nc.sbuf_tensor(name, shape, dt))

        def sem(name):
            return ctx.enter_context(nc.semaphore("c_" + name))

        R = 2
        index = sb("cindex", [P, R, TOPK], I32)
        weight = sb("weight", [P, R, TOPK], F32)
        rows = sb("crows", [P, R, TOPK, D], F32)
        sums = sb("csums", [P, R, 2, D], F32)
        index_made = sem("index_made")
        weight_made = sem("weight_made")
        gathered = [sem(f"gathered{i}") for i in range(R)]
        base_landed = [sem(f"base_landed{i}") for i in range(R)]
        added = sem("added")
        out_stored = [sem(f"out_stored{i}") for i in range(R)]

        def steps(eng, step):
            for t in range(R):
                step(Step(t))
            with eng.Fori(0, (NT - R) // R) as j:
                for r in range(R):
                    step(Step(R + r, j, R))

        with nc.Block() as block:
            @block.gpsimd
            def _(pool):
                def step(t):
                    par = t.base % R
                    pool.wait_ge(added, t.times(TOPK, (1 - R) * TOPK))
                    pool.sem_inc(apart, 1)
                    pool.tensor_copy(index[:, par, :], places[:, bass.ds(t.times(TOPK), TOPK)]).then_inc(index_made, 1)
                    pool.wait_ge(index_made, t.times(1, 1))
                    pool.sem_inc(apart, 1)
                    for k in range(TOPK):
                        pool.indirect_dma_start(
                            out=rows[:, par, k, :], out_offset=None, in_=outs_dram,
                            in_offset=bass.IndirectOffsetOnAxis(ap=index[:, par, k:k + 1], axis=0),
                            bounds_check=E * CAP - 1, oob_is_err=True).then_inc(gathered[par], 16)
                steps(pool, step)

            @block.sync
            def _(sp):
                def step(t):
                    par = t.base % R
                    sp.wait_ge(out_stored[par], t.half().times(16))
                    sp.sem_inc(apart, 1)
                    sp.dma_start(sums[:, par, 0, :], base_dram[bass.ds(t.times(P), P), :]).then_inc(base_landed[par], 16)
                steps(sp, step)

            @block.scalar
            def _(act):
                def step(t):
                    par = t.base % R
                    act.wait_ge(added, t.times(TOPK, TOPK))
                    act.dma_start(out[bass.ds(t.times(P), P), :], sums[:, par, 0, :]).then_inc(out_stored[par], 16)
                steps(act, step)
                for r in range(R):
                    act.wait_ge(out_stored[r], 16 * NT // R)

            @block.vector
            def _(dve):
                def step(t):
                    par = t.base % R
                    dve.wait_ge(added, t.times(TOPK, (1 - R) * TOPK))
                    dve.tensor_copy(weight[:, par, :], weights[:, bass.ds(t.times(TOPK), TOPK)]).then_inc(weight_made, 1)
                    dve.wait_ge(weight_made, t.times(1, 1))
                    dve.wait_ge(base_landed[par], t.half().times(16, 16))
                    dve.wait_ge(gathered[par], t.half().times(16 * TOPK, 16 * TOPK))
                    for k in range(TOPK):
                        dve.wait_ge(added, t.times(TOPK, k))
                        dve.scalar_tensor_tensor(sums[:, par, (k + 1) % 2, :], rows[:, par, k, :],
                                                 weight[:, par, k:k + 1], sums[:, par, k % 2, :], ALU.mult, ALU.add
                                                 ).then_inc(added, 1)
                steps(dve, step)


def gated_cross_attention_and_moe(nc, x, ctx_t, w_qkv, b_qkv, w_o, b_o, gains, w_gate, w_shared_up,
                                  w_shared_down, w_up, w_down, out):
    attn_dram = nc.dram_tensor("attn_dram", [NBLK * P, KC * BLK], F32, kind="Internal").ap()
    rows_dram = nc.dram_tensor("rows_dram", [N, D], F32, kind="Internal").ap()
    base_dram = nc.dram_tensor("base_dram", [N, D], F32, kind="Internal").ap()
    outs_dram = nc.dram_tensor("outs_dram", [E * CAP, D], F32, kind="Internal").ap()
    table_dram = nc.dram_tensor("table_dram", [E * CAP, 1], I32, kind="Internal").ap()
    with ExitStack() as ctx:
        def sb(name, shape, dt):
            return ctx.enter_context(nc.sbuf_tensor(name, shape, dt))

        persistent = {
            "ident": sb("ident", [P, P], F32),
            "gates": sb("gates", [P, 4], F32),
            "places": sb("places", [P, NT * TOPK], I32),
            "weights": sb("weights", [P, NT * TOPK], F32),
        }
        ident, gates = persistent["ident"], persistent["gates"]
        persistent["apart"] = apart = ctx.enter_context(nc.semaphore("apart"))
        cleared = ctx.enter_context(nc.semaphore("cleared"))
        gains_landed = ctx.enter_context(nc.semaphore("gains_landed"))
        tanh_made = ctx.enter_context(nc.semaphore("tanh_made"))
        with nc.Block() as block:
            @block.sync
            def _(sp):
                sp.dma_start(gates[:, 2:4], gains.to_broadcast([P, 2])).then_inc(gains_landed, 16)

            @block.scalar
            def _(act):
                act.wait_ge(gains_landed, 16)
                act.activation(gates[:, 0:2], gates[:, 2:4], ACT.Tanh).then_inc(tanh_made, 1)
                act.wait_ge(tanh_made, 1)
                act.activation(gates[:, 2:4], gates[:, 0:2], ACT.Copy, scale=1.0 / SCALE).then_inc(tanh_made, 1)

            @block.gpsimd
            def _(pool):
                pool.memset(ident[:], 0.0).then_inc(cleared, 1)
                pool.wait_ge(cleared, 1)
                pool.affine_select(out=ident[:], in_=ident[:], compare_op=ALU.not_equal, fill=1.0, base=0,
                                   pattern=[[-1, P]], channel_multiplier=1)
        attention_phase(nc, persistent, x, ctx_t, w_qkv, b_qkv, attn_dram)
        routing_phase(nc, persistent, x, w_o, b_o, gains, w_gate, w_shared_up, w_shared_down, attn_dram,
                      rows_dram, base_dram, table_dram)
        expert_phase(nc, persistent, w_up, w_down, rows_dram, outs_dram, table_dram)
        combining_phase(nc, persistent, base_dram, outs_dram, out)


def kernel(**inputs):
    import numpy as np
    import concourse.bacc as bacc
    from concourse.bass_utils import run_bass_kernel_spmd

    a = {name: np.asarray(value) for name, value in inputs.items()}
    w = "L0_xattn_"
    f = "L0_ffn_"
    arrays = {
        "x": a["x"].reshape(N, D),
        "ctx_t": a["ctx_2048"].reshape(N, D).T,
        "w_qkv": np.concatenate([a[w + "Wq"].T, a[w + "Wk"].T, a[w + "Wv"].T], axis=0),
        "b_qkv": np.concatenate([a[w + "bq"], a[w + "bk"], a[w + "bv"]]).reshape(3 * KC, P).T,
        "w_o": a[w + "Wo"].T,
        "b_o": a[w + "bo"].reshape(1, D),
        "gains": np.concatenate([a["g_xattn"], a["g_ffn"]]).reshape(1, 2),
        "w_gate": a[f + "w_gate"],
        "w_shared_up": a[f + "w_shared_up"],
        "w_shared_down": a[f + "w_shared_down"],
        "w_up": a[f + "w_up"].reshape(E * D, 2 * HR),
        "w_down": a[f + "w_down"].reshape(E * HR, D),
    }
    arrays = {name: np.ascontiguousarray(v) for name, v in arrays.items()}
    nc = bacc.Bacc("TRN2", target_bir_lowering=False, num_devices=1)
    args = [nc.dram_tensor(n, v.shape, mybir.dt.from_np(v.dtype), kind="ExternalInput").ap()
            for n, v in arrays.items()]
    out = nc.dram_tensor("out", (N, D), F32, kind="ExternalOutput").ap()
    gated_cross_attention_and_moe(nc, *args, out)
    r = run_bass_kernel_spmd(nc, [arrays], core_ids=[0])
    return r.results[0]["out"].reshape(4, N // 4, D)
```

```python
from contextlib import ExitStack

import concourse.bass as bass
from concourse import mybir

F32 = mybir.dt.float32
F16 = mybir.dt.float16
BF16 = mybir.dt.bfloat16
I32 = mybir.dt.int32
U32 = mybir.dt.uint32
ALU = mybir.AluOpType
ACT = mybir.ActivationFunctionType
AX_X = mybir.AxisListType.X

P = 128
N = 4096
D = 1024
H = 16
HD = D // H
KC = D // P
EPS = 1e-5
SCALE = 64.0
NEG = -1e30

BLK = 256
NBLK = N // BLK
TOK = P // H
QUAD = 4
PEELED = 3
NQ = BLK // (TOK * QUAD)
NT = N // P

E = 64
TOPK = 6
CAP = 512
TPE = CAP // P
HR = 128
HS = 256




class Step:

    def __init__(self, base, register=None, factor=0):
        self.base, self.register, self.factor = base, register, factor

    def plus(self, n):
        return Step(self.base + n, self.register, self.factor)

    def half(self):
        return Step(self.base // 2, self.register, self.factor // 2)

    def times(self, per, extra=0):
        n = self.base * per + extra
        return max(n, 0) if self.register is None else self.register * (self.factor * per) + n


CHUNKS = 3 * KC
SLOT = [0, 2, 5, 8, 10, 13, 16, 18]
TURN = [12, 18]
STATS = [3, 4]


def work_after(n):
    found = []
    for q, s in enumerate(SLOT):
        for stage, lag in (("weighted", 4), ("turned", 3), ("values", 1), ("scores", 0)):
            if s + lag == n:
                found.append((stage, q))
    return sorted(found, key=lambda f: f[1])


def attention_phase(nc, persistent, x, ctx_t, w_qkv, b_qkv, attn_dram):
    ident, apart = persistent["ident"], persistent["apart"]
    with ExitStack() as ctx:
        def sb(name, shape, dt):
            return ctx.enter_context(nc.sbuf_tensor(name, shape, dt))

        def ps(name, shape, dt=F32):
            return ctx.enter_context(nc.psum_tensor(name, shape, dt))

        def sem(name):
            return ctx.enter_context(nc.semaphore(name))

        w_hi = sb("w_hi", [P, 3, KC, D], F16)
        w_lo = sb("w_lo", [P, 3, KC, D], F16)
        bias = sb("bias", [P, 3 * KC], F32)
        x_in = sb("x_in", [P, 2, D], F32)
        c_in = sb("c_in", [P, KC, BLK], F32)
        xt_hi = sb("xt_hi", [P, KC, BLK], F16)
        xt_lo = sb("xt_lo", [P, KC, BLK], F16)
        ct_hi = sb("ct_hi", [P, KC, BLK], F16)
        ct_lo = sb("ct_lo", [P, KC, BLK], F16)
        qkv = sb("qkv", [P, 2, 3, P, H], F32)
        probs = sb("probs", [P, 2, QUAD, P], F32)
        probs_t = sb("probs_t", [P, 2, QUAD, P], F32)
        values = sb("values", [P, 2, QUAD, HD], F32)
        attn = sb("attn", [P, 2, 2, KC, P], F32)
        stats = sb("stats", [P, 2, 2, 6], F32)
        moments = sb("moments", [P, 2, 2], F32)
        veps = sb("veps", [P, 2], F32)
        rstd = sb("rstd", [P, 2], F32)
        power = sb("power", [P, 1], F32)
        neg_max = sb("neg_max", [P, 2, QUAD], F32)
        sums = sb("sums", [P, 2, QUAD], F32)
        rsums = sb("rsums", [P, 2, QUAD], F32)
        own = sb("own", [TOK, P], BF16)
        others = sb("others", [TOK, QUAD * P], BF16)

        turn_ps = ps("turn_ps", [P, KC, P])
        proj_ps = [ps(f"proj_ps{i}", [P, 512]) for i in range(2)]
        score_ps = [ps(f"score_ps{i}", [P, QUAD, P]) for i in range(2)]
        probs_ps = ps("probs_ps", [P, QUAD, P])
        attn_ps = ps("attn_ps", [HD, QUAD, P])
        values_ps = turn_ps[:, 0:2, :].rearrange("p k (c d) -> p (k c) d", d=HD)

        w_landed = [sem(f"w_landed{i}") for i in range(4)]
        w_hi_made = sem("w_hi_made")
        w_lo_made = sem("w_lo_made")
        bias_landed = sem("bias_landed")
        consts_made = sem("consts_made")
        x_landed = sem("x_landed")
        c_landed = sem("c_landed")
        stats_made = sem("stats_made")
        moments_made = sem("moments_made")
        veps_made = sem("veps_made")
        rstd_made = sem("rstd_made")
        x_normed = sem("x_normed")
        x_turned = sem("x_turned")
        xt_hi_made = sem("xt_hi_made")
        xt_lo_made = sem("xt_lo_made")
        ct_hi_made = sem("ct_hi_made")
        ct_made = sem("ct_made")
        projected = sem("projected")
        even_kept = sem("even_kept")
        odd_kept = sem("odd_kept")
        scored = sem("scored")
        max_made = sem("max_made")
        exp_made = sem("exp_made")
        rsum_made = sem("rsum_made")
        probs_made = sem("probs_made")
        probs_turned = sem("probs_turned")
        probs_kept = sem("probs_kept")
        values_turned = sem("values_turned")
        values_kept = sem("values_kept")
        attn_made = sem("attn_made")
        attn_kept = sem("attn_kept")
        attn_stored = [sem(f"attn_stored{i}") for i in range(2)]

        stage_w = attn[:, :, :, :, :].rearrange("p a b k t -> p (a b) (k t)")

        def steps(eng, first, step):
            first()
            step(Step(0), True, False, True)
            for b in range(1, PEELED):
                step(Step(b), True, True, True)
            with eng.Fori(0, (NBLK - 1 - PEELED) // 2) as j:
                for r in range(2):
                    step(Step(PEELED + r, j, 2), True, True, True)
            step(Step(NBLK - 1), True, True, False)
            step(Step(NBLK), False, True, False)

        with nc.Block() as block:
            @block.sync
            def _(sp):
                sp.dma_start(bias[:], b_qkv).then_inc(bias_landed, 16)

                def load_x(b):
                    sp.wait_ge(x_turned, b.times(2))
                    sp.sem_inc(apart, 1)
                    sp.dma_start(x_in[:], x[bass.ds(b.times(BLK), BLK), :].rearrange("(a p) d -> p a d", p=P)
                                 ).then_inc(x_landed, 16)

                def load_ctx(b):
                    sp.wait_ge(ct_made, b.times(1))
                    sp.sem_inc(apart, 1)
                    sp.dma_start(c_in[:], ctx_t[:, bass.ds(b.times(BLK), BLK)].rearrange("(k p) t -> p k t", p=P)
                                 ).then_inc(c_landed, 16)

                def store(b):
                    sp.wait_ge(attn_kept, b.times(NQ, NQ))
                    sp.sem_inc(apart, 1)
                    par = b.base % 2
                    sp.dma_start(attn_dram[bass.ds(b.times(P), P), :],
                                 attn[:, par].rearrange("p a k t -> p (a k t)")).then_inc(attn_stored[par], 16)

                def first():
                    load_x(Step(0))
                    load_ctx(Step(0))
                    for m in range(CHUNKS):
                        sp.wait_ge(w_lo_made, max(m - 3, 0))
                        sp.sem_inc(apart, 1)
                        sp.dma_start(stage_w[:, m % 4, :], w_qkv[m * P:(m + 1) * P, :]).then_inc(w_landed[m % 4], 16)

                def step(b, proj, attend, more):
                    if more:
                        load_x(b.plus(1))
                        load_ctx(b.plus(1))
                    if attend:
                        store(b.plus(-1))

                steps(sp, first, step)
                for par in range(2):
                    sp.wait_ge(attn_stored[par], 16 * NBLK // 2)

            @block.gpsimd
            def _(pool):
                pool.memset(power[:], -0.5).then_inc(consts_made, 1)
                pool.memset(own[:], 0.0).then_inc(consts_made, 1)
                pool.memset(others[:], NEG).then_inc(consts_made, 1)
                pool.wait_ge(consts_made, 3)
                pool.affine_select(out=own[:].rearrange("k (t h) -> k t h", h=H),
                                   in_=own[:].rearrange("k (t h) -> k t h", h=H),
                                   compare_op=ALU.not_equal, fill=1.0, base=0,
                                   pattern=[[-1, TOK], [0, H]], channel_multiplier=1).then_inc(consts_made, 1)
                pool.affine_select(out=others[:].rearrange("k (g t h) -> k g t h", g=QUAD, h=H),
                                   in_=others[:].rearrange("k (g t h) -> k g t h", g=QUAD, h=H),
                                   compare_op=ALU.not_equal, fill=0.0, base=0,
                                   pattern=[[0, QUAD], [-1, TOK], [0, H]],
                                   channel_multiplier=1).then_inc(consts_made, 1)

                def deviation(b, t):
                    pool.wait_ge(moments_made, b.times(2, t + 1))
                    pool.sem_inc(apart, 1)
                    pool.tensor_scalar(veps[:, t:t + 1], moments[:, t, 1:2], EPS, None, ALU.add).then_inc(veps_made, 1)
                    pool.wait_ge(veps_made, b.times(2, t + 1))
                    pool.sem_inc(apart, 1)
                    pool.wait_ge(x_normed, b.times(2, t - 1))
                    pool.tensor_tensor(rstd[:, t:t + 1], veps[:, t:t + 1], power[:], ALU.pow).then_inc(rstd_made, 1)

                def split_ctx(b):
                    pool.wait_ge(ct_hi_made, b.times(1, 1))
                    pool.tensor_tensor(ct_lo[:], c_in[:], ct_hi[:], ALU.subtract).then_inc(ct_made, 1)

                def divide(a, q):
                    pool.wait_ge(rsum_made, a.times(NQ, q + 1))
                    pool.sem_inc(apart, 1)
                    pool.tensor_tensor(probs[:, q % 2], probs[:, q % 2],
                                       rsums[:, q % 2, :].unsqueeze(2).broadcast_to([P, QUAD, P]),
                                       ALU.mult).then_inc(probs_made, 1)

                def first():
                    for t in range(2):
                        deviation(Step(0), t)

                def step(b, proj, attend, more):
                    if proj:
                        split_ctx(b)
                    for n in range(CHUNKS):
                        if more and n in STATS:
                            deviation(b.plus(1), STATS.index(n))
                        if attend:
                            for stage, q in work_after(n - 1):
                                if stage == "scores":
                                    divide(b.plus(-1), q)

                steps(pool, first, step)

            @block.scalar
            def _(act):
                def split_ctx(b):
                    act.wait_ge(c_landed, b.times(16, 16))
                    act.wait_ge(projected, b.times(CHUNKS))
                    act.activation(ct_hi[:], c_in[:], ACT.Copy).then_inc(ct_hi_made, 1)

                def turn(b, t):
                    act.wait_ge(x_turned, b.times(2, t + 1))
                    act.wait_ge(projected, b.times(CHUNKS, KC - CHUNKS))
                    act.activation(xt_hi[:, :, t * P:(t + 1) * P], turn_ps[:], ACT.Copy).then_inc(xt_hi_made, 1)

                def keep(b, n):
                    par, part, head = b.base % 2, n // KC, 2 * (n % KC)
                    act.wait_ge(projected, b.times(CHUNKS, n + 1))
                    if n == 0:
                        act.wait_ge(attn_made, b.times(NQ, -NQ))
                    for half in range(2):
                        last = act.activation(qkv[half * HD:(half + 1) * HD, par, part, :, head],
                                              proj_ps[n % 2][0:HD, half * P:(half + 1) * P], ACT.Identity,
                                              bias=bias[0:HD, n:n + 1], scale=1.0 / SCALE)
                    last.then_inc(even_kept, 1)

                def exps(a, q):
                    act.wait_ge(max_made, a.times(NQ, q + 1))
                    act.wait_ge(probs_turned, a.times(NQ, q - 1))
                    act.wait_ge(rsum_made, a.times(NQ, q - 1))
                    for g in range(QUAD):
                        last = act.activation(probs[:, q % 2, g, :], score_ps[q % 2][:, g, :], ACT.Exp,
                                              bias=neg_max[:, q % 2, g:g + 1],
                                              accum_out=sums[:, q % 2, g:g + 1])
                    last.then_inc(exp_made, 1)

                def keep_probs(a, q):
                    act.wait_ge(probs_turned, a.times(NQ, q + 1))
                    act.wait_ge(attn_made, a.times(NQ, q - 1))
                    act.activation(probs_t[:, q % 2], probs_ps[:], ACT.Copy).then_inc(probs_kept, 1)

                def first():
                    for m in range(CHUNKS):
                        act.wait_ge(w_landed[m % 4], 16 * (m // 4 + 1))
                        act.activation(w_hi[:, m // KC, m % KC, :], stage_w[:, m % 4, :], ACT.Copy, scale=SCALE
                                       ).then_inc(w_hi_made, 1)
                    for t in range(2):
                        turn(Step(0), t)
                    act.wait_ge(bias_landed, 16)

                def step(b, proj, attend, more):
                    if proj:
                        split_ctx(b)
                    for n in range(CHUNKS):
                        if proj:
                            keep(b, n)
                        if attend:
                            for stage, q in work_after(n):
                                if stage == "scores":
                                    exps(b.plus(-1), q)
                                if stage == "turned":
                                    keep_probs(b.plus(-1), q)
                        if more and n in TURN:
                            turn(b.plus(1), TURN.index(n))

                steps(act, first, step)

            @block.vector
            def _(dve):
                def moment(b, t):
                    dve.wait_ge(x_landed, b.times(16, 16))
                    for half in range(2):
                        last = dve.bn_stats(stats[:, t, half, :], x_in[:, t, half * 512:(half + 1) * 512])
                    last.then_inc(stats_made, 1)
                    dve.wait_ge(stats_made, b.times(2, t + 1))
                    dve.wait_ge(x_normed, b.times(2, t - 1))
                    dve.sem_inc(apart, 1)
                    dve.bn_aggr(moments[:, t, :], stats[:, t]).then_inc(moments_made, 1)

                def norm(b, t):
                    dve.wait_ge(rstd_made, b.times(2, t + 1))
                    dve.tensor_scalar(x_in[:, t, :], x_in[:, t, :], moments[:, t, 0:1], rstd[:, t:t + 1],
                                      ALU.subtract, ALU.mult).then_inc(x_normed, 1)

                def turn(b, t):
                    dve.wait_ge(xt_hi_made, b.times(2, t + 1))
                    dve.tensor_tensor(xt_lo[:, :, t * P:(t + 1) * P], turn_ps[:], xt_hi[:, :, t * P:(t + 1) * P],
                                      ALU.subtract).then_inc(xt_lo_made, 1)

                def keep(b, n):
                    par, part, head = b.base % 2, n // KC, 2 * (n % KC) + 1
                    dve.wait_ge(projected, b.times(CHUNKS, n + 1))
                    if n == 0:
                        dve.wait_ge(attn_made, b.times(NQ, -NQ))
                    for half in range(2):
                        last = dve.tensor_scalar(qkv[half * HD:(half + 1) * HD, par, part, :, head],
                                                 proj_ps[n % 2][HD:P, half * P:(half + 1) * P],
                                                 1.0 / SCALE, bias[HD:P, n:n + 1], ALU.mult, ALU.add)
                    last.then_inc(odd_kept, 1)

                def maxima(a, q):
                    dve.wait_ge(scored, a.times(NQ, q + 1))
                    dve.wait_ge(exp_made, a.times(NQ, q - 1))
                    dve.tensor_reduce(neg_max[:, q % 2, :], score_ps[q % 2][:], AX_X, ALU.max, negate=True
                                      ).then_inc(max_made, 1)

                def inverses(a, q):
                    dve.wait_ge(exp_made, a.times(NQ, q + 1))
                    dve.wait_ge(probs_made, a.times(NQ, q - 1))
                    dve.reciprocal(rsums[:, q % 2, :], sums[:, q % 2, :]).then_inc(rsum_made, 1)

                def keep_values(a, q):
                    dve.wait_ge(values_turned, a.times(NQ, q + 1))
                    dve.wait_ge(attn_made, a.times(NQ, q - 1))
                    dve.tensor_copy(values[:, q % 2], values_ps).then_inc(values_kept, 1)

                def keep_attn(a, q):
                    par, half, t0 = a.base % 2, q % 2, (q // 2) * TOK * QUAD
                    dve.wait_ge(attn_made, a.times(NQ, q + 1))
                    if q == 0:
                        dve.wait_ge(attn_stored[par], a.half().times(16))
                    got = attn_ps[:].rearrange("d g (t o r) -> d r o (g t)", o=KC, r=2)
                    for r in range(2):
                        last = dve.tensor_copy(attn[r * HD:(r + 1) * HD, par, half, :, t0:t0 + TOK * QUAD],
                                               got[:, r])
                    last.then_inc(attn_kept, 1)

                def first():
                    for t in range(2):
                        moment(Step(0), t)
                    for t in range(2):
                        norm(Step(0), t)
                    for m in range(CHUNKS):
                        dve.wait_ge(w_hi_made, m + 1)
                        dve.scalar_tensor_tensor(w_lo[:, m // KC, m % KC, :], stage_w[:, m % 4, :], SCALE,
                                                 w_hi[:, m // KC, m % KC, :], ALU.mult, ALU.subtract
                                                 ).then_inc(w_lo_made, 1)
                    for t in range(2):
                        turn(Step(0), t)
                    dve.wait_ge(bias_landed, 16)

                def step(b, proj, attend, more):
                    for n in range(CHUNKS):
                        if proj:
                            keep(b, n)
                        if attend:
                            for stage, q in work_after(n - 1):
                                if stage == "scores":
                                    inverses(b.plus(-1), q)
                            for stage, q in work_after(n):
                                if stage == "scores":
                                    maxima(b.plus(-1), q)
                                if stage == "values":
                                    keep_values(b.plus(-1), q)
                                if stage == "weighted":
                                    keep_attn(b.plus(-1), q)
                        if more and n in STATS:
                            moment(b.plus(1), STATS.index(n))
                        if more and n - 2 in STATS:
                            norm(b.plus(1), STATS.index(n - 2))
                        if more and n in TURN:
                            turn(b.plus(1), TURN.index(n))

                steps(dve, first, step)

            @block.tensor
            def _(pe):
                def turn(b, t):
                    pe.wait_ge(x_normed, b.times(2, t + 1))
                    pe.wait_ge(xt_lo_made, b.times(2, t))
                    if b.base >= 2:
                        ahead = sum(s + 1 <= TURN[t] for s in SLOT)
                        pe.wait_ge(values_kept, b.plus(-2).times(NQ, ahead))
                    for k in range(KC):
                        last = pe.transpose(turn_ps[:, k, :], x_in[:, t, k * P:(k + 1) * P], ident[:])
                    last.then_inc(x_turned, 1)

                def project(b, n):
                    part, o = n // KC, n % KC
                    if n == 0:
                        pe.wait_ge(xt_lo_made, b.times(2, 2))
                    if n == KC:
                        pe.wait_ge(ct_made, b.times(1, 1))
                    pe.wait_ge(even_kept, b.times(CHUNKS, n - 1))
                    pe.wait_ge(odd_kept, b.times(CHUNKS, n - 1))
                    hi, lo = (xt_hi, xt_lo) if part == 0 else (ct_hi, ct_lo)
                    out = proj_ps[n % 2][:, 0:BLK]
                    for k in range(KC):
                        wh, wl = (w[:, part, k, o * P:(o + 1) * P] for w in (w_hi, w_lo))
                        pe.matmul(out, wh, hi[:, k, :], start=(k == 0), stop=False)
                        pe.matmul(out, wh, lo[:, k, :], start=False, stop=False)
                        last = pe.matmul(out, wl, hi[:, k, :], start=False, stop=(k == KC - 1))
                    last.then_inc(projected, 1)

                def rows(q):
                    half = q % 2
                    return slice(half * HD, (half + 1) * HD)

                def group(a, part, q, g):
                    t0 = ((q // 2) * QUAD + g) * TOK
                    return qkv[rows(q), a.base % 2, part, t0:t0 + TOK, :].rearrange("d t h -> d (t h)")

                def scores(a, q):
                    if q == 0:
                        pe.wait_ge(even_kept, a.times(CHUNKS, CHUNKS))
                        pe.wait_ge(odd_kept, a.times(CHUNKS, CHUNKS))
                    pe.wait_ge(exp_made, a.times(NQ, q - 1))
                    out = score_ps[q % 2]
                    pe.matmul(out[:].rearrange("p g c -> p (g c)"), own[:], others[:], start=True, stop=False,
                              skip_group_check=True)
                    for g in range(QUAD):
                        last = pe.matmul(out[:, g, :], group(a, 0, q, g), group(a, 1, q, g), start=False, stop=True,
                                         skip_group_check=True)
                    last.then_inc(scored, 1)

                def turn_values(a, q):
                    pe.wait_ge(values_kept, a.times(NQ, q))
                    ahead = a.plus(2).times(2, sum(SLOT[q] + 1 > n for n in TURN))
                    pe.wait_ge(xt_lo_made, min(ahead, 2 * NBLK) if isinstance(ahead, int) else ahead)
                    pe.sem_inc(apart, 1)
                    for g in range(QUAD):
                        last = pe.transpose(values_ps[:, g, :], group(a, 2, q, g), ident[rows(q), rows(q)])
                    last.then_inc(values_turned, 1)

                def turn_probs(a, q):
                    pe.wait_ge(probs_made, a.times(NQ, q + 1))
                    pe.wait_ge(probs_kept, a.times(NQ, q))
                    for g in range(QUAD):
                        last = pe.transpose(probs_ps[:, g, :], probs[:, q % 2, g, :], ident[:])
                    last.then_inc(probs_turned, 1)

                def weigh(a, q):
                    pe.wait_ge(probs_kept, a.times(NQ, q + 1))
                    pe.wait_ge(values_kept, a.times(NQ, q + 1))
                    pe.wait_ge(attn_kept, a.times(NQ, q))
                    for g in range(QUAD):
                        last = pe.matmul(attn_ps[:, g, :], values[:, q % 2, g, :], probs_t[:, q % 2, g, :],
                                         start=True, stop=True)
                    last.then_inc(attn_made, 1)

                def first():
                    pe.wait_ge(consts_made, 5)
                    for t in range(2):
                        turn(Step(0), t)
                    pe.wait_ge(w_lo_made, CHUNKS)

                def step(b, proj, attend, more):
                    for n in range(CHUNKS):
                        if proj:
                            project(b, n)
                        if attend:
                            for stage, q in work_after(n):
                                {"scores": scores, "values": turn_values, "turned": turn_probs,
                                 "weighted": weigh}[stage](b.plus(-1), q)
                        if more and n in TURN:
                            turn(b.plus(1), TURN.index(n))

                steps(pe, first, step)


def routing_phase(nc, persistent, x, w_o, b_o, gains, w_gate, attn_dram, rows_dram, y_dram,
                  table_dram):
    ident, gates, apart = persistent["ident"], persistent["gates"], persistent["apart"]
    places, weights = persistent["places"], persistent["weights"]
    with ExitStack() as ctx:
        def sb(name, shape, dt):
            return ctx.enter_context(nc.sbuf_tensor(name, shape, dt))

        def ps(name, shape, dt=F32):
            return ctx.enter_context(nc.psum_tensor(name, shape, dt))

        def sem(name):
            return ctx.enter_context(nc.semaphore("r_" + name))

        def pair(name, shape):
            return sb(name + "_hi", shape, F16), sb(name + "_lo", shape, F16)

        wo = pair("wo", [P, KC, D])
        wg = pair("wg", [P, KC, E])
        stage_w = sb("stage_w", [P, 4, D], F32)
        bo_row = sb("bo_row", [P, D], F32)
        x_in = sb("rx_in", [P, 2, D], F32)
        a_in = sb("a_in", [P, 2, KC, P], F32)
        at = pair("at", [P, 2, KC, P])
        y = sb("y", [P, 2, D], F32)
        yn = sb("yn", [P, 2, D], F32)
        yt = pair("yt", [P, KC, P])
        stats = sb("rstats", [P, 2, 6], F32)
        moments = sb("rmoments", [P, 2], F32)
        veps = sb("rveps", [P, 1], F32)
        rstd = sb("rrstd", [P, 1], F32)
        power = sb("rpower", [P, 1], F32)
        score = sb("score", [P, E], F32)
        best = sb("best", [P, 8], F32)
        best_at = sb("best_at", [P, 8], U32)
        expert = sb("expert", [P, TOPK], F32)
        number = sb("number", [P, E], F32)
        chosen = sb("chosen", [P, TOPK, E], BF16)
        member = sb("member", [P, E], BF16)
        members = sb("members", [P, E], BF16)
        earlier = sb("earlier", [P, P], BF16)
        ones = sb("ones", [P, P], BF16)
        picked = sb("picked", [P, TOPK, E], F32)
        pos = sb("pos", [P, TOPK], F32)
        total = sb("total", [P, 1], F32)
        rtotal = sb("rtotal", [P, 1], F32)
        valid = sb("valid", [P, TOPK], F32)
        tile1 = sb("tile1", [P, TOPK], F32)
        tile2 = sb("tile2", [P, TOPK], F32)
        tile3 = sb("tile3", [P, TOPK], F32)
        four_e = sb("four_e", [P, TOPK], F32)
        raw = sb("raw", [P, TOPK], F32)
        capped = sb("capped", [P, TOPK], F32)
        entry = sb("entry", [P, 2, TOPK], I32)
        tokens = sb("tokens", [P, 2], I32)
        zeros = sb("zeros", [P, E * TPE], I32)

        o_ps = [ps(f"o_ps{i}", [P, D]) for i in range(2)]
        turn_ps = ps("rturn_ps", [P, KC, P])
        gate_ps = ps("gate_ps", [P, E])
        pos_ps = ps("pos_ps", [P, E])

        consts_made = sem("consts_made")
        w_landed = [sem(f"w_landed{i}") for i in range(4)]
        w_hi_made = sem("w_hi_made")
        w_lo_made = sem("w_lo_made")
        row_landed = sem("row_landed")
        bo_made = sem("bo_made")
        table_cleared = sem("table_cleared")
        x_landed = [sem(f"x_landed{i}") for i in range(2)]
        a_landed = [sem(f"a_landed{i}") for i in range(2)]
        at_hi_made = sem("at_hi_made")
        at_lo_made = sem("at_lo_made")
        x_biased = sem("x_biased")
        o_made = sem("o_made")
        y_made = sem("y_made")
        stats_made = sem("stats_made")
        moments_made = sem("moments_made")
        veps_made = sem("veps_made")
        rstd_made = sem("rstd_made")
        y_normed = sem("y_normed")
        rows_stored = [sem(f"rows_stored{i}") for i in range(2)]
        y_turned = sem("y_turned")
        yt_hi_made = sem("yt_hi_made")
        yt_lo_made = sem("yt_lo_made")
        gate_done = sem("gate_done")
        score_made = sem("score_made")
        y_stored = [sem(f"y_stored{i}") for i in range(2)]
        counted = sem("counted")
        member_made = sem("member_made")
        members_added = sem("members_added")
        route_step = sem("route_step")
        entry_made = sem("entry_made")
        scattered = [sem(f"scattered{i}") for i in range(2)]
        tokens_made = sem("tokens_made")
        table_landed = sem("table_landed")

        jobs = [(w_o[k * P:(k + 1) * P, :], D, wo[0][:, k, :], wo[1][:, k, :]) for k in range(KC)]
        jobs += [(w_gate[k * P:(k + 1) * P, :], E, wg[0][:, k, :], wg[1][:, k, :]) for k in range(KC)]
        CHAIN = 17

        def steps(eng, first, step):
            first()
            for t in range(4):
                step(Step(t), True, t >= 1, t >= 2)
            with eng.Fori(0, (NT - 6) // 2) as j:
                for r in range(2):
                    step(Step(4 + r, j, 2), True, True, True)
            step(Step(NT - 2), True, True, True)
            step(Step(NT - 1), True, True, True)
            step(Step(NT), False, True, True)
            step(Step(NT + 1), False, False, True)

        with nc.Block() as block:
            @block.sync
            def _(sp):
                def load(t):
                    par = t.base % 2
                    sp.wait_ge(y_made, t.times(1, -1))
                    sp.sem_inc(apart, 1)
                    sp.dma_start(x_in[:, par], x[bass.ds(t.times(P), P), :]).then_inc(x_landed[par], 16)
                    sp.wait_ge(at_lo_made, t.times(1, -1))
                    sp.sem_inc(apart, 1)
                    half = par
                    sp.dma_start(a_in[:, par].rearrange("p k t -> p (k t)"),
                                 attn_dram[bass.ds(t.plus(-half).times(P // 2), P), half * D:(half + 1) * D]
                                 ).then_inc(a_landed[par], 16)

                def first():
                    sp.dma_start(bo_row[:], b_o.to_broadcast([P, D])).then_inc(row_landed, 16)
                    sp.wait_ge(consts_made, 7)
                    sp.dma_start(table_dram.rearrange("(p c) o -> p (c o)", p=P), zeros[:]).then_inc(table_cleared, 16)
                    for m, (source, width, _, _) in enumerate(jobs):
                        sp.wait_ge(w_lo_made, max(m - 3, 0))
                        sp.sem_inc(apart, 1)
                        sp.dma_start(stage_w[:, m % 4, 0:width], source).then_inc(w_landed[m % 4], 16)
                    load(Step(0))

                def step(t, project, up, down):
                    if isinstance(t.times(1), int) and t.base + 1 >= NT:
                        pass
                    else:
                        load(t.plus(1))
                    if up:
                        s = t.plus(-1)
                        sp.wait_ge(y_normed, s.times(1, 1))
                        sp.sem_inc(apart, 1)
                        sp.dma_start(rows_dram[bass.ds(s.times(P), P), :], yn[:, s.base % 2]
                                     ).then_inc(rows_stored[s.base % 2], 16)
                        sp.dma_start(y_dram[bass.ds(s.times(P), P), :], y[:, s.base % 2]
                                     ).then_inc(y_stored[s.base % 2], 16)

                steps(sp, first, step)
                for par in range(2):
                    sp.wait_ge(rows_stored[par], 16 * NT // 2)
                    sp.wait_ge(y_stored[par], 16 * NT // 2)

            @block.gpsimd
            def _(pool):
                pool.memset(power[:], -0.5).then_inc(consts_made, 1)
                pool.memset(ones[:], 1.0).then_inc(consts_made, 1)
                pool.memset(earlier[:], 1.0).then_inc(consts_made, 1)
                pool.memset(zeros[:], 0).then_inc(consts_made, 1)
                pool.memset(members[:], 0.0).then_inc(consts_made, 1)
                pool.iota(number[:], pattern=[[1, E]], base=0, channel_multiplier=0,
                          allow_small_or_imprecise_dtypes=True).then_inc(consts_made, 1)
                pool.wait_ge(consts_made, 6)
                pool.affine_select(out=earlier[:], in_=earlier[:], compare_op=ALU.is_gt, fill=0.0, base=0,
                                   pattern=[[1, P]], channel_multiplier=-1).then_inc(consts_made, 1)
                for r in range(2):
                    pool.iota(tokens[:, r:r + 1], pattern=[[0, 1]], base=r * P, channel_multiplier=1
                              ).then_inc(tokens_made, 1)

                def add_bias(t):
                    par = t.base % 2
                    pool.wait_ge(x_landed[par], t.half().times(16, 16))
                    pool.sem_inc(apart, 1)
                    pool.tensor_tensor(x_in[:, par], x_in[:, par], bo_row[:], ALU.add).then_inc(x_biased, 1)

                def deviation(t):
                    pool.wait_ge(moments_made, t.times(1, 1))
                    pool.sem_inc(apart, 1)
                    pool.tensor_scalar(veps[:], moments[:, 1:2], EPS, None, ALU.add).then_inc(veps_made, 1)
                    pool.wait_ge(veps_made, t.times(1, 1))
                    pool.sem_inc(apart, 1)
                    pool.wait_ge(y_normed, t.times(1))
                    pool.tensor_tensor(rstd[:], veps[:], power[:], ALU.pow).then_inc(rstd_made, 1)

                def scatter(t):
                    par = t.base % 2
                    pool.wait_ge(entry_made, t.times(1, 1))
                    pool.sem_inc(apart, 1)
                    pool.wait_ge(tokens_made, t.times(1, 1))
                    pool.sem_inc(apart, 1)
                    for k in range(TOPK):
                        pool.indirect_dma_start(
                            out=table_dram, out_offset=bass.IndirectOffsetOnAxis(ap=entry[:, par, k:k + 1], axis=0),
                            in_=tokens[:, par:par + 1], in_offset=None, bounds_check=E * CAP - 1,
                            oob_is_err=False).then_inc(scattered[par], 16)

                def advance(t):
                    par = t.base % 2
                    pool.wait_ge(scattered[par], t.half().times(16 * TOPK, 16 * TOPK))
                    pool.sem_inc(apart, 1)
                    pool.tensor_scalar(tokens[:, par:par + 1], tokens[:, par:par + 1], 2 * P, None, ALU.add
                                       ).then_inc(tokens_made, 1)

                def first():
                    pool.wait_ge(bo_made, 1)
                    pool.wait_ge(table_cleared, 16)
                    add_bias(Step(0))

                def step(t, project, up, down):
                    if not (isinstance(t.times(1), int) and t.base + 1 >= NT):
                        add_bias(t.plus(1))
                    if project:
                        deviation(t)
                    if down:
                        if t.base >= 4:
                            advance(t.plus(-4))
                        scatter(t.plus(-2))

                steps(pool, first, step)
                for r in range(2):
                    pool.wait_ge(scattered[r], 16 * TOPK * NT // 2)

            @block.scalar
            def _(act):
                def split_attn(t):
                    act.wait_ge(a_landed[t.base % 2], t.half().times(16, 16))
                    act.wait_ge(o_made, t.times(1, -1))
                    act.activation(at[0][:, t.base % 2], a_in[:, t.base % 2], ACT.Copy).then_inc(at_hi_made, 1)

                def first():
                    for m, (_, width, hi, _) in enumerate(jobs):
                        act.wait_ge(w_landed[m % 4], 16 * (m // 4 + 1))
                        act.activation(hi, stage_w[:, m % 4, 0:width], ACT.Copy, scale=SCALE).then_inc(w_hi_made, 1)
                    act.wait_ge(row_landed, 16)
                    act.activation(bo_row[:], bo_row[:], ACT.Copy, scale=gates[:, 0:1]).then_inc(bo_made, 1)
                    split_attn(Step(0))

                def step(t, project, up, down):
                    if not (isinstance(t.times(1), int) and t.base + 1 >= NT):
                        split_attn(t.plus(1))
                    if up:
                        s = t.plus(-1)
                        act.wait_ge(y_turned, s.times(1, 1))
                        act.wait_ge(gate_done, s.times(1))
                        act.activation(yt[0][:], turn_ps[:], ACT.Copy).then_inc(yt_hi_made, 1)
                    if up:
                        s = t.plus(-1)
                        act.wait_ge(gate_done, s.times(1, 1))
                        act.wait_ge(member_made, s.times(1))
                        act.activation(score[:], gate_ps[:], ACT.Sigmoid, scale=1.0 / SCALE).then_inc(score_made, 1)

                steps(act, first, step)

            @block.vector
            def _(dve):
                def split_attn(t):
                    dve.wait_ge(at_hi_made, t.times(1, 1))
                    dve.tensor_tensor(at[1][:, t.base % 2], a_in[:, t.base % 2], at[0][:, t.base % 2], ALU.subtract
                                      ).then_inc(at_lo_made, 1)

                def norm(t):
                    par = t.base % 2
                    dve.wait_ge(rows_stored[par], t.half().times(16))
                    dve.wait_ge(y_turned, t.times(1, -1))
                    dve.wait_ge(rstd_made, t.times(1, 1))
                    dve.tensor_scalar(yn[:, par], y[:, par], moments[:, 0:1], rstd[:], ALU.subtract, ALU.mult
                                      ).then_inc(y_normed, 1)

                def result(t, n):
                    return Step(t.base * CHAIN, t.register, t.factor * CHAIN).times(1, n + 1)

                def route(t):
                    dve.wait_ge(score_made, t.times(1, 1))
                    dve.sem_inc(apart, 1)
                    dve.max(out=best[:], in_=score[:]).then_inc(route_step, 1)
                    dve.wait_ge(route_step, result(t, 0))
                    dve.sem_inc(apart, 1)
                    dve.max_index(out=best_at[:], in_max=best[:], in_values=score[:]).then_inc(route_step, 1)
                    dve.reduce_sum(total[:], best[:, 0:TOPK], AX_X).then_inc(route_step, 1)
                    dve.wait_ge(route_step, result(t, 1))
                    dve.tensor_copy(expert[:], best_at[:, 0:TOPK]).then_inc(route_step, 1)
                    dve.wait_ge(route_step, result(t, 2))
                    dve.reciprocal(rtotal[:], total[:]).then_inc(route_step, 1)
                    dve.wait_ge(route_step, result(t, 3))
                    dve.tensor_tensor(chosen[:], number[:].unsqueeze(1).broadcast_to([P, TOPK, E]),
                                      expert[:].unsqueeze(2).broadcast_to([P, TOPK, E]), ALU.is_equal
                                      ).then_inc(route_step, 1)
                    dve.tensor_scalar(four_e[:], expert[:], float(TPE), None, ALU.mult).then_inc(route_step, 1)
                    dve.wait_ge(route_step, result(t, 5))
                    dve.wait_ge(counted, t.times(1))
                    with nc.allow_low_precision("small whole numbers"):
                        dve.tensor_reduce(member[:], chosen[:].rearrange("p k e -> p e k"), AX_X, ALU.add
                                          ).then_inc(member_made, 1)

                def place(t):
                    par = t.base % 2
                    dve.wait_ge(counted, t.times(1, 1))
                    dve.tensor_tensor(members[:], members[:], member[:], ALU.add).then_inc(members_added, 1)
                    dve.tensor_tensor(picked[:], chosen[:], pos_ps[:].unsqueeze(1).broadcast_to([P, TOPK, E]),
                                      ALU.mult).then_inc(route_step, 1)
                    dve.wait_ge(route_step, result(t, 7))
                    dve.tensor_reduce(pos[:], picked[:], AX_X, ALU.add).then_inc(route_step, 1)
                    dve.wait_ge(route_step, result(t, 8))
                    dve.tensor_scalar(tile1[:], pos[:], float(P), None, ALU.is_ge).then_inc(route_step, 1)
                    dve.tensor_scalar(valid[:], pos[:], float(CAP), rtotal[:], ALU.is_lt, ALU.mult
                                      ).then_inc(route_step, 1)
                    dve.tensor_scalar(capped[:], pos[:], CAP - 1.0, None, ALU.min).then_inc(route_step, 1)
                    dve.wait_ge(route_step, result(t, 9))
                    dve.scalar_tensor_tensor(tile2[:], pos[:], 2.0 * P, tile1[:], ALU.is_ge, ALU.add
                                             ).then_inc(route_step, 1)
                    dve.scalar_tensor_tensor(raw[:], pos[:], float(E * TPE), four_e[:], ALU.mult, ALU.add
                                             ).then_inc(route_step, 1)
                    dve.wait_ge(route_step, result(t, 11))
                    dve.scalar_tensor_tensor(places[:, bass.ds(t.times(TOPK), TOPK)], expert[:], float(CAP),
                                             capped[:], ALU.mult, ALU.add).then_inc(route_step, 1)
                    dve.wait_ge(route_step, result(t, 12))
                    dve.scalar_tensor_tensor(tile3[:], pos[:], 3.0 * P, tile2[:], ALU.is_ge, ALU.add
                                             ).then_inc(route_step, 1)
                    dve.scalar_tensor_tensor(weights[:, bass.ds(t.times(TOPK), TOPK)], best[:, 0:TOPK],
                                             gates[:, 1:2], valid[:], ALU.mult, ALU.mult
                                             ).then_inc(route_step, 1)
                    dve.wait_ge(route_step, result(t, 16))
                    dve.wait_ge(scattered[par], t.half().times(16 * TOPK))
                    dve.scalar_tensor_tensor(entry[:, par], tile3[:], float(1 - P * E * TPE), raw[:], ALU.mult, ALU.add
                                             ).then_inc(entry_made, 1)

                def first():
                    for m, (_, width, hi, lo) in enumerate(jobs):
                        dve.wait_ge(w_hi_made, m + 1)
                        dve.scalar_tensor_tensor(lo, stage_w[:, m % 4, 0:width], SCALE, hi, ALU.mult, ALU.subtract
                                                 ).then_inc(w_lo_made, 1)
                    dve.wait_ge(consts_made, 7)
                    split_attn(Step(0))

                def step(t, project, up, down):
                    if not (isinstance(t.times(1), int) and t.base + 1 >= NT):
                        split_attn(t.plus(1))
                    if up:
                        s = t.plus(-1)
                        dve.wait_ge(yt_hi_made, s.times(1, 1))
                        dve.tensor_tensor(yt[1][:], turn_ps[:], yt[0][:], ALU.subtract).then_inc(yt_lo_made, 1)
                    if down:
                        s = t.plus(-2)
                        place(s)
                    if project:
                        dve.wait_ge(o_made, t.times(1, 1))
                        dve.wait_ge(x_biased, t.times(1, 1))
                        dve.wait_ge(y_normed, t.times(1, -1))
                        dve.wait_ge(y_stored[t.base % 2], t.half().times(16))
                        dve.scalar_tensor_tensor(y[:, t.base % 2], o_ps[t.base % 2][:], gates[:, 2:3], x_in[:, t.base % 2],
                                                 ALU.mult, ALU.add).then_inc(y_made, 1)
                        dve.wait_ge(y_made, t.times(1, 1))
                        for half in range(2):
                            last = dve.bn_stats(stats[:, half, :], y[:, t.base % 2, half * 512:(half + 1) * 512])
                        last.then_inc(stats_made, 1)
                        dve.wait_ge(stats_made, t.times(1, 1))
                        dve.wait_ge(y_normed, t.times(1))
                        dve.sem_inc(apart, 1)
                        dve.bn_aggr(moments[:], stats[:]).then_inc(moments_made, 1)
                    if up:
                        route(t.plus(-1))
                    if project:
                        norm(t)

                steps(dve, first, step)

            @block.tensor
            def _(pe):
                def three(out, stationary, moving, chunks, last_inc=None):
                    for c in range(chunks):
                        pe.matmul(out, stationary(0, c), moving(0, c), start=(c == 0), stop=False)
                        pe.matmul(out, stationary(0, c), moving(1, c), start=False, stop=False)
                        last = pe.matmul(out, stationary(1, c), moving(0, c), start=False, stop=(c == chunks - 1))
                    return last

                def project(t, half):
                    cols = slice(half * 512, (half + 1) * 512)
                    if half == 0:
                        pe.wait_ge(at_lo_made, t.times(1, 1))
                        pe.wait_ge(y_made, t.times(1, -1))
                    last = three(o_ps[t.base % 2][:, cols], lambda i, c: at[i][:, t.base % 2, c, :], lambda i, c: wo[i][:, c, cols], KC)
                    if half == 1:
                        last.then_inc(o_made, 1)

                def first():
                    pe.wait_ge(consts_made, 7)
                    pe.wait_ge(w_lo_made, len(jobs))

                def step(t, project_it, up, down):
                    if project_it:
                        project(t, 0)
                    if down:
                        s = t.plus(-2)
                        pe.wait_ge(member_made, s.times(1, 1))
                        pe.wait_ge(members_added, s.times(1))
                        pe.wait_ge(route_step, Step(s.base * CHAIN, s.register, s.factor * CHAIN).times(1))
                        pe.matmul(pos_ps[:], earlier[:], member[:], start=True, stop=False)
                        pe.matmul(pos_ps[:], ones[:], members[:], start=False, stop=True).then_inc(counted, 1)
                    if up:
                        s = t.plus(-1)
                        pe.wait_ge(y_normed, s.times(1, 1))
                        pe.wait_ge(yt_lo_made, s.times(1))
                        for k in range(KC):
                            last = pe.transpose(turn_ps[:, k, :], yn[:, s.base % 2, k * P:(k + 1) * P], ident[:])
                        last.then_inc(y_turned, 1)
                    if project_it:
                        project(t, 1)
                    if up:
                        s = t.plus(-1)
                        pe.wait_ge(yt_lo_made, s.times(1, 1))
                        pe.wait_ge(score_made, s.times(1))
                        for c in range(KC):
                            for i in range(2):
                                for w in range(2):
                                    last = pe.matmul(gate_ps[:], yt[i][:, c, :], wg[w][:, c, :],
                                                     start=(c == 0 and i == 0 and w == 0),
                                                     stop=(c == KC - 1 and i == 1 and w == 1))
                        last.then_inc(gate_done, 1)

                steps(pe, first, step)


def expert_phase(nc, persistent, shared, w_shared_up, w_shared_down, w_up, w_down, rows_dram, outs_dram, table_dram):
    ident, apart = persistent["ident"], persistent["apart"]
    with ExitStack() as ctx:
        def sb(name, shape, dt):
            return ctx.enter_context(nc.sbuf_tensor(name, shape, dt))

        def ps(name, shape, dt=F32):
            return ctx.enter_context(nc.psum_tensor(name, shape, dt))

        def sem(name):
            return ctx.enter_context(nc.semaphore("e_" + name))

        table = sb("table", [P, E * TPE], I32)
        index = sb("index", [P, 2, TPE], I32)
        rows = sb("rows", [P, 2 * TPE, D], F32)
        WU = KC * 2 * HR
        UP, DOWN = 0, 1
        part_cols = (slice(0, WU), slice(WU, WU + D))
        w_in = sb("ew_in", [P, 2, WU + D], F32)
        w_hi = sb("ew_hi", [P, 2, WU + D], F16)
        w_lo = sb("ew_lo", [P, 2, WU + D], F16)
        xt_hi = sb("ext_hi", [P, 2, KC, CAP], F16)
        xt_lo = sb("ext_lo", [P, 2, KC, CAP], F16)
        gsig = sb("egsig", [P, CAP], F32)
        gated = sb("egated", [P, CAP], F32)
        hidden = sb("ehidden", [P, CAP], F32)
        h_hi = sb("h_hi", [P, 2, CAP], F16)
        h_lo = sb("h_lo", [P, 2, CAP], F16)
        outs = sb("outs", [P, TPE, D], F32)

        jobs = [(w_shared_up[k * P:(k + 1) * P, :], 2 * HS, shared["up_hi"][:, k, :], shared["up_lo"][:, k, :])
                for k in range(KC)]
        jobs += [(w_shared_down[k * P:(k + 1) * P, :], D, shared["down_hi"][:, k, :], shared["down_lo"][:, k, :])
                 for k in range(HS // P)]

        turn_ps = ps("eturn_ps", [P, KC, P])
        g_ps = ps("g_ps", [P, CAP])
        v_ps = ps("v_ps", [P, CAP])
        down_ps = [[ps(f"edown_ps{i}{j}", [P, 512]) for j in range(2)] for i in range(2)]

        table_landed = sem("table_landed")
        index_made = sem("index_made")
        gathered = [sem(f"gathered{i}") for i in range(2)]
        w_landed = [[sem(f"w_landed{part}{i}") for i in range(2)] for part in (UP, DOWN)]
        w_hi_made = [sem(f"w_hi_made{part}") for part in (UP, DOWN)]
        w_lo_made = [sem(f"w_lo_made{part}") for part in (UP, DOWN)]
        shared_landed = [sem(f"shared_landed{i}") for i in range(TPE)]
        shared_hi_made = sem("shared_hi_made")
        shared_lo_made = sem("shared_lo_made")
        turned = sem("turned")
        xt_hi_made = sem("xt_hi_made")
        xt_lo_made = sem("xt_lo_made")
        g_made = sem("g_made")
        v_made = sem("v_made")
        gsig_made = sem("gsig_made")
        gated_made = sem("gated_made")
        hidden_made = sem("hidden_made")
        h_hi_made = sem("h_hi_made")
        h_lo_made = sem("h_lo_made")
        down_made = sem("down_made")
        left_kept = sem("left_kept")
        right_kept = sem("right_kept")
        outs_stored = [sem(f"outs_stored{k}") for k in range(TPE)]

        def more(e, ahead):
            return not (isinstance(e.times(1), int) and e.base + ahead >= E)

        def steps(eng, first, step):
            first()
            for e in range(4):
                step(Step(e), True, e >= 1)
            with eng.Fori(0, (E - 6) // 2) as j:
                for r in range(2):
                    step(Step(4 + r, j, 2), True, True)
            step(Step(E - 2), True, True)
            step(Step(E - 1), True, True)
            step(Step(E), False, True)

        with nc.Block() as block:
            @block.sync
            def _(sp):
                def load_w(e):
                    par = e.base % 2
                    for part in (UP, DOWN):
                        sp.wait_ge(w_lo_made[part], e.times(1, -1))
                        sp.sem_inc(apart, 1)
                    sp.dma_start(w_in[:, par, 0:WU].rearrange("p (k n) -> p k n", k=KC),
                                 w_up[bass.ds(e.times(D), D), :].rearrange("(k p) n -> p k n", p=P)
                                 ).then_inc(w_landed[UP][par], 16)
                    sp.dma_start(w_in[:, par, WU:WU + D], w_down[bass.ds(e.times(HR), HR), :]
                                 ).then_inc(w_landed[DOWN][par], 16)

                def first():
                    sp.dma_start(table[:], table_dram.rearrange("(p c) o -> p (c o)", p=P)).then_inc(table_landed, 16)
                    load_w(Step(0))
                    load_w(Step(1))
                    for m, (source, width, _, _) in enumerate(jobs):
                        sp.wait_ge(shared_lo_made, max(m - TPE + 1, 0))
                        sp.dma_start(outs[:, m % TPE, 0:width], source).then_inc(shared_landed[m % TPE], 16)

                def step(e, up, down):
                    if more(e, 2):
                        load_w(e.plus(2))
                    if down:
                        s = e.plus(-1)
                        for k in range(TPE):
                            sp.wait_ge(left_kept, s.times(TPE, k + 1))
                            sp.sem_inc(apart, 1)
                            sp.wait_ge(right_kept, s.times(TPE, k + 1))
                            sp.sem_inc(apart, 1)
                            sp.dma_start(outs_dram[bass.ds(s.times(CAP, k * P), P), :], outs[:, k, :]
                                         ).then_inc(outs_stored[k], 16)

                steps(sp, first, step)
                for k in range(TPE):
                    sp.wait_ge(outs_stored[k], 16 * E)

            @block.gpsimd
            def _(pool):
                def gather(e):
                    par = e.base % 2
                    pool.wait_ge(gathered[par], e.half().times(16 * TPE))
                    pool.sem_inc(apart, 1)
                    pool.wait_ge(turned, e.times(TPE, -TPE))
                    pool.sem_inc(apart, 1)
                    pool.tensor_copy(index[:, par, :], table[:, bass.ds(e.times(TPE), TPE)]).then_inc(index_made, 1)
                    pool.wait_ge(index_made, e.times(1, 1))
                    pool.sem_inc(apart, 1)
                    for k in range(TPE):
                        pool.indirect_dma_start(
                            out=rows[:, par * TPE + k, :], out_offset=None, in_=rows_dram,
                            in_offset=bass.IndirectOffsetOnAxis(ap=index[:, par, k:k + 1], axis=0),
                            bounds_check=N - 1, oob_is_err=True).then_inc(gathered[par], 16)

                def first():
                    pool.wait_ge(table_landed, 16)
                    gather(Step(0))
                    gather(Step(1))

                def step(e, up, down):
                    if more(e, 2):
                        gather(e.plus(2))

                steps(pool, first, step)

            @block.scalar
            def _(act):
                def split_w(e, part):
                    w = (slice(None), e.base % 2, part_cols[part])
                    act.wait_ge(w_landed[part][e.base % 2], e.half().times(16, 16))
                    if part == UP:
                        act.wait_ge(v_made, e.times(1, -1))
                    else:
                        act.wait_ge(down_made, e.times(2 * TPE, -2 * TPE))
                    act.activation(w_hi[w], w_in[w], ACT.Copy, scale=SCALE).then_inc(w_hi_made[part], 1)

                def split_h(e):
                    act.wait_ge(hidden_made, e.times(1, 1))
                    act.wait_ge(down_made, e.times(2 * TPE, -2 * TPE))
                    act.activation(h_hi[:, e.base % 2, :], hidden[:], ACT.Copy).then_inc(h_hi_made, 1)

                def turn(e, k):
                    act.wait_ge(turned, e.times(TPE, k + 1))
                    if k == 0:
                        act.wait_ge(v_made, e.times(1, -1))
                    act.activation(xt_hi[:, e.base % 2, :, k * P:(k + 1) * P], turn_ps[:], ACT.Copy
                                   ).then_inc(xt_hi_made, 1)

                def first():
                    split_w(Step(0), UP)
                    for m, (_, width, hi, _) in enumerate(jobs):
                        act.wait_ge(shared_landed[m % TPE], 16 * (m // TPE + 1))
                        act.activation(hi, outs[:, m % TPE, 0:width], ACT.Copy, scale=SCALE
                                       ).then_inc(shared_hi_made, 1)
                    for k in range(TPE):
                        turn(Step(0), k)

                def step(e, up, down):
                    par = e.base % 2
                    for k in range(TPE):
                        if up and more(e, 1):
                            turn(e.plus(1), k)
                        if k == 0 and more(e, 1):
                            split_w(e.plus(1), UP)
                        if up and k == 1:
                            act.wait_ge(g_made, e.times(1, 1))
                            act.wait_ge(gated_made, e.times(1))
                            act.activation(gsig[:], g_ps[:], ACT.Sigmoid, scale=1.0 / SCALE).then_inc(gsig_made, 1)
                        if up and k == 2:
                            split_w(e, DOWN)
                    if down:
                        s = e.plus(-1)
                        for k in range(TPE):
                            act.wait_ge(down_made, s.times(2 * TPE, 2 * k + 1))
                            act.wait_ge(outs_stored[k], s.times(16))
                            act.activation(outs[:, k, 0:512], down_ps[k % 2][0][:], ACT.Copy, scale=1.0 / SCALE
                                           ).then_inc(left_kept, 1)
                            if up and k == 0:
                                split_h(e)
                    elif up:
                        split_h(e)

                steps(act, first, step)

            @block.vector
            def _(dve):
                def split_w(e, part):
                    w = (slice(None), e.base % 2, part_cols[part])
                    dve.wait_ge(w_hi_made[part], e.times(1, 1))
                    dve.scalar_tensor_tensor(w_lo[w], w_in[w], SCALE, w_hi[w], ALU.mult, ALU.subtract
                                             ).then_inc(w_lo_made[part], 1)

                def turn(e, k):
                    dve.wait_ge(xt_hi_made, e.times(TPE, k + 1))
                    cols = slice(k * P, (k + 1) * P)
                    dve.tensor_tensor(xt_lo[:, e.base % 2, :, cols], turn_ps[:], xt_hi[:, e.base % 2, :, cols],
                                      ALU.subtract).then_inc(xt_lo_made, 1)

                def multiply(e):
                    dve.wait_ge(v_made, e.times(1, 1))
                    dve.wait_ge(gated_made, e.times(1, 1))
                    dve.wait_ge(h_lo_made, e.times(1))
                    dve.tensor_tensor(hidden[:], gated[:], v_ps[:], ALU.mult).then_inc(hidden_made, 1)

                def split_h(e):
                    dve.wait_ge(h_hi_made, e.times(1, 1))
                    dve.tensor_tensor(h_lo[:, e.base % 2, :], hidden[:], h_hi[:, e.base % 2, :], ALU.subtract
                                      ).then_inc(h_lo_made, 1)

                def first():
                    split_w(Step(0), UP)
                    for m, (_, width, hi, lo) in enumerate(jobs):
                        dve.wait_ge(shared_hi_made, m + 1)
                        dve.scalar_tensor_tensor(lo, outs[:, m % TPE, 0:width], SCALE, hi, ALU.mult, ALU.subtract
                                                 ).then_inc(shared_lo_made, 1)
                    for k in range(TPE):
                        turn(Step(0), k)

                def step(e, up, down):
                    par = e.base % 2
                    for k in range(TPE):
                        if up and more(e, 1):
                            turn(e.plus(1), k)
                        if k == 1 and more(e, 1):
                            split_w(e.plus(1), UP)
                        if up and k == 2:
                            dve.wait_ge(gsig_made, e.times(1, 1))
                            dve.scalar_tensor_tensor(gated[:], g_ps[:], 1.0 / SCALE ** 2, gsig[:],
                                                     ALU.mult, ALU.mult).then_inc(gated_made, 1)
                            split_w(e, DOWN)
                    if up:
                        multiply(e)
                    if down:
                        s = e.plus(-1)
                        for k in range(TPE):
                            dve.wait_ge(down_made, s.times(2 * TPE, 2 * k + 2))
                            dve.wait_ge(outs_stored[k], s.times(16))
                            dve.tensor_scalar(outs[:, k, 512:D], down_ps[k % 2][1][:], 1.0 / SCALE, None, ALU.mult
                                              ).then_inc(right_kept, 1)
                            if up and k == 1:
                                split_h(e)
                    elif up:
                        split_h(e)
                steps(dve, first, step)

            @block.tensor
            def _(pe):
                def turn(e, k):
                    par = e.base % 2
                    if k == 0:
                        pe.wait_ge(gathered[par], e.half().times(16 * TPE, 16 * TPE))
                    pe.wait_ge(xt_lo_made, e.times(TPE, k))
                    for c in range(KC):
                        last = pe.transpose(turn_ps[:, c, :], rows[:, par * TPE + k, c * P:(c + 1) * P], ident[:])
                    last.then_inc(turned, 1)

                def up_half(e, part, half):
                    par = e.base % 2
                    out = (g_ps, v_ps)[part][:]
                    for c in range(half * KC // 2, (half + 1) * KC // 2):
                        at = c * 2 * HR + part * HR
                        wh, wl = (w[:, par, at:at + HR] for w in (w_hi, w_lo))
                        pe.matmul(out, wh, xt_hi[:, par, c, :], start=(c == 0), stop=False)
                        pe.matmul(out, wh, xt_lo[:, par, c, :], start=False, stop=False)
                        last = pe.matmul(out, wl, xt_hi[:, par, c, :], start=False, stop=(c == KC - 1))
                    if half == 1:
                        last.then_inc((g_made, v_made)[part], 1)

                def down_tile(s, k):
                    par = s.base % 2
                    for half, kept in ((0, left_kept), (1, right_kept)):
                        pe.wait_ge(kept, s.times(TPE, k - 1))
                        cols = slice(WU + half * 512, WU + (half + 1) * 512)
                        hh, hl = (h[:, par, k * P:(k + 1) * P] for h in (h_hi, h_lo))
                        pe.matmul(down_ps[k % 2][half][:], hh, w_hi[:, par, cols], start=True, stop=False)
                        pe.matmul(down_ps[k % 2][half][:], hh, w_lo[:, par, cols], start=False, stop=False)
                        pe.matmul(down_ps[k % 2][half][:], hl, w_hi[:, par, cols], start=False, stop=True
                                  ).then_inc(down_made, 1)

                def first():
                    for k in range(TPE):
                        turn(Step(0), k)

                def step(e, up, down):
                    if up:
                        pe.wait_ge(w_lo_made[UP], e.times(1, 1))
                        pe.wait_ge(xt_lo_made, e.times(TPE, TPE))
                        pe.wait_ge(hidden_made, e.times(1))
                        for part in range(2):
                            for half in range(2):
                                if more(e, 1):
                                    turn(e.plus(1), 2 * part + half)
                                up_half(e, part, half)
                    if down:
                        s = e.plus(-1)
                        pe.wait_ge(h_lo_made, s.times(1, 1))
                        pe.wait_ge(w_lo_made[DOWN], s.times(1, 1))
                        for k in range(TPE):
                            down_tile(s, k)

                steps(pe, first, step)


def combining_phase(nc, persistent, shared, rows_dram, y_dram, outs_dram, out):
    places, weights = persistent["places"], persistent["weights"]
    ident, gates, apart = persistent["ident"], persistent["gates"], persistent["apart"]
    HC = HS // P
    up = (shared["up_hi"], shared["up_lo"])
    down = (shared["down_hi"], shared["down_lo"])
    with ExitStack() as ctx:
        def sb(name, shape, dt):
            return ctx.enter_context(nc.sbuf_tensor(name, shape, dt))

        def ps(name, shape):
            return ctx.enter_context(nc.psum_tensor(name, shape, F32))

        def sem(name):
            return ctx.enter_context(nc.semaphore("c_" + name))

        index = sb("cindex", [P, 2, TOPK], I32)
        weight = sb("weight", [P, 2, TOPK], F32)
        rows = sb("crows", [P, 2, TOPK, D], F32)
        sums = sb("csums", [P, 2, 2, D], F32)
        yn = sb("cyn", [P, 2, D], F32)
        yt = [sb(f"cyt{i}", [P, 2, KC, P], F16) for i in range(2)]
        gsig = sb("cgsig", [P, HS], F32)
        gated = sb("cgated", [P, HS], F32)
        hidden = sb("chidden", [P, HS], F32)
        ht = [sb(f"cht{i}", [P, HC, P], F16) for i in range(2)]

        turn_ps = ps("cturn_ps", [P, KC, P])
        up_ps = ps("cup_ps", [P, 2 * HS])
        ht_ps = ps("cht_ps", [P, HC, P])
        down_ps = ps("cdown_ps", [P, D])

        index_made = sem("index_made")
        weight_made = sem("weight_made")
        gathered = [sem(f"gathered{i}") for i in range(2)]
        yn_landed = [sem(f"yn_landed{i}") for i in range(2)]
        y_landed = [sem(f"y_landed{i}") for i in range(2)]
        y_turned = sem("y_turned")
        yt_hi_made = sem("yt_hi_made")
        yt_lo_made = sem("yt_lo_made")
        up_made = sem("up_made")
        gsig_made = sem("gsig_made")
        gated_made = sem("gated_made")
        hidden_made = sem("hidden_made")
        h_turned = sem("h_turned")
        ht_hi_made = sem("ht_hi_made")
        ht_lo_made = sem("ht_lo_made")
        down_made = sem("down_made")
        added = sem("added")
        out_stored = [sem(f"out_stored{i}") for i in range(2)]

        ADDS = TOPK + 1

        def more(t, ahead):
            return not (isinstance(t.times(1), int) and t.base + ahead >= NT)

        def steps(eng, first, step):
            first()
            for t in range(4):
                step(Step(t), True, t >= 1, t >= 2)
            with eng.Fori(0, (NT - 6) // 2) as j:
                for r in range(2):
                    step(Step(4 + r, j, 2), True, True, True)
            step(Step(NT - 2), True, True, True)
            step(Step(NT - 1), True, True, True)
            step(Step(NT), False, True, True)
            step(Step(NT + 1), False, False, True)

        with nc.Block() as block:
            @block.gpsimd
            def _(pool):
                def gather(t):
                    par = t.base % 2
                    pool.wait_ge(added, t.times(ADDS, -ADDS))
                    pool.sem_inc(apart, 1)
                    pool.tensor_copy(index[:, par, :], places[:, bass.ds(t.times(TOPK), TOPK)]).then_inc(index_made, 1)
                    pool.wait_ge(index_made, t.times(1, 1))
                    pool.sem_inc(apart, 1)
                    for k in range(TOPK):
                        pool.indirect_dma_start(
                            out=rows[:, par, k, :], out_offset=None, in_=outs_dram,
                            in_offset=bass.IndirectOffsetOnAxis(ap=index[:, par, k:k + 1], axis=0),
                            bounds_check=E * CAP - 1, oob_is_err=True).then_inc(gathered[par], 16)

                def first():
                    gather(Step(0))
                    gather(Step(1))

                def step(t, turn, project, finish):
                    if finish and more(t, 0):
                        gather(t)

                steps(pool, first, step)

            @block.sync
            def _(sp):
                def load_yn(t):
                    sp.wait_ge(y_turned, t.times(1, -1))
                    sp.sem_inc(apart, 1)
                    sp.dma_start(yn[:, t.base % 2], rows_dram[bass.ds(t.times(P), P), :]
                                 ).then_inc(yn_landed[t.base % 2], 16)

                def load_y(t):
                    sp.wait_ge(out_stored[t.base % 2], t.half().times(16))
                    sp.sem_inc(apart, 1)
                    sp.dma_start(sums[:, t.base % 2, 0], y_dram[bass.ds(t.times(P), P), :]
                                 ).then_inc(y_landed[t.base % 2], 16)

                def first():
                    for t in range(2):
                        load_yn(Step(t))
                    for t in range(2):
                        load_y(Step(t))

                def step(t, turn, project, finish):
                    if more(t, 2):
                        load_yn(t.plus(2))
                    if finish:
                        s = t.plus(-2)
                        sp.wait_ge(added, s.times(ADDS, ADDS))
                        sp.sem_inc(apart, 1)
                        sp.dma_start(out[bass.ds(s.times(P), P), :], sums[:, s.base % 2, ADDS % 2]
                                     ).then_inc(out_stored[s.base % 2], 16)
                        if more(t, 0):
                            load_y(t)

                steps(sp, first, step)
                for par in range(2):
                    sp.wait_ge(out_stored[par], 16 * NT // 2)

            @block.scalar
            def _(act):
                def first():
                    pass

                def step(t, turn, project, finish):
                    if finish:
                        s = t.plus(-2)
                        act.wait_ge(h_turned, s.times(1, 1))
                        act.wait_ge(down_made, s.times(1))
                        act.activation(ht[0][:], ht_ps[:], ACT.Copy).then_inc(ht_hi_made, 1)
                    if turn:
                        act.wait_ge(y_turned, t.times(1, 1))
                        act.wait_ge(up_made, t.times(1, -1))
                        act.activation(yt[0][:, t.base % 2], turn_ps[:], ACT.Copy).then_inc(yt_hi_made, 1)
                    if project:
                        s = t.plus(-1)
                        act.wait_ge(up_made, s.times(1, 1))
                        act.wait_ge(gated_made, s.times(1))
                        act.activation(gsig[:], up_ps[:, HS:2 * HS], ACT.Sigmoid, scale=1.0 / SCALE
                                       ).then_inc(gsig_made, 1)

                steps(act, first, step)

            @block.vector
            def _(dve):
                def add_rows(t, some):
                    par = t.base % 2
                    if some[0] == 0:
                        dve.wait_ge(added, t.times(ADDS, -ADDS))
                        dve.tensor_copy(weight[:, par, :], weights[:, bass.ds(t.times(TOPK), TOPK)]
                                        ).then_inc(weight_made, 1)
                        dve.wait_ge(weight_made, t.times(1, 1))
                        dve.wait_ge(y_landed[par], t.half().times(16, 16))
                        dve.wait_ge(gathered[par], t.half().times(16 * TOPK, 16 * TOPK))
                    for k in some:
                        dve.wait_ge(added, t.times(ADDS, k))
                        dve.scalar_tensor_tensor(sums[:, par, (k + 1) % 2, :], rows[:, par, k, :],
                                                 weight[:, par, k:k + 1], sums[:, par, k % 2, :], ALU.mult, ALU.add
                                                 ).then_inc(added, 1)

                def first():
                    pass

                def step(t, turn, project, finish):
                    if finish:
                        s = t.plus(-2)
                        dve.wait_ge(ht_hi_made, s.times(1, 1))
                        dve.tensor_tensor(ht[1][:], ht_ps[:], ht[0][:], ALU.subtract).then_inc(ht_lo_made, 1)
                    if turn:
                        dve.wait_ge(yt_hi_made, t.times(1, 1))
                        dve.tensor_tensor(yt[1][:, t.base % 2], turn_ps[:], yt[0][:, t.base % 2], ALU.subtract
                                          ).then_inc(yt_lo_made, 1)
                    if finish:
                        add_rows(t.plus(-2), range(0, 3))
                    if project:
                        s = t.plus(-1)
                        dve.wait_ge(gsig_made, s.times(1, 1))
                        dve.scalar_tensor_tensor(gated[:], up_ps[:, HS:2 * HS], 1.0 / SCALE ** 2, gsig[:],
                                                 ALU.mult, ALU.mult).then_inc(gated_made, 1)
                        dve.wait_ge(gated_made, s.times(1, 1))
                        dve.wait_ge(h_turned, s.times(1))
                        dve.tensor_tensor(hidden[:], gated[:], up_ps[:, 0:HS], ALU.mult).then_inc(hidden_made, 1)
                    if finish:
                        s = t.plus(-2)
                        par = s.base % 2
                        add_rows(s, range(3, TOPK))
                        dve.wait_ge(down_made, s.times(1, 1))
                        dve.wait_ge(added, s.times(ADDS, TOPK))
                        dve.scalar_tensor_tensor(sums[:, par, ADDS % 2, :], down_ps[:], gates[:, 3:4],
                                                 sums[:, par, TOPK % 2, :], ALU.mult, ALU.add).then_inc(added, 1)

                steps(dve, first, step)

            @block.tensor
            def _(pe):
                def three(out, stationary, moving, chunks):
                    for c in range(chunks):
                        pe.matmul(out, stationary(0, c), moving(0, c), start=(c == 0), stop=False)
                        pe.matmul(out, stationary(0, c), moving(1, c), start=False, stop=False)
                        last = pe.matmul(out, stationary(1, c), moving(0, c), start=False, stop=(c == chunks - 1))
                    return last

                def first():
                    pass

                def step(t, turn, project, finish):
                    if finish:
                        s = t.plus(-2)
                        pe.wait_ge(hidden_made, s.times(1, 1))
                        pe.wait_ge(ht_lo_made, s.times(1))
                        for c in range(HC):
                            last = pe.transpose(ht_ps[:, c, :], hidden[:, c * P:(c + 1) * P], ident[:])
                        last.then_inc(h_turned, 1)
                    if turn:
                        pe.wait_ge(yn_landed[t.base % 2], t.half().times(16, 16))
                        pe.wait_ge(yt_lo_made, t.times(1))
                        for k in range(KC):
                            last = pe.transpose(turn_ps[:, k, :], yn[:, t.base % 2, k * P:(k + 1) * P], ident[:])
                        last.then_inc(y_turned, 1)
                    if project:
                        s = t.plus(-1)
                        pe.wait_ge(yt_lo_made, s.times(1, 1))
                        pe.wait_ge(hidden_made, s.times(1))
                        three(up_ps[:], lambda i, c: yt[i][:, s.base % 2, c, :], lambda i, c: up[i][:, c, :], KC
                              ).then_inc(up_made, 1)
                    if finish:
                        s = t.plus(-2)
                        pe.wait_ge(ht_lo_made, s.times(1, 1))
                        pe.wait_ge(added, s.times(ADDS))
                        for half in range(2):
                            cols = slice(half * 512, (half + 1) * 512)
                            last = three(down_ps[:, cols], lambda i, c: ht[i][:, c, :],
                                         lambda i, c: down[i][:, c, cols], HC)
                        last.then_inc(down_made, 1)

                steps(pe, first, step)


def gated_cross_attention_and_moe(nc, x, ctx_t, w_qkv, b_qkv, w_o, b_o, gains, w_gate, w_shared_up,
                                  w_shared_down, w_up, w_down, out):
    attn_dram = nc.dram_tensor("attn_dram", [NBLK * P, KC * BLK], F32, kind="Internal").ap()
    rows_dram = nc.dram_tensor("rows_dram", [N, D], F32, kind="Internal").ap()
    y_dram = nc.dram_tensor("y_dram", [N, D], F32, kind="Internal").ap()
    outs_dram = nc.dram_tensor("outs_dram", [E * CAP, D], F32, kind="Internal").ap()
    table_dram = nc.dram_tensor("table_dram", [E * CAP, 1], I32, kind="Internal").ap()
    with ExitStack() as ctx:
        def sb(name, shape, dt):
            return ctx.enter_context(nc.sbuf_tensor(name, shape, dt))

        persistent = {
            "ident": sb("ident", [P, P], F32),
            "gates": sb("gates", [P, 4], F32),
            "places": sb("places", [P, NT * TOPK], I32),
            "weights": sb("weights", [P, NT * TOPK], F32),
        }
        ident, gates = persistent["ident"], persistent["gates"]
        persistent["apart"] = apart = ctx.enter_context(nc.semaphore("apart"))
        cleared = ctx.enter_context(nc.semaphore("cleared"))
        gains_landed = ctx.enter_context(nc.semaphore("gains_landed"))
        tanh_made = ctx.enter_context(nc.semaphore("tanh_made"))
        with nc.Block() as block:
            @block.sync
            def _(sp):
                sp.dma_start(gates[:, 2:4], gains.to_broadcast([P, 2])).then_inc(gains_landed, 16)

            @block.scalar
            def _(act):
                act.wait_ge(gains_landed, 16)
                act.activation(gates[:, 0:2], gates[:, 2:4], ACT.Tanh).then_inc(tanh_made, 1)
                act.wait_ge(tanh_made, 1)
                act.activation(gates[:, 2:4], gates[:, 0:2], ACT.Copy, scale=1.0 / SCALE).then_inc(tanh_made, 1)

            @block.gpsimd
            def _(pool):
                pool.memset(ident[:], 0.0).then_inc(cleared, 1)
                pool.wait_ge(cleared, 1)
                pool.affine_select(out=ident[:], in_=ident[:], compare_op=ALU.not_equal, fill=1.0, base=0,
                                   pattern=[[-1, P]], channel_multiplier=1)
        attention_phase(nc, persistent, x, ctx_t, w_qkv, b_qkv, attn_dram)
        routing_phase(nc, persistent, x, w_o, b_o, gains, w_gate, attn_dram, rows_dram, y_dram, table_dram)
        shared = {
            "up_hi": sb("shared_up_hi", [P, KC, 2 * HS], F16),
            "up_lo": sb("shared_up_lo", [P, KC, 2 * HS], F16),
            "down_hi": sb("shared_down_hi", [P, HS // P, D], F16),
            "down_lo": sb("shared_down_lo", [P, HS // P, D], F16),
        }
        expert_phase(nc, persistent, shared, w_shared_up, w_shared_down, w_up, w_down, rows_dram, outs_dram,
                     table_dram)
        combining_phase(nc, persistent, shared, rows_dram, y_dram, outs_dram, out)


def kernel(**inputs):
    import numpy as np
    import concourse.bacc as bacc
    from concourse.bass_utils import run_bass_kernel_spmd

    a = {name: np.asarray(value) for name, value in inputs.items()}
    w = "L0_xattn_"
    f = "L0_ffn_"
    arrays = {
        "x": a["x"].reshape(N, D),
        "ctx_t": a["ctx_2048"].reshape(N, D).T,
        "w_qkv": np.concatenate([a[w + "Wq"].T, a[w + "Wk"].T, a[w + "Wv"].T], axis=0),
        "b_qkv": np.concatenate([a[w + "bq"], a[w + "bk"], a[w + "bv"]]).reshape(3 * KC, P).T,
        "w_o": a[w + "Wo"].T,
        "b_o": a[w + "bo"].reshape(1, D),
        "gains": np.concatenate([a["g_xattn"], a["g_ffn"]]).reshape(1, 2),
        "w_gate": a[f + "w_gate"],
        "w_shared_up": a[f + "w_shared_up"],
        "w_shared_down": a[f + "w_shared_down"],
        "w_up": a[f + "w_up"].reshape(E * D, 2 * HR),
        "w_down": a[f + "w_down"].reshape(E * HR, D),
    }
    arrays = {name: np.ascontiguousarray(v) for name, v in arrays.items()}
    nc = bacc.Bacc("TRN2", target_bir_lowering=False, num_devices=1)
    args = [nc.dram_tensor(n, v.shape, mybir.dt.from_np(v.dtype), kind="ExternalInput").ap()
            for n, v in arrays.items()]
    out = nc.dram_tensor("out", (N, D), F32, kind="ExternalOutput").ap()
    gated_cross_attention_and_moe(nc, *args, out)
    r = run_bass_kernel_spmd(nc, [arrays], core_ids=[0])
    return r.results[0]["out"].reshape(4, N // 4, D)
```

```python
from contextlib import ExitStack

import concourse.bass as bass
from concourse import mybir

F32 = mybir.dt.float32
F16 = mybir.dt.float16
BF16 = mybir.dt.bfloat16
I32 = mybir.dt.int32
U32 = mybir.dt.uint32
ALU = mybir.AluOpType
ACT = mybir.ActivationFunctionType
AX_X = mybir.AxisListType.X

P = 128
N = 4096
D = 1024
H = 16
HD = D // H
KC = D // P
EPS = 1e-5
SCALE = 64.0
NEG = -1e30

BLK = 256
NBLK = N // BLK
TOK = P // H
QUAD = 4
PEELED = 3
NQ = BLK // (TOK * QUAD)
NT = N // P

E = 64
TOPK = 6
CAP = 512
TPE = CAP // P
HR = 128
HS = 256




class Step:

    def __init__(self, base, register=None, factor=0):
        self.base, self.register, self.factor = base, register, factor

    def plus(self, n):
        return Step(self.base + n, self.register, self.factor)

    def half(self):
        return Step(self.base // 2, self.register, self.factor // 2)

    def times(self, per, extra=0):
        n = self.base * per + extra
        return max(n, 0) if self.register is None else self.register * (self.factor * per) + n


CHUNKS = 3 * KC
QKC = 2 * KC
WHOLE = 4
SLOT = [0, 2, 5, 8, 10, 13, 16, 18]
ALONE = [0, 2, 4, 6, 8, 10, 12, 14]
TURN = [12, 20]
WO_SPLIT = 10
STATS = [3, 4]


def work_after(n, proj):
    found = []
    for q, s in enumerate(SLOT if proj else ALONE):
        for stage, lag in (("weighted", 4 if proj else 5), ("turned", 3), ("values", 1), ("scores", 0)):
            if s + lag == n:
                found.append((stage, q))
    return sorted(found, key=lambda f: f[1])


def attention_phase(nc, persistent, gains, wq_wo, x, ctx_t, w_qkv, b_qkv, w_o, attn_dram):
    ident, gates, apart = persistent["ident"], persistent["gates"], persistent["apart"]
    with ExitStack() as ctx:
        def sb(name, shape, dt):
            return ctx.enter_context(nc.sbuf_tensor(name, shape, dt))

        def ps(name, shape, dt=F32):
            return ctx.enter_context(nc.psum_tensor(name, shape, dt))

        def sem(name):
            return ctx.enter_context(nc.semaphore(name))

        wk_wv = [sb(f"wk_wv_{part}", [P, 2, KC, D], F16) for part in ("hi", "lo")]

        def weights(i):
            return [wq_wo[i][:], wk_wv[i][:, 0], wk_wv[i][:, 1]]

        w_hi, w_lo = weights(0), weights(1)
        bias = sb("bias", [P, 3 * KC], F32)
        x_in = sb("x_in", [P, 2, D], F32)
        c_in = sb("c_in", [P, KC, BLK], F32)
        xt_hi = sb("xt_hi", [P, KC, BLK], F16)
        xt_lo = sb("xt_lo", [P, KC, BLK], F16)
        ct_hi = sb("ct_hi", [P, KC, BLK], F16)
        ct_lo = sb("ct_lo", [P, KC, BLK], F16)
        v = sb("v", [P, 2, P, H], F32)
        qk = [sb(f"qk_{part}", [P, 2, 2, P, H], F16) for part in ("hi", "lo")]
        whole = sb("whole", [P, WHOLE, 2, P], F32)
        probs = sb("probs", [P, 2, QUAD, P], F32)
        probs_t = [sb(f"probs_t_{part}", [P, 2, QUAD, P], F16) for part in ("hi", "lo")]
        values = [sb(f"values_{part}", [P, 2, QUAD, HD], F16) for part in ("hi", "lo")]
        attn = sb("attn", [P, 2, 2, KC, P], F32)
        stats = sb("stats", [P, 2, 2, 6], F32)
        moments = sb("moments", [P, 2, 2], F32)
        veps = sb("veps", [P, 2], F32)
        rstd = sb("rstd", [P, 2], F32)
        power = sb("power", [P, 1], F32)
        neg_max = sb("neg_max", [P, 2, QUAD], F32)
        sums = sb("sums", [P, 2, QUAD], F32)
        rsums = sb("rsums", [P, 2, QUAD], F32)
        mask = sb("mask", [P, P], F32)

        turn_ps = ps("turn_ps", [P, KC, P])
        proj_ps = [ps(f"proj_ps{i}", [P, 512]) for i in range(2)]
        score_ps = [ps(f"score_ps{i}", [P, QUAD, P]) for i in range(2)]
        probs_ps = ps("probs_ps", [P, QUAD, P])
        attn_ps = ps("attn_ps", [HD, QUAD, P])
        values_ps = turn_ps[:, 0:2, :].rearrange("p k (c d) -> p (k c) d", d=HD)

        w_landed = [sem(f"w_landed{i}") for i in range(4)]
        wo_landed = [sem(f"wo_landed{i}") for i in range(4)]
        wo_hi_made = sem("wo_hi_made")
        wo_lo_made = sem("wo_lo_made")
        w_hi_made = sem("w_hi_made")
        w_lo_made = sem("w_lo_made")
        bias_landed = sem("bias_landed")
        consts_made = sem("consts_made")
        ident_made = sem("ident_made")
        gains_landed = sem("gains_landed")
        tanh_made = sem("tanh_made")
        x_landed = sem("x_landed")
        c_landed = sem("c_landed")
        stats_made = sem("stats_made")
        moments_made = sem("moments_made")
        veps_made = sem("veps_made")
        rstd_made = sem("rstd_made")
        x_normed = sem("x_normed")
        x_turned = sem("x_turned")
        xt_hi_made = sem("xt_hi_made")
        xt_lo_made = sem("xt_lo_made")
        ct_hi_made = sem("ct_hi_made")
        ct_made = sem("ct_made")
        projected = sem("projected")
        even_kept = sem("even_kept")
        odd_kept = sem("odd_kept")
        qk_hi_made = sem("qk_hi_made")
        qk_lo_made = sem("qk_lo_made")
        scored = sem("scored")
        masked_made = sem("masked_made")
        max_made = sem("max_made")
        exp_made = sem("exp_made")
        rsum_made = sem("rsum_made")
        probs_made = sem("probs_made")
        probs_turned = sem("probs_turned")
        probs_hi_kept = sem("probs_hi_kept")
        probs_kept = sem("probs_kept")
        values_turned = sem("values_turned")
        values_hi_kept = sem("values_hi_kept")
        values_kept = sem("values_kept")
        attn_made = sem("attn_made")
        attn_kept = sem("attn_kept")
        attn_stored = [sem(f"attn_stored{i}") for i in range(2)]

        stage_w = attn[:, :, :, :, :].rearrange("p a b k t -> p (a b) (k t)")
        stage_wo = [x_in[:, i] for i in range(2)] + [
            c_in[:, i * 4:(i + 1) * 4, :].rearrange("p k t -> p (k t)") for i in range(2)]

        def kept(b, n, half, odd):
            rows = slice(half * HD, (half + 1) * HD)
            if n < QKC:
                return whole[rows, n % WHOLE, odd, :]
            return v[rows, b.base % 2, :, 2 * (n - QKC) + odd]

        def whole_chunk(n):
            return whole[:, n % WHOLE].rearrange("p h t -> p t h")

        def part_of_qk(i, b, n):
            head = 2 * (n % KC)
            return qk[i][:, b.base % 2, n // KC, :, head:head + 2]

        def steps(eng, first, step):
            first()
            step(Step(0), True, False, True)
            for b in range(1, PEELED):
                step(Step(b), True, True, True)
            with eng.Fori(0, (NBLK - 1 - PEELED) // 2) as j:
                for r in range(2):
                    step(Step(PEELED + r, j, 2), True, True, True)
            step(Step(NBLK - 1), True, True, False)
            step(Step(NBLK), False, True, False)

        with nc.Block() as block:
            @block.sync
            def _(sp):
                def load_x(b):
                    sp.wait_ge(x_turned, b.times(2))
                    sp.sem_inc(apart, 1)
                    sp.dma_start(x_in[:], x[bass.ds(b.times(BLK), BLK), :].rearrange("(a p) d -> p a d", p=P)
                                 ).then_inc(x_landed, 16)

                def load_ctx(b):
                    sp.wait_ge(ct_made, b.times(1))
                    sp.sem_inc(apart, 1)
                    sp.dma_start(c_in[:], ctx_t[:, bass.ds(b.times(BLK), BLK)].rearrange("(k p) t -> p k t", p=P)
                                 ).then_inc(c_landed, 16)

                def store(b):
                    sp.wait_ge(attn_kept, b.times(NQ, NQ))
                    sp.sem_inc(apart, 1)
                    par = b.base % 2
                    sp.dma_start(attn_dram[bass.ds(b.times(P), P), :],
                                 attn[:, par].rearrange("p a k t -> p (a k t)")).then_inc(attn_stored[par], 16)

                def first():
                    load_x(Step(0))
                    sp.dma_start(gates[:, 2:4], gains.to_broadcast([P, 2])).then_inc(gains_landed, 16)
                    sp.dma_start(bias[:], b_qkv).then_inc(bias_landed, 16)
                    for m in range(CHUNKS):
                        sp.wait_ge(w_lo_made, max(m - 3, 0))
                        sp.dma_start(stage_w[:, m % 4, :], w_qkv[m * P:(m + 1) * P, :]).then_inc(w_landed[m % 4], 16)
                        if m == KC - 1:
                            load_ctx(Step(0))
                        if m == CHUNKS // 2:
                            load_x(Step(1))

                def load_wo():
                    sp.wait_ge(x_turned, 2 * NBLK)
                    sp.wait_ge(ct_made, NBLK)
                    for m in range(KC):
                        sp.wait_ge(wo_lo_made, max(m - 3, 0))
                        sp.dma_start(stage_wo[m % 4], w_o[m * P:(m + 1) * P, :]).then_inc(wo_landed[m % 4], 16)

                def step(b, proj, attend, more):
                    if more:
                        if attend:
                            load_x(b.plus(1))
                        load_ctx(b.plus(1))
                    elif proj:
                        load_wo()
                    if attend:
                        store(b.plus(-1))

                steps(sp, first, step)
                for par in range(2):
                    sp.wait_ge(attn_stored[par], 16 * NBLK // 2)

            @block.gpsimd
            def _(pool):
                pool.memset(ident[:], 0.0).then_inc(ident_made, 1)
                pool.wait_ge(ident_made, 1)
                pool.affine_select(out=ident[:], in_=ident[:], compare_op=ALU.not_equal, fill=1.0, base=0,
                                   pattern=[[-1, P]], channel_multiplier=1).then_inc(ident_made, 1)
                pool.memset(power[:], -0.5).then_inc(consts_made, 1)
                pool.memset(mask[:], 0.0).then_inc(consts_made, 1)
                pool.wait_ge(consts_made, 2)
                by_token = mask[:].rearrange("p (t h) -> p t h", h=H)
                pool.affine_select(out=by_token, in_=by_token, compare_op=ALU.is_ge, fill=NEG, base=0,
                                   pattern=[[-H, TOK], [0, H]], channel_multiplier=1).then_inc(consts_made, 1)
                pool.wait_ge(consts_made, 3)
                pool.affine_select(out=by_token, in_=by_token, compare_op=ALU.is_ge, fill=NEG, base=H - 1,
                                   pattern=[[H, TOK], [0, H]], channel_multiplier=-1).then_inc(consts_made, 1)

                def deviation(b, t):
                    pool.wait_ge(moments_made, b.times(2, t + 1))
                    pool.sem_inc(apart, 1)
                    pool.tensor_scalar(veps[:, t:t + 1], moments[:, t, 1:2], EPS, None, ALU.add).then_inc(veps_made, 1)
                    pool.wait_ge(veps_made, b.times(2, t + 1))
                    pool.sem_inc(apart, 1)
                    pool.wait_ge(x_normed, b.times(2, t - 1))
                    pool.tensor_tensor(rstd[:, t:t + 1], veps[:, t:t + 1], power[:], ALU.pow).then_inc(rstd_made, 1)

                def split_ctx(b):
                    pool.wait_ge(ct_hi_made, b.times(1, 1))
                    pool.tensor_tensor(ct_lo[:], c_in[:], ct_hi[:], ALU.subtract).then_inc(ct_made, 1)

                def divide(a, q):
                    pool.wait_ge(rsum_made, a.times(NQ, q + 1))
                    pool.sem_inc(apart, 1)
                    pool.tensor_tensor(probs[:, q % 2], probs[:, q % 2],
                                       rsums[:, q % 2, :].unsqueeze(2).broadcast_to([P, QUAD, P]),
                                       ALU.mult).then_inc(probs_made, 1)

                def first():
                    for t in range(2):
                        deviation(Step(0), t)

                def step(b, proj, attend, more):
                    if proj:
                        split_ctx(b)
                    for n in range(CHUNKS):
                        if more and n in STATS:
                            deviation(b.plus(1), STATS.index(n))
                        if attend:
                            for stage, q in work_after(n - 1, proj):
                                if stage == "scores":
                                    divide(b.plus(-1), q)

                steps(pool, first, step)

            @block.scalar
            def _(act):
                def split_ctx(b):
                    act.wait_ge(c_landed, b.times(16, 16))
                    act.wait_ge(projected, b.times(CHUNKS))
                    act.activation(ct_hi[:], c_in[:], ACT.Copy).then_inc(ct_hi_made, 1)

                def split_w(m):
                    act.wait_ge(w_landed[m % 4], 16 * (m // 4 + 1))
                    act.activation(w_hi[m // KC][:, m % KC, :], stage_w[:, m % 4, :], ACT.Copy, scale=SCALE
                                   ).then_inc(w_hi_made, 1)

                def split_wo(m):
                    act.wait_ge(projected, (NBLK - 1) * CHUNKS + KC)
                    act.wait_ge(wo_landed[m % 4], 16 * (m // 4 + 1))
                    act.activation(wq_wo[0][:, m, :], stage_wo[m % 4], ACT.Copy, scale=SCALE).then_inc(wo_hi_made, 1)

                def turn(b, t):
                    act.wait_ge(x_turned, b.times(2, t + 1))
                    act.wait_ge(projected, b.times(CHUNKS, KC - CHUNKS))
                    act.activation(xt_hi[:, :, t * P:(t + 1) * P], turn_ps[:], ACT.Copy).then_inc(xt_hi_made, 1)

                def keep(b, n):
                    act.wait_ge(projected, b.times(CHUNKS, n + 1))
                    if n < QKC:
                        act.wait_ge(qk_lo_made, b.times(QKC, n + 1 - WHOLE))
                    if n == QKC:
                        act.wait_ge(attn_made, b.times(NQ, -NQ))
                    for half in range(2):
                        last = act.activation(kept(b, n, half, 0),
                                              proj_ps[n % 2][0:HD, half * P:(half + 1) * P], ACT.Identity,
                                              bias=bias[0:HD, n:n + 1], scale=1.0 / SCALE)
                    last.then_inc(even_kept, 1)

                def split_qk(b, n):
                    act.wait_ge(even_kept, b.times(CHUNKS, n + 1))
                    act.wait_ge(odd_kept, b.times(CHUNKS, n + 1))
                    if n == 0:
                        act.wait_ge(attn_made, b.times(NQ, -NQ))
                    act.activation(part_of_qk(0, b, n), whole_chunk(n), ACT.Copy).then_inc(qk_hi_made, 1)

                def exps(a, q):
                    act.wait_ge(max_made, a.times(NQ, q + 1))
                    act.wait_ge(rsum_made, a.times(NQ, q - 1))
                    for g in range(QUAD):
                        last = act.activation(probs[:, q % 2, g, :], probs[:, q % 2, g, :], ACT.Exp,
                                              bias=neg_max[:, q % 2, g:g + 1],
                                              accum_out=sums[:, q % 2, g:g + 1])
                    last.then_inc(exp_made, 1)

                def keep_probs(a, q):
                    act.wait_ge(probs_turned, a.times(NQ, q + 1))
                    act.wait_ge(attn_made, a.times(NQ, q - 1))
                    act.activation(probs_t[0][:, q % 2], probs_ps[:], ACT.Copy).then_inc(probs_hi_kept, 1)

                def keep_values(a, q):
                    act.wait_ge(values_turned, a.times(NQ, q + 1))
                    act.wait_ge(attn_made, a.times(NQ, q - 1))
                    act.activation(values[0][:, q % 2], values_ps, ACT.Copy).then_inc(values_hi_kept, 1)

                def first():
                    act.wait_ge(gains_landed, 16)
                    act.activation(gates[:, 0:2], gates[:, 2:4], ACT.Tanh).then_inc(tanh_made, 1)
                    act.wait_ge(tanh_made, 1)
                    act.activation(gates[:, 2:4], gates[:, 0:2], ACT.Copy, scale=1.0 / SCALE).then_inc(tanh_made, 1)
                    for m in range(KC):
                        split_w(m)
                        if m in (1, 4):
                            turn(Step(0), m // 4)
                    act.wait_ge(bias_landed, 16)

                def step(b, proj, attend, more):
                    if proj:
                        split_ctx(b)
                    for n in range(CHUNKS):
                        if proj and not attend and n < 2 * KC:
                            split_w(KC + n)
                        if proj:
                            keep(b, n)
                        if proj and 0 <= n - 1 < QKC:
                            split_qk(b, n - 1)
                        if proj and not more and 0 <= n - WO_SPLIT < KC:
                            split_wo(n - WO_SPLIT)
                        if attend:
                            for stage, q in work_after(n, proj):
                                if stage == "scores":
                                    exps(b.plus(-1), q)
                                if stage == "turned":
                                    keep_probs(b.plus(-1), q)
                                if stage == "values":
                                    keep_values(b.plus(-1), q)
                        if more and n in TURN:
                            turn(b.plus(1), TURN.index(n))

                steps(act, first, step)

            @block.vector
            def _(dve):
                def moment(b, t):
                    dve.wait_ge(x_landed, b.times(16, 16))
                    for half in range(2):
                        last = dve.bn_stats(stats[:, t, half, :], x_in[:, t, half * 512:(half + 1) * 512])
                    last.then_inc(stats_made, 1)
                    dve.wait_ge(stats_made, b.times(2, t + 1))
                    dve.wait_ge(x_normed, b.times(2, t - 1))
                    dve.sem_inc(apart, 1)
                    dve.bn_aggr(moments[:, t, :], stats[:, t]).then_inc(moments_made, 1)

                def norm(b, t):
                    dve.wait_ge(rstd_made, b.times(2, t + 1))
                    dve.tensor_scalar(x_in[:, t, :], x_in[:, t, :], moments[:, t, 0:1], rstd[:, t:t + 1],
                                      ALU.subtract, ALU.mult).then_inc(x_normed, 1)

                def turn(b, t):
                    dve.wait_ge(xt_hi_made, b.times(2, t + 1))
                    dve.tensor_tensor(xt_lo[:, :, t * P:(t + 1) * P], turn_ps[:], xt_hi[:, :, t * P:(t + 1) * P],
                                      ALU.subtract).then_inc(xt_lo_made, 1)

                def keep(b, n):
                    dve.wait_ge(projected, b.times(CHUNKS, n + 1))
                    if n < QKC:
                        dve.wait_ge(qk_lo_made, b.times(QKC, n + 1 - WHOLE))
                    if n == QKC:
                        dve.wait_ge(attn_made, b.times(NQ, -NQ))
                    for half in range(2):
                        last = dve.tensor_scalar(kept(b, n, half, 1),
                                                 proj_ps[n % 2][HD:P, half * P:(half + 1) * P],
                                                 1.0 / SCALE, bias[HD:P, n:n + 1], ALU.mult, ALU.add)
                    last.then_inc(odd_kept, 1)

                def split_qk(b, n):
                    dve.wait_ge(qk_hi_made, b.times(QKC, n + 1))
                    dve.tensor_tensor(part_of_qk(1, b, n), whole_chunk(n), part_of_qk(0, b, n), ALU.subtract
                                      ).then_inc(qk_lo_made, 1)

                def split_w(m):
                    dve.wait_ge(w_hi_made, m + 1)
                    dve.scalar_tensor_tensor(w_lo[m // KC][:, m % KC, :], stage_w[:, m % 4, :], SCALE,
                                             w_hi[m // KC][:, m % KC, :], ALU.mult, ALU.subtract
                                             ).then_inc(w_lo_made, 1)

                def split_wo(m):
                    dve.wait_ge(wo_hi_made, m + 1)
                    dve.scalar_tensor_tensor(wq_wo[1][:, m, :], stage_wo[m % 4], SCALE, wq_wo[0][:, m, :],
                                             ALU.mult, ALU.subtract).then_inc(wo_lo_made, 1)

                def maxima(a, q):
                    dve.wait_ge(scored, a.times(NQ, q + 1))
                    dve.wait_ge(exp_made, a.times(NQ, q - 1))
                    dve.wait_ge(probs_turned, a.times(NQ, q - 1))
                    dve.tensor_tensor(probs[:, q % 2], score_ps[q % 2][:],
                                      mask[:].unsqueeze(1).broadcast_to([P, QUAD, P]), ALU.add
                                      ).then_inc(masked_made, 1)
                    dve.wait_ge(masked_made, a.times(NQ, q + 1))
                    dve.tensor_reduce(neg_max[:, q % 2, :], probs[:, q % 2], AX_X, ALU.max, negate=True
                                      ).then_inc(max_made, 1)

                def inverses(a, q):
                    dve.wait_ge(exp_made, a.times(NQ, q + 1))
                    dve.wait_ge(probs_made, a.times(NQ, q - 1))
                    dve.reciprocal(rsums[:, q % 2, :], sums[:, q % 2, :]).then_inc(rsum_made, 1)

                def keep_values(a, q):
                    dve.wait_ge(values_hi_kept, a.times(NQ, q + 1))
                    dve.tensor_tensor(values[1][:, q % 2], values_ps, values[0][:, q % 2], ALU.subtract
                                      ).then_inc(values_kept, 1)

                def keep_probs(a, q):
                    dve.wait_ge(probs_hi_kept, a.times(NQ, q + 1))
                    dve.tensor_tensor(probs_t[1][:, q % 2], probs_ps[:], probs_t[0][:, q % 2], ALU.subtract
                                      ).then_inc(probs_kept, 1)

                def keep_attn(a, q):
                    par, half, t0 = a.base % 2, q % 2, (q // 2) * TOK * QUAD
                    dve.wait_ge(attn_made, a.times(NQ, q + 1))
                    if q == 0:
                        dve.wait_ge(attn_stored[par], a.half().times(16))
                    got = attn_ps[:].rearrange("d g (t o r) -> d r o (g t)", o=KC, r=2)
                    for r in range(2):
                        last = dve.tensor_copy(attn[r * HD:(r + 1) * HD, par, half, :, t0:t0 + TOK * QUAD],
                                               got[:, r])
                    last.then_inc(attn_kept, 1)

                def first():
                    for t in range(2):
                        moment(Step(0), t)
                    for t in range(2):
                        norm(Step(0), t)
                    for m in range(KC):
                        split_w(m)
                        if m in (1, 4):
                            turn(Step(0), m // 4)
                    dve.wait_ge(bias_landed, 16)
                    dve.wait_ge(consts_made, 4)

                def step(b, proj, attend, more):
                    for n in range(CHUNKS):
                        if proj and not attend and n < 2 * KC:
                            split_w(KC + n)
                        if proj:
                            keep(b, n)
                        if proj and 0 <= n - 2 < QKC:
                            split_qk(b, n - 2)
                        if proj and not more and 0 <= n - WO_SPLIT < KC:
                            split_wo(n - WO_SPLIT)
                        if attend:
                            for stage, q in work_after(n - 1, proj):
                                if stage == "scores":
                                    inverses(b.plus(-1), q)
                            for stage, q in work_after(n, proj):
                                if stage == "scores":
                                    maxima(b.plus(-1), q)
                                if stage == "turned":
                                    keep_probs(b.plus(-1), q)
                                if stage == "values":
                                    keep_values(b.plus(-1), q)
                                if stage == "weighted":
                                    keep_attn(b.plus(-1), q)
                        if more and n in STATS:
                            moment(b.plus(1), STATS.index(n))
                        if more and n - 2 in STATS:
                            norm(b.plus(1), STATS.index(n - 2))
                        if more and n in TURN:
                            turn(b.plus(1), TURN.index(n))

                steps(dve, first, step)

            @block.tensor
            def _(pe):
                def turn(b, t):
                    pe.wait_ge(x_normed, b.times(2, t + 1))
                    pe.wait_ge(xt_lo_made, b.times(2, t))
                    if b.base >= 2:
                        ahead = sum(s + 1 <= TURN[t] for s in SLOT)
                        pe.wait_ge(values_kept, b.plus(-2).times(NQ, ahead))
                    for k in range(KC):
                        last = pe.transpose(turn_ps[:, k, :], x_in[:, t, k * P:(k + 1) * P], ident[:])
                    last.then_inc(x_turned, 1)

                def project(b, n):
                    part, o = n // KC, n % KC
                    if n == 0:
                        pe.wait_ge(xt_lo_made, b.times(2, 2))
                    if n == KC:
                        pe.wait_ge(ct_made, b.times(1, 1))
                    first = b.register is None and b.base == 0
                    if first and o == 0 and n > 0:
                        pe.wait_ge(w_lo_made, n + KC)
                    pe.wait_ge(even_kept, b.times(CHUNKS, n - 1))
                    pe.wait_ge(odd_kept, b.times(CHUNKS, n - 1))
                    hi, lo = (xt_hi, xt_lo) if part == 0 else (ct_hi, ct_lo)
                    out = proj_ps[n % 2][:, 0:BLK]
                    for k in range(KC):
                        if first and n == 0:
                            pe.wait_ge(w_lo_made, k + 1)
                        wh, wl = (w[part][:, k, o * P:(o + 1) * P] for w in (w_hi, w_lo))
                        pe.matmul(out, wh, hi[:, k, :], start=(k == 0), stop=False)
                        pe.matmul(out, wh, lo[:, k, :], start=False, stop=False)
                        last = pe.matmul(out, wl, hi[:, k, :], start=False, stop=(k == KC - 1))
                    last.then_inc(projected, 1)

                def rows(q):
                    half = q % 2
                    return slice(half * HD, (half + 1) * HD)

                def group(of, q, g):
                    t0 = ((q // 2) * QUAD + g) * TOK
                    return of[rows(q), t0:t0 + TOK, :].rearrange("d t h -> d (t h)")

                def scores(a, q):
                    if q == 0:
                        pe.wait_ge(qk_lo_made, a.times(QKC, QKC))
                        pe.wait_ge(even_kept, a.times(CHUNKS, CHUNKS))
                        pe.wait_ge(odd_kept, a.times(CHUNKS, CHUNKS))
                    pe.wait_ge(masked_made, a.times(NQ, q - 1))
                    for g in range(QUAD):
                        out = score_ps[q % 2][:, g, :]
                        qh, ql = (group(part[:, a.base % 2, 0], q, g) for part in qk)
                        kh, kl = (group(part[:, a.base % 2, 1], q, g) for part in qk)
                        pe.matmul(out, qh, kh, start=True, stop=False)
                        pe.matmul(out, qh, kl, start=False, stop=False)
                        last = pe.matmul(out, ql, kh, start=False, stop=True)
                    last.then_inc(scored, 1)

                def turn_values(a, q):
                    pe.wait_ge(values_kept, a.times(NQ, q))
                    ahead = a.plus(2).times(2, sum(SLOT[q] + 1 > n for n in TURN))
                    pe.wait_ge(xt_lo_made, min(ahead, 2 * NBLK) if isinstance(ahead, int) else ahead)
                    pe.sem_inc(apart, 1)
                    for g in range(QUAD):
                        last = pe.transpose(values_ps[:, g, :], group(v[:, a.base % 2], q, g), ident[rows(q), rows(q)])
                    last.then_inc(values_turned, 1)

                def turn_probs(a, q):
                    pe.wait_ge(probs_made, a.times(NQ, q + 1))
                    pe.wait_ge(probs_kept, a.times(NQ, q))
                    for g in range(QUAD):
                        last = pe.transpose(probs_ps[:, g, :], probs[:, q % 2, g, :], ident[:])
                    last.then_inc(probs_turned, 1)

                def weigh(a, q):
                    pe.wait_ge(probs_kept, a.times(NQ, q + 1))
                    pe.wait_ge(values_kept, a.times(NQ, q + 1))
                    pe.wait_ge(attn_kept, a.times(NQ, q))
                    for g in range(QUAD):
                        vh, vl = (v[:, q % 2, g, :] for v in values)
                        ph, pl = (p[:, q % 2, g, :] for p in probs_t)
                        pe.matmul(attn_ps[:, g, :], vh, ph, start=True, stop=False)
                        pe.matmul(attn_ps[:, g, :], vh, pl, start=False, stop=False)
                        last = pe.matmul(attn_ps[:, g, :], vl, ph, start=False, stop=True)
                    last.then_inc(attn_made, 1)

                def first():
                    pe.wait_ge(ident_made, 2)
                    for t in range(2):
                        turn(Step(0), t)

                def step(b, proj, attend, more):
                    for n in range(CHUNKS):
                        if proj:
                            project(b, n)
                        if attend:
                            for stage, q in work_after(n, proj):
                                {"scores": scores, "values": turn_values, "turned": turn_probs,
                                 "weighted": weigh}[stage](b.plus(-1), q)
                        if more and n in TURN:
                            turn(b.plus(1), TURN.index(n))

                steps(pe, first, step)


def routing_phase(nc, persistent, wo, x, b_o, w_gate, w_shared_up, w_shared_down, attn_dram, rows_dram,
                  table_dram, out):
    ident, gates, apart = persistent["ident"], persistent["gates"], persistent["apart"]
    HC = HS // P
    with ExitStack() as ctx:
        def sb(name, shape, dt):
            return ctx.enter_context(nc.sbuf_tensor(name, shape, dt))

        def ps(name, shape, dt=F32):
            return ctx.enter_context(nc.psum_tensor(name, shape, dt))

        def sem(name):
            return ctx.enter_context(nc.semaphore("r_" + name))

        def pair(name, shape):
            return sb(name + "_hi", shape, F16), sb(name + "_lo", shape, F16)

        wg = pair("wg", [P, KC, E])
        up = pair("up", [P, KC, 2 * HS])
        down = pair("down", [P, HC, D])
        stage_w = sb("stage_w", [P, 4, D], F32)
        bo_row = sb("bo_row", [P, D], F32)
        x_in = sb("rx_in", [P, 2, D], F32)
        a_in = sb("a_in", [P, 2, KC, P], F32)
        at = pair("at", [P, 2, KC, P])
        y = sb("y", [P, 2, D], F32)
        yn = sb("yn", [P, 2, D], F32)
        yt = pair("yt", [P, KC, P])
        gsig = sb("gsig", [P, HS], F32)
        gated = sb("gated", [P, HS], F32)
        hidden = sb("hidden", [P, HS], F32)
        ht = pair("ht", [P, HC, P])
        result = sb("result", [P, 2, D], F32)
        stats = sb("rstats", [P, 2, 6], F32)
        moments = sb("rmoments", [P, 2], F32)
        veps = sb("rveps", [P, 1], F32)
        rstd = sb("rrstd", [P, 1], F32)
        power = sb("rpower", [P, 1], F32)
        score = sb("score", [P, E], F32)
        best = sb("best", [P, 8], F32)
        best_at = sb("best_at", [P, 8], U32)
        expert = sb("expert", [P, TOPK], F32)
        number = sb("number", [P, E], F32)
        chosen = sb("chosen", [P, TOPK, E], BF16)
        member = sb("member", [P, E], BF16)
        members = sb("members", [P, E], BF16)
        earlier = sb("earlier", [P, P], BF16)
        ones = sb("ones", [P, P], BF16)
        picked = sb("picked", [P, TOPK, E], F32)
        pos = sb("pos", [P, TOPK], F32)
        total = sb("total", [P, 1], F32)
        rtotal = sb("rtotal", [P, 1], F32)
        tile1 = sb("tile1", [P, TOPK], F32)
        tile2 = sb("tile2", [P, TOPK], F32)
        tile3 = sb("tile3", [P, TOPK], F32)
        four_e = sb("four_e", [P, TOPK], F32)
        raw = sb("raw", [P, TOPK], F32)
        entry = sb("entry", [P, 2, TOPK], I32)
        record = sb("record", [P, 2, TOPK, 2], F32)
        empty = sb("empty", [P, E * TPE, 2], F32)
        zeros = sb("zeros", [P, D], F32)

        o_ps = ps("o_ps", [P, D])
        turn_ps = ps("rturn_ps", [P, KC, P])
        up_ps = ps("up_ps", [P, 2 * HS])
        down_ps = ps("down_ps", [P, D])
        gate_pos_ps = ps("gate_pos_ps", [P, 2, E])
        gate_ps, pos_ps = gate_pos_ps[:, 0, :], gate_pos_ps[:, 1, :]
        ht_ps = turn_ps[:, 0:HC, :]

        consts_made = sem("consts_made")
        w_landed = [sem(f"w_landed{i}") for i in range(4)]
        w_hi_made = sem("w_hi_made")
        w_lo_made = sem("w_lo_made")
        row_landed = sem("row_landed")
        bo_made = sem("bo_made")
        empty_made = sem("empty_made")
        table_cleared = sem("table_cleared")
        zeros_made = sem("zeros_made")
        spare_cleared = [sem(f"spare_cleared{i}") for i in range(2)]
        x_landed = [sem(f"x_landed{i}") for i in range(2)]
        a_landed = [sem(f"a_landed{i}") for i in range(2)]
        at_hi_made = sem("at_hi_made")
        at_lo_made = sem("at_lo_made")
        x_biased = sem("x_biased")
        o_made = sem("o_made")
        y_made = sem("y_made")
        stats_made = sem("stats_made")
        moments_made = sem("moments_made")
        veps_made = sem("veps_made")
        rstd_made = sem("rstd_made")
        y_normed = sem("y_normed")
        rows_stored = [sem(f"rows_stored{i}") for i in range(2)]
        y_turned = sem("y_turned")
        yt_hi_made = sem("yt_hi_made")
        yt_lo_made = sem("yt_lo_made")
        gate_done = sem("gate_done")
        score_made = sem("score_made")
        up_made = sem("up_made")
        gsig_made = sem("gsig_made")
        gated_made = sem("gated_made")
        hidden_made = sem("hidden_made")
        h_turned = sem("h_turned")
        ht_hi_made = sem("ht_hi_made")
        ht_lo_made = sem("ht_lo_made")
        down_made = sem("down_made")
        result_made = sem("result_made")
        out_stored = [sem(f"out_stored{i}") for i in range(2)]
        counted = sem("counted")
        member_made = sem("member_made")
        members_added = sem("members_added")
        route_step = sem("route_step")
        entry_made = sem("entry_made")
        scattered = [sem(f"scattered{i}") for i in range(2)]
        tokens_made = sem("tokens_made")

        jobs = [(w_gate, (KC, E), wg[0][:], wg[1][:])]
        jobs += [(w_shared_up[k * P:(k + 2) * P, :], (2, 2 * HS), up[0][:, k:k + 2, :], up[1][:, k:k + 2, :])
                 for k in range(0, KC, 2)]
        jobs += [(w_shared_down[k * P:(k + 1) * P, :], (1, D), down[0][:, k:k + 1, :], down[1][:, k:k + 1, :])
                 for k in range(HC)]

        EARLY = 3

        def staged(m):
            chunks, width = jobs[m][1]
            return stage_w[:, m % 4, 0:chunks * width].rearrange("p (k n) -> p k n", k=chunks)

        CHAIN = 14

        def steps(eng, first, step):
            first()
            for t in range(4):
                step(Step(t), True, t >= 1, t >= 2)
            with eng.Fori(0, (NT - 6) // 2) as j:
                for r in range(2):
                    step(Step(4 + r, j, 2), True, True, True)
            step(Step(NT - 2), True, True, True)
            step(Step(NT - 1), True, True, True)
            step(Step(NT), False, True, True)
            step(Step(NT + 1), False, False, True)

        with nc.Block() as block:
            @block.sync
            def _(sp):
                def load(t):
                    par = t.base % 2
                    sp.wait_ge(at_lo_made, t.times(1, -1))
                    sp.sem_inc(apart, 1)
                    sp.dma_start(a_in[:, par].rearrange("p k t -> p (k t)"),
                                 attn_dram[bass.ds(t.plus(-par).times(P // 2), P), par * D:(par + 1) * D]
                                 ).then_inc(a_landed[par], 16)
                    sp.wait_ge(y_made, t.times(1, -1))
                    sp.sem_inc(apart, 1)
                    sp.dma_start(x_in[:, par], x[bass.ds(t.times(P), P), :]).then_inc(x_landed[par], 16)

                def first():
                    load(Step(0))
                    sp.dma_start(bo_row[:], b_o.to_broadcast([P, D])).then_inc(row_landed, 16)
                    for m, (source, _, _, _) in enumerate(jobs):
                        sp.wait_ge(w_lo_made, max(m - 3, 0))
                        sp.dma_start(staged(m), source.rearrange("(k p) n -> p k n", p=P)
                                     ).then_inc(w_landed[m % 4], 16)
                        if m == 3:
                            load(Step(1))

                def clear():
                    sp.wait_ge(empty_made, 2)
                    sp.dma_start(table_dram.rearrange("(p c) o -> p (c o)", p=P),
                                 empty[:].rearrange("p c o -> p (c o)")).then_inc(table_cleared, 16)
                    sp.wait_ge(zeros_made, 1)
                    for i, spare in enumerate((rows_dram, out)):
                        sp.dma_start(spare[N:N + CAP, :].rearrange("(p a) d -> p a d", p=P),
                                     zeros[:].unsqueeze(1).broadcast_to([P, TPE, D])).then_inc(spare_cleared[i], 16)

                def step(t, project, up, down):
                    loaded = t.register is None and t.base == 0
                    if not loaded and not (t.register is None and t.base + 1 >= NT):
                        load(t.plus(1))
                    if t.register is None and t.base == 1:
                        clear()
                    if up:
                        s = t.plus(-1)
                        sp.wait_ge(y_normed, s.times(1, 1))
                        sp.sem_inc(apart, 1)
                        sp.dma_start(rows_dram[bass.ds(s.times(P), P), :], yn[:, s.base % 2]
                                     ).then_inc(rows_stored[s.base % 2], 16)
                    if down:
                        s = t.plus(-2)
                        sp.wait_ge(result_made, s.times(1, 1))
                        sp.sem_inc(apart, 1)
                        sp.dma_start(out[bass.ds(s.times(P), P), :], result[:, s.base % 2]
                                     ).then_inc(out_stored[s.base % 2], 16)

                steps(sp, first, step)
                for par in range(2):
                    sp.wait_ge(rows_stored[par], 16 * NT // 2)
                    sp.wait_ge(out_stored[par], 16 * NT // 2)
                    sp.wait_ge(spare_cleared[par], 16)

            @block.gpsimd
            def _(pool):
                pool.memset(empty[:], 0.0).then_inc(empty_made, 1)
                pool.wait_ge(empty_made, 1)
                pool.iota(empty[:, :, 0].rearrange("p (e k) -> p e k", k=TPE), pattern=[[0, E], [P, TPE]], base=N,
                          channel_multiplier=1, allow_small_or_imprecise_dtypes=True).then_inc(empty_made, 1)
                pool.memset(zeros[:], 0.0).then_inc(zeros_made, 1)
                pool.memset(power[:], -0.5).then_inc(consts_made, 1)
                pool.memset(ones[:], 1.0).then_inc(consts_made, 1)
                pool.memset(earlier[:], 1.0).then_inc(consts_made, 1)
                pool.memset(members[:], 0.0).then_inc(consts_made, 1)
                pool.iota(number[:], pattern=[[1, E]], base=0, channel_multiplier=0,
                          allow_small_or_imprecise_dtypes=True).then_inc(consts_made, 1)
                pool.wait_ge(consts_made, 5)
                pool.affine_select(out=earlier[:], in_=earlier[:], compare_op=ALU.is_gt, fill=0.0, base=0,
                                   pattern=[[1, P]], channel_multiplier=-1).then_inc(consts_made, 1)
                for r in range(2):
                    pool.iota(record[:, r, :, 0], pattern=[[0, TOPK]], base=r * P, channel_multiplier=1,
                              allow_small_or_imprecise_dtypes=True).then_inc(tokens_made, 1)

                def add_bias(t):
                    par = t.base % 2
                    pool.wait_ge(x_landed[par], t.half().times(16, 16))
                    pool.sem_inc(apart, 1)
                    pool.tensor_tensor(x_in[:, par], x_in[:, par], bo_row[:], ALU.add).then_inc(x_biased, 1)

                def deviation(t):
                    pool.wait_ge(moments_made, t.times(1, 1))
                    pool.sem_inc(apart, 1)
                    pool.tensor_scalar(veps[:], moments[:, 1:2], EPS, None, ALU.add).then_inc(veps_made, 1)
                    pool.wait_ge(veps_made, t.times(1, 1))
                    pool.sem_inc(apart, 1)
                    pool.wait_ge(y_normed, t.times(1))
                    pool.tensor_tensor(rstd[:], veps[:], power[:], ALU.pow).then_inc(rstd_made, 1)

                def scatter(t):
                    par = t.base % 2
                    pool.wait_ge(entry_made, t.times(1, 1))
                    pool.sem_inc(apart, 1)
                    pool.wait_ge(tokens_made, t.times(1, 1))
                    pool.sem_inc(apart, 1)
                    for k in range(TOPK):
                        pool.indirect_dma_start(
                            out=table_dram, out_offset=bass.IndirectOffsetOnAxis(ap=entry[:, par, k:k + 1], axis=0),
                            in_=record[:, par, k, :], in_offset=None, bounds_check=E * CAP - 1,
                            oob_is_err=False).then_inc(scattered[par], 16)

                def advance(t):
                    par = t.base % 2
                    pool.wait_ge(scattered[par], t.half().times(16 * TOPK, 16 * TOPK))
                    pool.sem_inc(apart, 1)
                    pool.tensor_scalar(record[:, par, :, 0], record[:, par, :, 0], 2.0 * P, None, ALU.add
                                       ).then_inc(tokens_made, 1)

                def first():
                    pool.wait_ge(bo_made, 1)
                    add_bias(Step(0))

                def step(t, project, up, down):
                    if not (isinstance(t.times(1), int) and t.base + 1 >= NT):
                        add_bias(t.plus(1))
                    if project:
                        deviation(t)
                    if down:
                        if t.base == 2:
                            pool.wait_ge(table_cleared, 16)
                        if not (t.register is None and t.base == NT + 1):
                            if t.base >= 4:
                                advance(t.plus(-4))
                            scatter(t.plus(-2))
                        if t.register is None and t.base == NT:
                            advance(t.plus(-3))
                            scatter(t.plus(-1))

                steps(pool, first, step)
                for r in range(2):
                    pool.wait_ge(scattered[r], 16 * TOPK * NT // 2)

            @block.scalar
            def _(act):
                def split_attn(t):
                    act.wait_ge(a_landed[t.base % 2], t.half().times(16, 16))
                    act.wait_ge(o_made, t.times(1, -1))
                    act.activation(at[0][:, t.base % 2], a_in[:, t.base % 2], ACT.Copy).then_inc(at_hi_made, 1)

                def split_weights(some):
                    for m in some:
                        act.wait_ge(w_landed[m % 4], 16 * (m // 4 + 1))
                        act.activation(jobs[m][2], staged(m), ACT.Copy, scale=SCALE).then_inc(w_hi_made, 1)

                def first():
                    split_attn(Step(0))
                    act.wait_ge(row_landed, 16)
                    act.activation(bo_row[:], bo_row[:], ACT.Copy, scale=gates[:, 0:1]).then_inc(bo_made, 1)
                    split_weights(range(0, EARLY))

                def step(t, project, up_it, down_it):
                    if not (isinstance(t.times(1), int) and t.base + 1 >= NT):
                        split_attn(t.plus(1))
                    if t.register is None and t.base == 0:
                        split_weights(range(EARLY, len(jobs)))
                    if down_it:
                        s = t.plus(-2)
                        act.wait_ge(h_turned, s.times(1, 1))
                        act.wait_ge(down_made, s.times(1))
                        act.activation(ht[0][:], ht_ps, ACT.Copy).then_inc(ht_hi_made, 1)
                    if up_it:
                        s = t.plus(-1)
                        act.wait_ge(y_turned, s.times(1, 1))
                        act.wait_ge(up_made, s.times(1))
                        act.activation(yt[0][:], turn_ps[:], ACT.Copy).then_inc(yt_hi_made, 1)
                        act.wait_ge(gate_done, s.times(1, 1))
                        act.wait_ge(member_made, s.times(1))
                        act.activation(score[:], gate_ps, ACT.Sigmoid, scale=1.0 / SCALE).then_inc(score_made, 1)
                        act.wait_ge(up_made, s.times(1, 1))
                        act.wait_ge(gated_made, s.times(1))
                        act.activation(gsig[:], up_ps[:, HS:2 * HS], ACT.Sigmoid, scale=1.0 / SCALE
                                       ).then_inc(gsig_made, 1)

                steps(act, first, step)

            @block.vector
            def _(dve):
                def split_attn(t):
                    dve.wait_ge(at_hi_made, t.times(1, 1))
                    dve.tensor_tensor(at[1][:, t.base % 2], a_in[:, t.base % 2], at[0][:, t.base % 2], ALU.subtract
                                      ).then_inc(at_lo_made, 1)

                def norm(t):
                    par = t.base % 2
                    dve.wait_ge(rows_stored[par], t.half().times(16))
                    dve.wait_ge(y_turned, t.times(1, -1))
                    dve.wait_ge(rstd_made, t.times(1, 1))
                    dve.tensor_scalar(yn[:, par], y[:, par], moments[:, 0:1], rstd[:], ALU.subtract, ALU.mult
                                      ).then_inc(y_normed, 1)

                def after(t, n):
                    return Step(t.base * CHAIN, t.register, t.factor * CHAIN).times(1, n + 1)

                def route(t):
                    dve.wait_ge(score_made, t.times(1, 1))
                    dve.sem_inc(apart, 1)
                    dve.max(out=best[:], in_=score[:]).then_inc(route_step, 1)
                    dve.wait_ge(route_step, after(t, 0))
                    dve.sem_inc(apart, 1)
                    dve.max_index(out=best_at[:], in_max=best[:], in_values=score[:]).then_inc(route_step, 1)
                    dve.reduce_sum(total[:], best[:, 0:TOPK], AX_X).then_inc(route_step, 1)
                    dve.wait_ge(route_step, after(t, 1))
                    dve.tensor_copy(expert[:], best_at[:, 0:TOPK]).then_inc(route_step, 1)
                    dve.wait_ge(route_step, after(t, 2))
                    dve.reciprocal(rtotal[:], total[:]).then_inc(route_step, 1)
                    dve.wait_ge(route_step, after(t, 3))
                    dve.tensor_tensor(chosen[:], number[:].unsqueeze(1).broadcast_to([P, TOPK, E]),
                                      expert[:].unsqueeze(2).broadcast_to([P, TOPK, E]), ALU.is_equal
                                      ).then_inc(route_step, 1)
                    dve.tensor_scalar(four_e[:], expert[:], float(TPE), None, ALU.mult).then_inc(route_step, 1)
                    dve.wait_ge(route_step, after(t, 5))
                    dve.wait_ge(counted, t.times(1))
                    with nc.allow_low_precision("small whole numbers"):
                        dve.tensor_reduce(member[:], chosen[:].rearrange("p k e -> p e k"), AX_X, ALU.add
                                          ).then_inc(member_made, 1)

                def place(t):
                    par = t.base % 2
                    dve.wait_ge(counted, t.times(1, 1))
                    dve.tensor_tensor(members[:], members[:], member[:], ALU.add).then_inc(members_added, 1)
                    dve.tensor_tensor(picked[:], chosen[:], pos_ps.unsqueeze(1).broadcast_to([P, TOPK, E]),
                                      ALU.mult).then_inc(route_step, 1)
                    dve.wait_ge(route_step, after(t, 7))
                    dve.tensor_reduce(pos[:], picked[:], AX_X, ALU.add).then_inc(route_step, 1)
                    dve.wait_ge(route_step, after(t, 8))
                    dve.tensor_scalar(tile1[:], pos[:], float(P), None, ALU.is_ge).then_inc(route_step, 1)
                    dve.wait_ge(route_step, after(t, 9))
                    dve.scalar_tensor_tensor(tile2[:], pos[:], 2.0 * P, tile1[:], ALU.is_ge, ALU.add
                                             ).then_inc(route_step, 1)
                    dve.scalar_tensor_tensor(raw[:], pos[:], float(E * TPE), four_e[:], ALU.mult, ALU.add
                                             ).then_inc(route_step, 1)
                    dve.wait_ge(route_step, after(t, 10))
                    dve.scalar_tensor_tensor(tile3[:], pos[:], 3.0 * P, tile2[:], ALU.is_ge, ALU.add
                                             ).then_inc(route_step, 1)
                    dve.wait_ge(scattered[par], t.half().times(16 * TOPK))
                    dve.tensor_scalar(record[:, par, :, 1], best[:, 0:TOPK], gates[:, 3:4], rtotal[:],
                                      ALU.mult, ALU.mult).then_inc(route_step, 1)
                    dve.wait_ge(route_step, after(t, 13))
                    dve.scalar_tensor_tensor(entry[:, par], tile3[:], float(1 - P * E * TPE), raw[:], ALU.mult, ALU.add
                                             ).then_inc(entry_made, 1)

                def split_weights(some):
                    for m in some:
                        dve.wait_ge(w_hi_made, m + 1)
                        dve.scalar_tensor_tensor(jobs[m][3], staged(m), SCALE, jobs[m][2], ALU.mult, ALU.subtract
                                                 ).then_inc(w_lo_made, 1)

                def first():
                    split_attn(Step(0))
                    split_weights(range(0, EARLY))
                    dve.wait_ge(consts_made, 6)

                def step(t, project, up_it, down_it):
                    if not (isinstance(t.times(1), int) and t.base + 1 >= NT):
                        split_attn(t.plus(1))
                    if down_it:
                        s = t.plus(-2)
                        dve.wait_ge(ht_hi_made, s.times(1, 1))
                        dve.tensor_tensor(ht[1][:], ht_ps, ht[0][:], ALU.subtract).then_inc(ht_lo_made, 1)
                        if not (t.register is None and t.base == NT + 1):
                            place(s)
                        dve.wait_ge(down_made, s.times(1, 1))
                        dve.wait_ge(out_stored[s.base % 2], s.half().times(16))
                        dve.scalar_tensor_tensor(result[:, s.base % 2], down_ps[:], gates[:, 3:4], y[:, s.base % 2],
                                                 ALU.mult, ALU.add).then_inc(result_made, 1)
                    if up_it:
                        s = t.plus(-1)
                        dve.wait_ge(yt_hi_made, s.times(1, 1))
                        dve.tensor_tensor(yt[1][:], turn_ps[:], yt[0][:], ALU.subtract).then_inc(yt_lo_made, 1)
                    if project:
                        par = t.base % 2
                        dve.wait_ge(o_made, t.times(1, 1))
                        dve.wait_ge(x_biased, t.times(1, 1))
                        dve.wait_ge(y_normed, t.times(1, -1))
                        dve.wait_ge(result_made, t.times(1, -1))
                        dve.scalar_tensor_tensor(y[:, par], o_ps[:], gates[:, 2:3], x_in[:, par],
                                                 ALU.mult, ALU.add).then_inc(y_made, 1)
                        dve.wait_ge(y_made, t.times(1, 1))
                        for half in range(2):
                            last = dve.bn_stats(stats[:, half, :], y[:, par, half * 512:(half + 1) * 512])
                        last.then_inc(stats_made, 1)
                        dve.wait_ge(stats_made, t.times(1, 1))
                        dve.wait_ge(y_normed, t.times(1))
                        dve.sem_inc(apart, 1)
                        dve.bn_aggr(moments[:], stats[:]).then_inc(moments_made, 1)
                    if up_it:
                        route(t.plus(-1))
                    if t.register is None and t.base == NT:
                        place(t.plus(-1))
                    if project:
                        norm(t)
                    if t.register is None and t.base == 0:
                        split_weights(range(EARLY, len(jobs)))
                    if up_it:
                        s = t.plus(-1)
                        dve.wait_ge(gsig_made, s.times(1, 1))
                        dve.scalar_tensor_tensor(gated[:], up_ps[:, HS:2 * HS], 1.0 / SCALE ** 2, gsig[:],
                                                 ALU.mult, ALU.mult).then_inc(gated_made, 1)
                        dve.wait_ge(gated_made, s.times(1, 1))
                        dve.wait_ge(h_turned, s.times(1))
                        dve.tensor_tensor(hidden[:], gated[:], up_ps[:, 0:HS], ALU.mult).then_inc(hidden_made, 1)

                steps(dve, first, step)

            @block.tensor
            def _(pe):
                def three(to, stationary, moving, chunks, these=None):
                    for c in these or range(chunks):
                        pe.matmul(to, stationary(0, c), moving(0, c), start=(c == 0), stop=False)
                        pe.matmul(to, stationary(0, c), moving(1, c), start=False, stop=False)
                        last = pe.matmul(to, stationary(1, c), moving(0, c), start=False, stop=(c == chunks - 1))
                    return last

                def project(t, half, these=None):
                    cols = slice(half * 512, (half + 1) * 512)
                    return three(o_ps[:, cols], lambda i, c: at[i][:, t.base % 2, c, :],
                                 lambda i, c: wo[i][:, c, cols], KC, these)

                def first():
                    pe.wait_ge(consts_made, 6)

                def positions(s):
                    pe.wait_ge(member_made, s.times(1, 1))
                    pe.wait_ge(members_added, s.times(1))
                    pe.wait_ge(score_made, s.times(1, 1))
                    pe.matmul(pos_ps, earlier[:], member[:], start=True, stop=False)
                    pe.matmul(pos_ps, ones[:], members[:], start=False, stop=True).then_inc(counted, 1)

                def step(t, project_it, up_it, down_it):
                    if project_it:
                        pe.wait_ge(at_lo_made, t.times(1, 1))
                        pe.wait_ge(y_made, t.times(1))
                        project(t, 0)
                    if down_it:
                        s = t.plus(-2)
                        pe.wait_ge(hidden_made, s.times(1, 1))
                        pe.wait_ge(yt_lo_made, s.times(1, 1))
                        for c in range(HC):
                            last = pe.transpose(ht_ps[:, c, :], hidden[:, c * P:(c + 1) * P], ident[:])
                        last.then_inc(h_turned, 1)
                        if not (t.register is None and t.base == NT + 1):
                            positions(s)
                    if project_it:
                        project(t, 1, range(0, KC // 2))
                    if down_it:
                        s = t.plus(-2)
                        pe.wait_ge(ht_lo_made, s.times(1, 1))
                        pe.wait_ge(result_made, s.times(1))
                        for half in range(2):
                            cols = slice(half * 512, (half + 1) * 512)
                            last = three(down_ps[:, cols], lambda i, c: ht[i][:, c, :],
                                         lambda i, c: down[i][:, c, cols], HC)
                        last.then_inc(down_made, 1)
                    if up_it:
                        s = t.plus(-1)
                        pe.wait_ge(y_normed, s.times(1, 1))
                        pe.wait_ge(ht_lo_made, s.times(1))
                        for k in range(KC):
                            last = pe.transpose(turn_ps[:, k, :], yn[:, s.base % 2, k * P:(k + 1) * P], ident[:])
                        last.then_inc(y_turned, 1)
                    if project_it:
                        project(t, 1, range(KC // 2, KC)).then_inc(o_made, 1)
                    if up_it:
                        s = t.plus(-1)
                        if s.base == 0:
                            pe.wait_ge(w_lo_made, len(jobs))
                        pe.wait_ge(yt_lo_made, s.times(1, 1))
                        pe.wait_ge(route_step, s.times(CHAIN, 8 - CHAIN))
                        for c in range(KC):
                            for i in range(2):
                                for w in range(2):
                                    last = pe.matmul(gate_ps, yt[i][:, c, :], wg[w][:, c, :],
                                                     start=(c == 0 and i == 0 and w == 0),
                                                     stop=(c == KC - 1 and i == 1 and w == 1))
                        last.then_inc(gate_done, 1)
                        pe.wait_ge(hidden_made, s.times(1))
                        for these in (range(0, KC // 2), range(KC // 2, KC)):
                            last = three(up_ps[:], lambda i, c: yt[i][:, c, :], lambda i, c: up[i][:, c, :], KC,
                                         these)
                            if t.register is None and t.base == NT and these[0] == 0:
                                positions(s)
                        last.then_inc(up_made, 1)

                steps(pe, first, step)


def expert_phase(nc, persistent, w_up, w_down, rows_dram, table_dram, out):
    ident, apart = persistent["ident"], persistent["apart"]
    with ExitStack() as ctx:
        def sb(name, shape, dt):
            return ctx.enter_context(nc.sbuf_tensor(name, shape, dt))

        def ps(name, shape, dt=F32):
            return ctx.enter_context(nc.psum_tensor(name, shape, dt))

        def sem(name):
            return ctx.enter_context(nc.semaphore("e_" + name))

        table = sb("table", [P, E * TPE, 2], F32)
        index = sb("index", [P, 2, TPE], I32)
        target = sb("target", [P, TPE], I32)
        weight = sb("weight", [P, 2, TPE], F32)
        rows = sb("rows", [P, 2 * TPE, D], F32)
        WU = KC * 2 * HR
        UP, DOWN = 0, 1
        part_cols = (slice(0, WU), slice(WU, WU + D))
        w_in = sb("ew_in", [P, 2, WU + D], F32)
        w_hi = sb("ew_hi", [P, 2, WU + D], F16)
        w_lo = sb("ew_lo", [P, 2, WU + D], F16)
        xt_hi = sb("ext_hi", [P, 2, KC, CAP], F16)
        xt_lo = sb("ext_lo", [P, 2, KC, CAP], F16)
        gsig = sb("egsig", [P, CAP], F32)
        gated = sb("egated", [P, CAP], F32)
        hidden = sb("ehidden", [P, CAP], F32)
        h_hi = sb("h_hi", [P, 2, CAP], F16)
        h_lo = sb("h_lo", [P, 2, CAP], F16)
        outs = sb("outs", [P, TPE, D], F32)

        turn_ps = ps("eturn_ps", [P, KC, P])
        g_ps = ps("g_ps", [P, CAP])
        v_ps = ps("v_ps", [P, CAP])
        down_ps = [ps(f"edown_ps{i}", [P, D]) for i in range(2)]
        spare_turn_ps = down_ps[1][:].rearrange("p (k t) -> p k t", k=KC)

        table_landed = sem("table_landed")
        index_made = sem("index_made")
        target_made = sem("target_made")
        weight_made = sem("weight_made")
        gathered = [[sem(f"gathered{i}_{k}") for k in range(TPE)] for i in range(2)]
        w_landed = [[sem(f"w_landed{part}{i}") for i in range(2)] for part in (UP, DOWN)]
        w_hi_made = [sem(f"w_hi_made{part}") for part in (UP, DOWN)]
        w_lo_made = [sem(f"w_lo_made{part}") for part in (UP, DOWN)]
        turned = sem("turned")
        xt_hi_made = sem("xt_hi_made")
        xt_lo_made = sem("xt_lo_made")
        g_made = sem("g_made")
        v_made = sem("v_made")
        gsig_made = sem("gsig_made")
        gated_made = sem("gated_made")
        hidden_made = sem("hidden_made")
        h_hi_made = sem("h_hi_made")
        h_lo_made = sem("h_lo_made")
        down_made = sem("down_made")
        left_kept = sem("left_kept")
        right_kept = sem("right_kept")
        rows_added = [sem(f"rows_added{k}") for k in range(TPE)]

        def turned_ps(e, k):
            return spare_turn_ps if e.register is None and e.base == 0 and k % 2 else turn_ps[:]

        def more(e, ahead):
            return not (isinstance(e.times(1), int) and e.base + ahead >= E)

        def steps(eng, first, step):
            first()
            for e in range(4):
                step(Step(e), True, e >= 1)
            with eng.Fori(0, (E - 6) // 2) as j:
                for r in range(2):
                    step(Step(4 + r, j, 2), True, True)
            step(Step(E - 2), True, True)
            step(Step(E - 1), True, True)
            step(Step(E), False, True)

        with nc.Block() as block:
            @block.sync
            def _(sp):
                def load_w(e):
                    par = e.base % 2
                    for part in (UP, DOWN):
                        sp.wait_ge(w_lo_made[part], e.times(1, -1))
                        sp.sem_inc(apart, 1)
                    sp.dma_start(w_in[:, par, 0:WU].rearrange("p (k n) -> p k n", k=KC),
                                 w_up[bass.ds(e.times(D), D), :].rearrange("(k p) n -> p k n", p=P)
                                 ).then_inc(w_landed[UP][par], 16)
                    sp.dma_start(w_in[:, par, WU:WU + D], w_down[bass.ds(e.times(HR), HR), :]
                                 ).then_inc(w_landed[DOWN][par], 16)

                def first():
                    sp.dma_start(table[:].rearrange("p c o -> p (c o)"),
                                 table_dram.rearrange("(p c) o -> p (c o)", p=P)).then_inc(table_landed, 16)
                    load_w(Step(0))
                    for k in range(TPE):
                        sp.wait_ge(gathered[0][k], 16)
                    load_w(Step(1))

                def step(e, up, down):
                    if more(e, 2):
                        load_w(e.plus(2))

                steps(sp, first, step)
            @block.gpsimd
            def _(pool):
                def gather(e):
                    par = e.base % 2
                    for k in range(TPE):
                        pool.wait_ge(gathered[par][k], e.half().times(16))
                        pool.sem_inc(apart, 1)
                    pool.wait_ge(turned, e.times(TPE, -TPE))
                    pool.sem_inc(apart, 1)
                    pool.tensor_copy(index[:, par, :], table[:, bass.ds(e.times(TPE), TPE), 0]).then_inc(index_made, 1)
                    pool.wait_ge(index_made, e.times(1, 1))
                    pool.sem_inc(apart, 1)
                    for k in range(TPE):
                        pool.indirect_dma_start(
                            out=rows[:, par * TPE + k, :], out_offset=None, in_=rows_dram,
                            in_offset=bass.IndirectOffsetOnAxis(ap=index[:, par, k:k + 1], axis=0),
                            bounds_check=N + CAP - 1, oob_is_err=True).then_inc(gathered[par][k], 16)

                def weights(e):
                    pool.wait_ge(left_kept, e.times(TPE, -TPE))
                    pool.sem_inc(apart, 1)
                    pool.wait_ge(right_kept, e.times(TPE, -TPE))
                    pool.sem_inc(apart, 1)
                    pool.tensor_copy(weight[:, e.base % 2, :], table[:, bass.ds(e.times(TPE), TPE), 1]
                                     ).then_inc(weight_made, 1)

                def add(e):
                    for k in range(TPE):
                        pool.wait_ge(rows_added[k], e.times(16))
                        pool.sem_inc(apart, 1)
                    pool.tensor_copy(target[:], table[:, bass.ds(e.times(TPE), TPE), 0]).then_inc(target_made, 1)
                    pool.wait_ge(target_made, e.times(1, 1))
                    pool.sem_inc(apart, 1)
                    for k in range(TPE):
                        pool.wait_ge(left_kept, e.times(TPE, k + 1))
                        pool.sem_inc(apart, 1)
                        pool.wait_ge(right_kept, e.times(TPE, k + 1))
                        pool.sem_inc(apart, 1)
                        pool.indirect_dma_start(
                            out=out, out_offset=bass.IndirectOffsetOnAxis(ap=target[:, k:k + 1], axis=0),
                            in_=outs[:, k, :], in_offset=None, bounds_check=N + CAP - 1, oob_is_err=True,
                            compute_op=ALU.add).then_inc(rows_added[k], 16)

                def first():
                    pool.wait_ge(table_landed, 16)
                    gather(Step(0))
                    gather(Step(1))

                def step(e, up, down):
                    if more(e, 2):
                        gather(e.plus(2))
                    if up:
                        weights(e)
                    if down:
                        add(e.plus(-1))

                steps(pool, first, step)
                for k in range(TPE):
                    pool.wait_ge(rows_added[k], 16 * E)

            @block.scalar
            def _(act):
                def split_w(e, part):
                    w = (slice(None), e.base % 2, part_cols[part])
                    act.wait_ge(w_landed[part][e.base % 2], e.half().times(16, 16))
                    if part == UP:
                        act.wait_ge(v_made, e.times(1, -1))
                    else:
                        act.wait_ge(down_made, e.times(2 * TPE, -2 * TPE))
                    act.activation(w_hi[w], w_in[w], ACT.Copy, scale=SCALE).then_inc(w_hi_made[part], 1)

                def split_h(e):
                    act.wait_ge(hidden_made, e.times(1, 1))
                    act.wait_ge(down_made, e.times(2 * TPE, -2 * TPE))
                    act.activation(h_hi[:, e.base % 2, :], hidden[:], ACT.Copy).then_inc(h_hi_made, 1)

                def turn(e, k):
                    act.wait_ge(turned, e.times(TPE, k + 1))
                    if k == 0:
                        act.wait_ge(v_made, e.times(1, -1))
                    act.activation(xt_hi[:, e.base % 2, :, k * P:(k + 1) * P], turned_ps(e, k), ACT.Copy
                                   ).then_inc(xt_hi_made, 1)

                def first():
                    split_w(Step(0), UP)
                    for k in range(TPE):
                        turn(Step(0), k)

                def step(e, up, down):
                    par = e.base % 2
                    for k in range(TPE):
                        if up and more(e, 1):
                            turn(e.plus(1), k)
                        if k == 0 and more(e, 1):
                            split_w(e.plus(1), UP)
                        if up and k == 1:
                            act.wait_ge(g_made, e.times(1, 1))
                            act.wait_ge(gated_made, e.times(1))
                            act.activation(gsig[:], g_ps[:], ACT.Sigmoid, scale=1.0 / SCALE).then_inc(gsig_made, 1)
                        if up and k == 2:
                            split_w(e, DOWN)
                    if down:
                        s = e.plus(-1)
                        for k in range(TPE):
                            act.wait_ge(down_made, s.times(2 * TPE, 2 * k + 1))
                            if k == 0:
                                act.wait_ge(weight_made, s.times(1, 1))
                            act.wait_ge(rows_added[k], s.times(16))
                            act.activation(outs[:, k, 0:512], down_ps[k % 2][:, 0:512], ACT.Copy,
                                           scale=weight[:, s.base % 2, k:k + 1]
                                           ).then_inc(left_kept, 1)
                            if up and k == 0:
                                split_h(e)
                    elif up:
                        split_h(e)

                steps(act, first, step)

            @block.vector
            def _(dve):
                def split_w(e, part):
                    w = (slice(None), e.base % 2, part_cols[part])
                    dve.wait_ge(w_hi_made[part], e.times(1, 1))
                    dve.scalar_tensor_tensor(w_lo[w], w_in[w], SCALE, w_hi[w], ALU.mult, ALU.subtract
                                             ).then_inc(w_lo_made[part], 1)

                def turn(e, k):
                    dve.wait_ge(xt_hi_made, e.times(TPE, k + 1))
                    cols = slice(k * P, (k + 1) * P)
                    dve.tensor_tensor(xt_lo[:, e.base % 2, :, cols], turned_ps(e, k), xt_hi[:, e.base % 2, :, cols],
                                      ALU.subtract).then_inc(xt_lo_made, 1)

                def multiply(e):
                    dve.wait_ge(v_made, e.times(1, 1))
                    dve.wait_ge(gated_made, e.times(1, 1))
                    dve.wait_ge(h_lo_made, e.times(1))
                    dve.tensor_tensor(hidden[:], gated[:], v_ps[:], ALU.mult).then_inc(hidden_made, 1)

                def split_h(e):
                    dve.wait_ge(h_hi_made, e.times(1, 1))
                    dve.tensor_tensor(h_lo[:, e.base % 2, :], hidden[:], h_hi[:, e.base % 2, :], ALU.subtract
                                      ).then_inc(h_lo_made, 1)

                def first():
                    split_w(Step(0), UP)
                    for k in range(TPE):
                        turn(Step(0), k)

                def step(e, up, down):
                    par = e.base % 2
                    for k in range(TPE):
                        if up and more(e, 1):
                            turn(e.plus(1), k)
                        if k == 1 and more(e, 1):
                            split_w(e.plus(1), UP)
                        if up and k == 2:
                            dve.wait_ge(gsig_made, e.times(1, 1))
                            dve.scalar_tensor_tensor(gated[:], g_ps[:], 1.0 / SCALE ** 2, gsig[:],
                                                     ALU.mult, ALU.mult).then_inc(gated_made, 1)
                            split_w(e, DOWN)
                    if up:
                        multiply(e)
                    if down:
                        s = e.plus(-1)
                        for k in range(TPE):
                            dve.wait_ge(down_made, s.times(2 * TPE, 2 * k + 2))
                            if k == 0:
                                dve.wait_ge(weight_made, s.times(1, 1))
                            dve.wait_ge(rows_added[k], s.times(16))
                            dve.tensor_scalar(outs[:, k, 512:D], down_ps[k % 2][:, 512:D],
                                              weight[:, s.base % 2, k:k + 1], None, ALU.mult
                                              ).then_inc(right_kept, 1)
                            if up and k == 1:
                                split_h(e)
                    elif up:
                        split_h(e)
                steps(dve, first, step)

            @block.tensor
            def _(pe):
                def turn(e, k):
                    par = e.base % 2
                    pe.wait_ge(gathered[par][k], e.half().times(16, 16))
                    first = e.register is None and e.base == 0
                    pe.wait_ge(xt_lo_made, max(k - 1, 0) if first else e.times(TPE, k))
                    for c in range(KC):
                        last = pe.transpose(turned_ps(e, k)[:, c, :],
                                            rows[:, par * TPE + k, c * P:(c + 1) * P], ident[:])
                    last.then_inc(turned, 1)

                def up_half(e, part, half):
                    par = e.base % 2
                    out = (g_ps, v_ps)[part][:]
                    for c in range(half * KC // 2, (half + 1) * KC // 2):
                        at = c * 2 * HR + part * HR
                        wh, wl = (w[:, par, at:at + HR] for w in (w_hi, w_lo))
                        pe.matmul(out, wh, xt_hi[:, par, c, :], start=(c == 0), stop=False)
                        pe.matmul(out, wh, xt_lo[:, par, c, :], start=False, stop=False)
                        last = pe.matmul(out, wl, xt_hi[:, par, c, :], start=False, stop=(c == KC - 1))
                    if half == 1:
                        last.then_inc((g_made, v_made)[part], 1)

                def down_tile(s, k):
                    par = s.base % 2
                    for half, kept in ((0, left_kept), (1, right_kept)):
                        pe.wait_ge(kept, s.times(TPE, k - 1))
                        cols = slice(WU + half * 512, WU + (half + 1) * 512)
                        to = down_ps[k % 2][:, half * 512:(half + 1) * 512]
                        hh, hl = (h[:, par, k * P:(k + 1) * P] for h in (h_hi, h_lo))
                        pe.matmul(to, hh, w_hi[:, par, cols], start=True, stop=False)
                        pe.matmul(to, hh, w_lo[:, par, cols], start=False, stop=False)
                        pe.matmul(to, hl, w_hi[:, par, cols], start=False, stop=True
                                  ).then_inc(down_made, 1)

                def first():
                    for k in range(TPE):
                        turn(Step(0), k)

                def step(e, up, down):
                    if up:
                        pe.wait_ge(w_lo_made[UP], e.times(1, 1))
                        pe.wait_ge(xt_lo_made, e.times(TPE, TPE))
                        pe.wait_ge(hidden_made, e.times(1))
                        for part in range(2):
                            for half in range(2):
                                if more(e, 1):
                                    turn(e.plus(1), 2 * part + half)
                                up_half(e, part, half)
                    if down:
                        s = e.plus(-1)
                        pe.wait_ge(h_lo_made, s.times(1, 1))
                        pe.wait_ge(w_lo_made[DOWN], s.times(1, 1))
                        for k in range(TPE):
                            down_tile(s, k)

                steps(pe, first, step)


def gated_cross_attention_and_moe(nc, x, ctx_t, w_qkv, b_qkv, w_o, b_o, gains, w_gate, w_shared_up,
                                  w_shared_down, w_up, w_down, out):
    attn_dram = nc.dram_tensor("attn_dram", [NBLK * P, KC * BLK], F32, kind="Internal").ap()
    rows_dram = nc.dram_tensor("rows_dram", [N + CAP, D], F32, kind="Internal").ap()
    table_dram = nc.dram_tensor("table_dram", [E * CAP, 2], F32, kind="Internal").ap()
    with ExitStack() as ctx:
        def sb(name, shape, dt):
            return ctx.enter_context(nc.sbuf_tensor(name, shape, dt))

        persistent = {
            "ident": sb("ident", [P, P], F32),
            "gates": sb("gates", [P, 4], F32),
        }
        persistent["apart"] = ctx.enter_context(nc.semaphore("apart"))
        with ExitStack() as until_routed:
            wq_wo = [until_routed.enter_context(nc.sbuf_tensor(f"wq_wo_{part}", [P, KC, D], F16))
                     for part in ("hi", "lo")]
            attention_phase(nc, persistent, gains, wq_wo, x, ctx_t, w_qkv, b_qkv, w_o, attn_dram)
            routing_phase(nc, persistent, wq_wo, x, b_o, w_gate, w_shared_up, w_shared_down, attn_dram, rows_dram,
                          table_dram, out)
        expert_phase(nc, persistent, w_up, w_down, rows_dram, table_dram, out)


def kernel(**inputs):
    import numpy as np
    import concourse.bacc as bacc
    from concourse.bass_utils import run_bass_kernel_spmd

    a = {name: np.asarray(value) for name, value in inputs.items()}
    w = "L0_xattn_"
    f = "L0_ffn_"
    arrays = {
        "x": a["x"].reshape(N, D),
        "ctx_t": a["ctx_2048"].reshape(N, D).T,
        "w_qkv": np.concatenate([a[w + "Wq"].T, a[w + "Wk"].T, a[w + "Wv"].T], axis=0),
        "b_qkv": np.concatenate([a[w + "bq"], a[w + "bk"], a[w + "bv"]]).reshape(3 * KC, P).T,
        "w_o": a[w + "Wo"].T,
        "b_o": a[w + "bo"].reshape(1, D),
        "gains": np.concatenate([a["g_xattn"], a["g_ffn"]]).reshape(1, 2),
        "w_gate": a[f + "w_gate"],
        "w_shared_up": a[f + "w_shared_up"],
        "w_shared_down": a[f + "w_shared_down"],
        "w_up": a[f + "w_up"].reshape(E * D, 2 * HR),
        "w_down": a[f + "w_down"].reshape(E * HR, D),
    }
    arrays = {name: np.ascontiguousarray(v) for name, v in arrays.items()}
    nc = bacc.Bacc("TRN2", target_bir_lowering=False, num_devices=1)
    args = [nc.dram_tensor(n, v.shape, mybir.dt.from_np(v.dtype), kind="ExternalInput").ap()
            for n, v in arrays.items()]
    out = nc.dram_tensor("out", (N + CAP, D), F32, kind="ExternalOutput").ap()
    gated_cross_attention_and_moe(nc, *args, out)
    r = run_bass_kernel_spmd(nc, [arrays], core_ids=[0])
    return r.results[0]["out"][:N].reshape(4, N // 4, D)
```
